# Optimizing a Trainium2 kernel written in Bass

```python
import numpy as np
import jax
import jax.numpy as jnp

def _softmax(x, axis=-1):
    return jax.nn.softmax(x, axis=axis)

def _gelu(x):
    return jax.nn.gelu(x, approximate=True)

def _silu(x):
    return jax.nn.silu(x)

def _sigmoid(x):
    return jax.nn.sigmoid(x)

def _layernorm(x, axis=-1, eps=1e-05):
    m = jnp.mean(x, axis=axis, keepdims=True)
    v = jnp.var(x, axis=axis, keepdims=True)
    return (x - m) / jnp.sqrt(v + eps)

def _scatter_add(tgt, idx, src, axis=0):
    return tgt.at[idx].add(src)

def _segment_sum(src, seg, n):
    return jax.ops.segment_sum(src, seg, n)
kernel_name = 'mk_flamingo_gated_d4_seqx_r4_3864b2'

def setup_inputs(seed: int=0):
    np.random.seed(seed)
    _w = jnp.asarray

    def _rec_inputs():
        import jax
        import jax.numpy as jnp
        _rk = jax.random.key(seed)
        x = 0.0001212 + 1 * jax.random.normal(jax.random.fold_in(_rk, 1), (8, 256, 512), jnp.float32)
        _lenS = 256 - jax.random.randint(jax.random.fold_in(_rk, 7), (8,), 0, max(1, 256 // 4) + 1, jnp.int32)
        _lenS2 = 256 - jax.random.randint(jax.random.fold_in(_rk, 8), (8,), 0, max(1, 256 // 4) + 1, jnp.int32)
        _ctx_2048P = jax.random.normal(jax.random.fold_in(_rk, 11), (8, 16, 512), jnp.float32)
        _ctx_2048c = jax.random.dirichlet(jax.random.fold_in(_rk, 511), 0.3 * jnp.ones((16,), jnp.float32), (8, 256))
        _ctx_2048t = jnp.einsum('bsk,bkd->bsd', _ctx_2048c, _ctx_2048P)
        _ctx_2048t = _ctx_2048t * jax.lax.rsqrt(jnp.mean(jnp.square(_ctx_2048t)) + 1e-12) * 0.953939
        ctx_2048 = 0.000173663 + 1.0001 * (_ctx_2048t + 0.3 * jax.random.normal(jax.random.fold_in(_rk, 611), (8, 256, 512), jnp.float32))
        _g = jax.random.normal(jax.random.fold_in(_rk, 9001), (2, 4), jnp.float32)
        _g = jnp.sign(_g) * jnp.maximum(jnp.abs(_g), 1.0) + (_g == 0) * 1.0
        g_xattn = _g[0]
        g_ffn = _g[1]
        return (x, ctx_2048, g_xattn, g_ffn)
    x, ctx_2048, g_xattn, g_ffn = _rec_inputs()

    def _L0_xattn_setup():
        import jax, jax.numpy as jnp
        import numpy as np
        B_DIM, T_DIM, C_DIM = (16, 256, 512)

        def _wkv(w, u, k, v):
            Bn, Tn, Cn = k.shape
            NEG_INF = jnp.float32(-1e+38)

            def step(carry, kv_t):
                p, q, o = carry
                kt, vt = kv_t
                no = jnp.maximum(o, u + kt)
                A = jnp.exp(o - no)
                E = jnp.exp(u + kt - no)
                y = (A * p + E * vt) / (A * q + E)
                no2 = jnp.maximum(w + o, kt)
                A2 = jnp.exp(w + o - no2)
                E2 = jnp.exp(kt - no2)
                return ((A2 * p + E2 * vt, A2 * q + E2, no2), y)
            init = (jnp.zeros((Bn, Cn), k.dtype), jnp.zeros((Bn, Cn), k.dtype), jnp.full((Bn, Cn), NEG_INF, k.dtype))
            kT = jnp.moveaxis(k, 1, 0)
            vT = jnp.moveaxis(v, 1, 0)
            _, yT = jax.lax.scan(step, init, (kT, vT))
            return jnp.moveaxis(yT, 0, 1)
        key = jax.random.key(seed)
        k1, k2, k3, k4 = jax.random.split(key, 4)
        w = -jnp.exp(jax.random.normal(k1, (C_DIM,), jnp.float32))
        u = jax.random.normal(k2, (C_DIM,), jnp.float32)
        k = jax.random.normal(k3, (B_DIM, T_DIM, C_DIM), jnp.float32)
        v = jax.random.normal(k4, (B_DIM, T_DIM, C_DIM), jnp.float32)
        return {'B': B_DIM, 'T': T_DIM, 'C': C_DIM, 'w': w, 'u': u, 'k': k, 'v': v}
    _L0_xattn_all = _L0_xattn_setup()
    _L0_xattn_in = {k: v for k, v in _L0_xattn_all.items() if k in ('w', 'u')}
    del _L0_xattn_all

    def _L0_ffn_setup():
        import jax, jax.numpy as jnp
        import numpy as np
        EPS = 1e-05

        def rmsnorm(x, weight, eps=EPS):
            var = jnp.mean(x * x, axis=-1, keepdims=True)
            return x * jax.lax.rsqrt(var + eps) * weight

        def activation_quant(x):
            scale = 127.0 / jnp.clip(jnp.max(jnp.abs(x), axis=-1, keepdims=True), 1e-05, None)
            return jnp.clip(jnp.round(x * scale), -128, 127) / scale

        def weight_quant(w):
            scale = 1.0 / jnp.clip(jnp.mean(jnp.abs(w)), 1e-05, None)
            return jnp.clip(jnp.round(w * scale), -1, 1) / scale

        def bitlinear(x, w):
            xq = activation_quant(x)
            wq = weight_quant(w)
            return jnp.einsum('bsh,oh->bso', xq, wq)
        key = jax.random.key(seed)
        k1, k2, k3 = jax.random.split(key, 3)
        B, S, H, F = (4, 512, 512, 1408)
        x = jax.random.normal(k1, (B, S, H), dtype=jnp.float32)
        w_gate_up = jax.random.normal(k2, (2 * F, H), dtype=jnp.float32) * 0.02
        w_down = jax.random.normal(k3, (H, F), dtype=jnp.float32) * 0.02
        norm_weight = jnp.ones((H,), dtype=jnp.float32)
        return {'x': x, 'w_gate_up': w_gate_up, 'w_down': w_down, 'norm_weight': norm_weight}
    _L0_ffn_all = _L0_ffn_setup()
    _L0_ffn_in = {k: v for k, v in _L0_ffn_all.items() if k in ('w_gate_up', 'w_down', 'norm_weight')}
    del _L0_ffn_all

    def _L1_xattn_setup():
        import jax, jax.numpy as jnp
        import numpy as np
        EPS = 1e-06
        NUM_HEADS = 16

        def _feature_map(x):
            return jnp.where(x > 0, x + 1.0, jnp.exp(x))
        key = jax.random.key(seed)
        ks = jax.random.split(key, 7)
        B, L, S, D = (4, 1024, 1024, 512)
        sc = 1.0 / np.sqrt(D)
        return {'query': jax.random.normal(ks[0], (B, L, D), jnp.float32), 'kv': jax.random.normal(ks[1], (B, S, D), jnp.float32), 'Wq': jax.random.normal(ks[2], (D, D), jnp.float32) * sc, 'Wg': jax.random.normal(ks[3], (D, D), jnp.float32) * sc, 'bg': jnp.ones((D,), jnp.float32), 'Wkv': jax.random.normal(ks[4], (2 * D, D), jnp.float32) * sc, 'Wo': jax.random.normal(ks[5], (D, D), jnp.float32) * sc}
    _L1_xattn_all = _L1_xattn_setup()
    _L1_xattn_in = {k: v for k, v in _L1_xattn_all.items() if k in ('Wq', 'Wg', 'bg', 'Wkv', 'Wo')}
    del _L1_xattn_all

    def _L1_ffn_setup():
        import jax, jax.numpy as jnp
        import numpy as np
        D_MODEL = 512
        NUM_TILES = 64
        D_SLICE = D_MODEL // NUM_TILES
        TILES_PER_CLUSTER = 8
        NUM_CLUSTERS = NUM_TILES // TILES_PER_CLUSTER
        GRID = 16
        LN_EPS = 1e-05
        DIMS = (np.arange(NUM_TILES)[:, None] * D_SLICE + np.arange(D_SLICE)[None, :]) % D_MODEL
        DIMS = jnp.asarray(DIMS, dtype=jnp.int32)

        def _forward(x, ln_gamma, ln_beta, spline_bases, spline_slopes, output_scale):
            B, S, D = x.shape
            N = B * S
            mu = jnp.mean(x, axis=-1, keepdims=True)
            var = jnp.mean(jnp.square(x - mu), axis=-1, keepdims=True)
            xn = (x - mu) * jax.lax.rsqrt(var + LN_EPS) * ln_gamma + ln_beta
            xf = xn.reshape(N, D)
            slope_sign = jnp.sign(jnp.mean(spline_slopes, axis=-1))
            tile_sigs = jnp.zeros((NUM_TILES, D), dtype=x.dtype)
            tile_sigs = tile_sigs.at[jnp.arange(NUM_TILES)[:, None], DIMS].set(slope_sign)
            cluster_sigs = jnp.sign(tile_sigs.reshape(NUM_CLUSTERS, TILES_PER_CLUSTER, D).mean(axis=1))
            cluster_assign = jnp.arange(NUM_TILES, dtype=jnp.int32) // TILES_PER_CLUSTER
            input_sigs = jnp.sign(xf)
            cluster_scores = input_sigs @ cluster_sigs.T
            best_cluster = jnp.argmax(cluster_scores, axis=-1)
            tile_scores = input_sigs @ tile_sigs.T
            in_cluster = cluster_assign[None, :] == best_cluster[:, None]
            tile_idx = jnp.argmax(jnp.where(in_cluster, tile_scores, -jnp.inf), axis=-1)
            tok_dims = DIMS[tile_idx]
            x_slice = jnp.take_along_axis(xf, tok_dims, axis=1)
            tok_min = x_slice.min(axis=1)
            tok_max = x_slice.max(axis=1)
            onehot = tile_idx[None, :] == jnp.arange(NUM_TILES)[:, None]
            tile_min = jnp.where(onehot, tok_min[None, :], jnp.inf).min(axis=1)
            tile_max = jnp.where(onehot, tok_max[None, :], -jnp.inf).max(axis=1)
            mn = tile_min[tile_idx][:, None]
            mx = tile_max[tile_idx][:, None]
            u = jnp.clip((x_slice - mn) / (mx - mn + 1e-08), 0.0, 1.0 - 1e-06)
            gi = jnp.clip((u * GRID).astype(jnp.int32), 0, GRID - 1)
            j = jnp.arange(D_SLICE)[None, :]
            b = spline_bases[tile_idx[:, None], j, gi]
            s = spline_slopes[tile_idx[:, None], j, gi]
            x_local = (u - gi.astype(u.dtype) / GRID) * GRID
            delta = (b + s * x_local) * output_scale[tile_idx][:, None]
            out = jnp.zeros_like(xf).at[jnp.arange(N)[:, None], tok_dims].set(delta)
            return x + out.reshape(B, S, D)
        key = jax.random.key(seed)
        k1, k2, k3, k4, k5, k6 = jax.random.split(key, 6)
        x = jax.random.normal(k1, (4, 1024, D_MODEL), dtype=jnp.float32)
        ln_gamma = 1.0 + 0.1 * jax.random.normal(k2, (D_MODEL,), dtype=jnp.float32)
        ln_beta = 0.1 * jax.random.normal(k3, (D_MODEL,), dtype=jnp.float32)
        spline_bases = 0.1 * jax.random.normal(k4, (NUM_TILES, D_SLICE, GRID), dtype=jnp.float32)
        spline_slopes = 0.1 + 0.1 * jax.random.normal(k5, (NUM_TILES, D_SLICE, GRID), dtype=jnp.float32)
        output_scale = 1.0 + 0.1 * jax.random.normal(k6, (NUM_TILES,), dtype=jnp.float32)
        return {'x': x, 'ln_gamma': ln_gamma, 'ln_beta': ln_beta, 'spline_bases': spline_bases, 'spline_slopes': spline_slopes, 'output_scale': output_scale}
    _L1_ffn_all = _L1_ffn_setup()
    _L1_ffn_in = {k: v for k, v in _L1_ffn_all.items() if k in ('ln_gamma', 'ln_beta', 'spline_bases', 'spline_slopes', 'output_scale')}
    del _L1_ffn_all

    def _L2_xattn_setup():
        import jax, jax.numpy as jnp
        import numpy as np

        def _wkv(time_decay, time_first, k, v):
            w = -jnp.exp(time_decay)
            u = time_first
            B, T, C = k.shape
            aa = jnp.zeros((B, C), dtype=k.dtype)
            bb = jnp.zeros((B, C), dtype=k.dtype)
            pp = jnp.full((B, C), -1e+38, dtype=k.dtype)

            def step(carry, kv_t):
                aa, bb, pp = carry
                kt, vt = kv_t
                ww = u + kt
                q = jnp.maximum(pp, ww)
                e1 = jnp.exp(pp - q)
                e2 = jnp.exp(ww - q)
                y_t = (e1 * aa + e2 * vt) / (e1 * bb + e2)
                ww2 = pp + w
                q2 = jnp.maximum(ww2, kt)
                e1b = jnp.exp(ww2 - q2)
                e2b = jnp.exp(kt - q2)
                new_carry = (e1b * aa + e2b * vt, e1b * bb + e2b, q2)
                return (new_carry, y_t)
            ks = jnp.transpose(k, (1, 0, 2))
            vs = jnp.transpose(v, (1, 0, 2))
            _, ys = jax.lax.scan(step, (aa, bb, pp), (ks, vs))
            return jnp.transpose(ys, (1, 0, 2))
        key = jax.random.key(seed)
        k1, k2, k3, k4 = jax.random.split(key, 4)
        B, T, C = (8, 256, 512)
        return {'batch_size': B, 'seq_len': T, 'embedding_dim': C, 'time_decay': jax.random.normal(k1, (C,), dtype=jnp.float32), 'time_first': jax.random.normal(k2, (C,), dtype=jnp.float32), 'k': jax.random.normal(k3, (B, T, C), dtype=jnp.float32), 'v': jax.random.normal(k4, (B, T, C), dtype=jnp.float32)}
    _L2_xattn_all = _L2_xattn_setup()
    _L2_xattn_in = {k: v for k, v in _L2_xattn_all.items() if k in ('time_decay', 'time_first')}
    del _L2_xattn_all

    def _L2_ffn_setup():
        import jax, jax.numpy as jnp
        import numpy as np
        H = 512
        E = 8
        K = 2
        I = 16
        key = jax.random.key(seed)
        k1, k2, k3, k4 = jax.random.split(key, 4)
        B, T = (2, 1024)
        x = jax.random.normal(k1, (B, T, H), dtype=jnp.float32)
        router_w = jax.random.normal(k2, (E, H), dtype=jnp.float32) / np.sqrt(H)
        down_w = jax.random.normal(k3, (E, I, H), dtype=jnp.float32) / np.sqrt(H)
        up_w = jax.random.normal(k4, (E, H, I), dtype=jnp.float32) / np.sqrt(I)
        return {'x': x, 'router_w': router_w, 'down_w': down_w, 'up_w': up_w}
    _L2_ffn_all = _L2_ffn_setup()
    _L2_ffn_in = {k: v for k, v in _L2_ffn_all.items() if k in ('router_w', 'down_w', 'up_w')}
    del _L2_ffn_all

    def _L3_xattn_setup():
        import jax, jax.numpy as jnp
        import numpy as np
        from jax import lax
        LN_EPS = 1e-05
        key = jax.random.key(seed)
        ks = jax.random.split(key, 8)
        B, S, T, D = (4, 128, 512, 512)
        scale = 0.02
        return {'Z': jax.random.normal(ks[0], (B, S, D), dtype=jnp.float32), 'kv': jax.random.normal(ks[1], (B, T, D), dtype=jnp.float32), 'decay': jnp.float32(0.9), 'W_in': jax.random.normal(ks[2], (D, D), dtype=jnp.float32) * scale, 'b_in': jnp.zeros((D,), dtype=jnp.float32), 'W_out': jax.random.normal(ks[3], (D, D), dtype=jnp.float32) * scale, 'b_out': jnp.zeros((D,), dtype=jnp.float32), 'gamma': jnp.ones((D,), dtype=jnp.float32), 'beta': jnp.zeros((D,), dtype=jnp.float32)}
    _L3_xattn_all = _L3_xattn_setup()
    _L3_xattn_in = {k: v for k, v in _L3_xattn_all.items() if k in ('decay', 'W_in', 'b_in', 'W_out', 'b_out', 'gamma', 'beta')}
    del _L3_xattn_all

    def _L3_ffn_setup():
        import jax, jax.numpy as jnp
        import numpy as np
        B, T, D = (2, 256, 512)
        H, K, DK = (4, 8, 64)
        E = 4096
        NK = 128
        key = jax.random.key(seed)
        k1, k2, k3, k4, k5 = jax.random.split(key, 5)
        x = jax.random.normal(k1, (B, T, D), dtype=jnp.float32)
        Wq = jax.random.normal(k2, (D, 2 * H * DK), dtype=jnp.float32) * 0.02
        keys = jax.random.normal(k3, (H, NK, 2, DK), dtype=jnp.float32) * 0.02
        e_down = jax.random.normal(k4, (E, D), dtype=jnp.float32) * 0.01
        e_up = jax.random.normal(k5, (E, D), dtype=jnp.float32) * 0.01
        return {'x': x, 'Wq': Wq, 'keys': keys, 'e_down': e_down, 'e_up': e_up}
    _L3_ffn_all = _L3_ffn_setup()
    _L3_ffn_in = {k: v for k, v in _L3_ffn_all.items() if k in ('Wq', 'keys', 'e_down', 'e_up')}
    del _L3_ffn_all
    return {'x': x, 'ctx_2048': ctx_2048, 'g_xattn': g_xattn, 'g_ffn': g_ffn, 'L0_xattn_w': _L0_xattn_in['w'], 'L0_xattn_u': _L0_xattn_in['u'], 'L0_ffn_w_gate_up': _L0_ffn_in['w_gate_up'], 'L0_ffn_w_down': _L0_ffn_in['w_down'], 'L0_ffn_norm_weight': _L0_ffn_in['norm_weight'], 'L1_xattn_Wq': _L1_xattn_in['Wq'], 'L1_xattn_Wg': _L1_xattn_in['Wg'], 'L1_xattn_bg': _L1_xattn_in['bg'], 'L1_xattn_Wkv': _L1_xattn_in['Wkv'], 'L1_xattn_Wo': _L1_xattn_in['Wo'], 'L1_ffn_ln_gamma': _L1_ffn_in['ln_gamma'], 'L1_ffn_ln_beta': _L1_ffn_in['ln_beta'], 'L1_ffn_spline_bases': _L1_ffn_in['spline_bases'], 'L1_ffn_spline_slopes': _L1_ffn_in['spline_slopes'], 'L1_ffn_output_scale': _L1_ffn_in['output_scale'], 'L2_xattn_time_decay': _L2_xattn_in['time_decay'], 'L2_xattn_time_first': _L2_xattn_in['time_first'], 'L2_ffn_router_w': _L2_ffn_in['router_w'], 'L2_ffn_down_w': _L2_ffn_in['down_w'], 'L2_ffn_up_w': _L2_ffn_in['up_w'], 'L3_xattn_decay': _L3_xattn_in['decay'], 'L3_xattn_W_in': _L3_xattn_in['W_in'], 'L3_xattn_b_in': _L3_xattn_in['b_in'], 'L3_xattn_W_out': _L3_xattn_in['W_out'], 'L3_xattn_b_out': _L3_xattn_in['b_out'], 'L3_xattn_gamma': _L3_xattn_in['gamma'], 'L3_xattn_beta': _L3_xattn_in['beta'], 'L3_ffn_Wq': _L3_ffn_in['Wq'], 'L3_ffn_keys': _L3_ffn_in['keys'], 'L3_ffn_e_down': _L3_ffn_in['e_down'], 'L3_ffn_e_up': _L3_ffn_in['e_up']}

def reference(x, ctx_2048, g_xattn, g_ffn, L0_xattn_w, L0_xattn_u, L0_ffn_w_gate_up, L0_ffn_w_down, L0_ffn_norm_weight, L1_xattn_Wq, L1_xattn_Wg, L1_xattn_bg, L1_xattn_Wkv, L1_xattn_Wo, L1_ffn_ln_gamma, L1_ffn_ln_beta, L1_ffn_spline_bases, L1_ffn_spline_slopes, L1_ffn_output_scale, L2_xattn_time_decay, L2_xattn_time_first, L2_ffn_router_w, L2_ffn_down_w, L2_ffn_up_w, L3_xattn_decay, L3_xattn_W_in, L3_xattn_b_in, L3_xattn_W_out, L3_xattn_b_out, L3_xattn_gamma, L3_xattn_beta, L3_ffn_Wq, L3_ffn_keys, L3_ffn_e_down, L3_ffn_e_up):
    import jax
    import jax.numpy as jnp

    def _L0_xattn_ref(B, T, C, w, u, k, v):
        import jax, jax.numpy as jnp
        import numpy as np
        B_DIM, T_DIM, C_DIM = (16, 256, 512)

        def _wkv(w, u, k, v):
            Bn, Tn, Cn = k.shape
            NEG_INF = jnp.float32(-1e+38)

            def step(carry, kv_t):
                p, q, o = carry
                kt, vt = kv_t
                no = jnp.maximum(o, u + kt)
                A = jnp.exp(o - no)
                E = jnp.exp(u + kt - no)
                y = (A * p + E * vt) / (A * q + E)
                no2 = jnp.maximum(w + o, kt)
                A2 = jnp.exp(w + o - no2)
                E2 = jnp.exp(kt - no2)
                return ((A2 * p + E2 * vt, A2 * q + E2, no2), y)
            init = (jnp.zeros((Bn, Cn), k.dtype), jnp.zeros((Bn, Cn), k.dtype), jnp.full((Bn, Cn), NEG_INF, k.dtype))
            kT = jnp.moveaxis(k, 1, 0)
            vT = jnp.moveaxis(v, 1, 0)
            _, yT = jax.lax.scan(step, init, (kT, vT))
            return jnp.moveaxis(yT, 0, 1)
        return _wkv(w, u, k, v)

    def _L0_ffn_ref(x, w_gate_up, w_down, norm_weight):
        import jax, jax.numpy as jnp
        import numpy as np
        EPS = 1e-05

        def rmsnorm(x, weight, eps=EPS):
            var = jnp.mean(x * x, axis=-1, keepdims=True)
            return x * jax.lax.rsqrt(var + eps) * weight

        def activation_quant(x):
            scale = 127.0 / jnp.clip(jnp.max(jnp.abs(x), axis=-1, keepdims=True), 1e-05, None)
            return jnp.clip(jnp.round(x * scale), -128, 127) / scale

        def weight_quant(w):
            scale = 1.0 / jnp.clip(jnp.mean(jnp.abs(w)), 1e-05, None)
            return jnp.clip(jnp.round(w * scale), -1, 1) / scale

        def bitlinear(x, w):
            xq = activation_quant(x)
            wq = weight_quant(w)
            return jnp.einsum('bsh,oh->bso', xq, wq)
        x_norm = rmsnorm(x, norm_weight)
        gate_up = bitlinear(x_norm, w_gate_up)
        gate, up = jnp.split(gate_up, 2, axis=-1)
        hidden = jnp.square(jax.nn.relu(gate)) * up
        return bitlinear(hidden, w_down)

    def _L1_xattn_ref(query, kv, Wq, Wg, bg, Wkv, Wo):
        import jax, jax.numpy as jnp
        import numpy as np
        EPS = 1e-06
        NUM_HEADS = 16

        def _feature_map(x):
            return jnp.where(x > 0, x + 1.0, jnp.exp(x))
        B, L, D = query.shape
        S = kv.shape[1]
        H = NUM_HEADS
        hd = D // H
        q = query @ Wq.T
        gate = jax.nn.sigmoid(query @ Wg.T + bg)
        kvp = kv @ Wkv.T
        k, v = jnp.split(kvp, 2, axis=-1)
        q = _feature_map(q.reshape(B, L, H, hd).transpose(0, 2, 1, 3))
        k = _feature_map(k.reshape(B, S, H, hd).transpose(0, 2, 1, 3))
        v = v.reshape(B, S, H, hd).transpose(0, 2, 1, 3)
        kv_summary = jnp.einsum('bhsd,bhse->bhde', k, v)
        k_sum = k.sum(axis=-2)
        z = 1.0 / (jnp.einsum('bhld,bhd->bhl', q, k_sum)[..., None] + EPS)
        attn = jnp.einsum('bhld,bhde->bhle', q, kv_summary) * z
        attn = attn.transpose(0, 2, 1, 3).reshape(B, L, D)
        out = attn * gate @ Wo.T
        return out

    def _L1_ffn_ref(x, ln_gamma, ln_beta, spline_bases, spline_slopes, output_scale):
        import jax, jax.numpy as jnp
        import numpy as np
        D_MODEL = 512
        NUM_TILES = 64
        D_SLICE = D_MODEL // NUM_TILES
        TILES_PER_CLUSTER = 8
        NUM_CLUSTERS = NUM_TILES // TILES_PER_CLUSTER
        GRID = 16
        LN_EPS = 1e-05
        DIMS = (np.arange(NUM_TILES)[:, None] * D_SLICE + np.arange(D_SLICE)[None, :]) % D_MODEL
        DIMS = jnp.asarray(DIMS, dtype=jnp.int32)

        def _forward(x, ln_gamma, ln_beta, spline_bases, spline_slopes, output_scale):
            B, S, D = x.shape
            N = B * S
            mu = jnp.mean(x, axis=-1, keepdims=True)
            var = jnp.mean(jnp.square(x - mu), axis=-1, keepdims=True)
            xn = (x - mu) * jax.lax.rsqrt(var + LN_EPS) * ln_gamma + ln_beta
            xf = xn.reshape(N, D)
            slope_sign = jnp.sign(jnp.mean(spline_slopes, axis=-1))
            tile_sigs = jnp.zeros((NUM_TILES, D), dtype=x.dtype)
            tile_sigs = tile_sigs.at[jnp.arange(NUM_TILES)[:, None], DIMS].set(slope_sign)
            cluster_sigs = jnp.sign(tile_sigs.reshape(NUM_CLUSTERS, TILES_PER_CLUSTER, D).mean(axis=1))
            cluster_assign = jnp.arange(NUM_TILES, dtype=jnp.int32) // TILES_PER_CLUSTER
            input_sigs = jnp.sign(xf)
            cluster_scores = input_sigs @ cluster_sigs.T
            best_cluster = jnp.argmax(cluster_scores, axis=-1)
            tile_scores = input_sigs @ tile_sigs.T
            in_cluster = cluster_assign[None, :] == best_cluster[:, None]
            tile_idx = jnp.argmax(jnp.where(in_cluster, tile_scores, -jnp.inf), axis=-1)
            tok_dims = DIMS[tile_idx]
            x_slice = jnp.take_along_axis(xf, tok_dims, axis=1)
            tok_min = x_slice.min(axis=1)
            tok_max = x_slice.max(axis=1)
            onehot = tile_idx[None, :] == jnp.arange(NUM_TILES)[:, None]
            tile_min = jnp.where(onehot, tok_min[None, :], jnp.inf).min(axis=1)
            tile_max = jnp.where(onehot, tok_max[None, :], -jnp.inf).max(axis=1)
            mn = tile_min[tile_idx][:, None]
            mx = tile_max[tile_idx][:, None]
            u = jnp.clip((x_slice - mn) / (mx - mn + 1e-08), 0.0, 1.0 - 1e-06)
            gi = jnp.clip((u * GRID).astype(jnp.int32), 0, GRID - 1)
            j = jnp.arange(D_SLICE)[None, :]
            b = spline_bases[tile_idx[:, None], j, gi]
            s = spline_slopes[tile_idx[:, None], j, gi]
            x_local = (u - gi.astype(u.dtype) / GRID) * GRID
            delta = (b + s * x_local) * output_scale[tile_idx][:, None]
            out = jnp.zeros_like(xf).at[jnp.arange(N)[:, None], tok_dims].set(delta)
            return x + out.reshape(B, S, D)
        return _forward(x, ln_gamma, ln_beta, spline_bases, spline_slopes, output_scale)

    def _L2_xattn_ref(batch_size, seq_len, embedding_dim, time_decay, time_first, k, v):
        import jax, jax.numpy as jnp
        import numpy as np

        def _wkv(time_decay, time_first, k, v):
            w = -jnp.exp(time_decay)
            u = time_first
            B, T, C = k.shape
            aa = jnp.zeros((B, C), dtype=k.dtype)
            bb = jnp.zeros((B, C), dtype=k.dtype)
            pp = jnp.full((B, C), -1e+38, dtype=k.dtype)

            def step(carry, kv_t):
                aa, bb, pp = carry
                kt, vt = kv_t
                ww = u + kt
                q = jnp.maximum(pp, ww)
                e1 = jnp.exp(pp - q)
                e2 = jnp.exp(ww - q)
                y_t = (e1 * aa + e2 * vt) / (e1 * bb + e2)
                ww2 = pp + w
                q2 = jnp.maximum(ww2, kt)
                e1b = jnp.exp(ww2 - q2)
                e2b = jnp.exp(kt - q2)
                new_carry = (e1b * aa + e2b * vt, e1b * bb + e2b, q2)
                return (new_carry, y_t)
            ks = jnp.transpose(k, (1, 0, 2))
            vs = jnp.transpose(v, (1, 0, 2))
            _, ys = jax.lax.scan(step, (aa, bb, pp), (ks, vs))
            return jnp.transpose(ys, (1, 0, 2))
        assert seq_len <= 256
        return _wkv(time_decay, time_first, k, v)

    def _L2_ffn_ref(x, router_w, down_w, up_w):
        import jax, jax.numpy as jnp
        import numpy as np
        H = 512
        E = 8
        K = 2
        I = 16
        logits = jnp.einsum('bth,eh->bte', x, router_w)
        weights = jax.nn.softmax(logits, axis=-1)
        top_w, top_idx = jax.lax.top_k(weights, K)
        topk_mask = jnp.sum(jax.nn.one_hot(top_idx, E, dtype=x.dtype), axis=-2)
        gate = weights * topk_mask
        h = jnp.einsum('bth,eih->beti', x, down_w)
        a = jax.nn.silu(h)
        expert_out = jnp.einsum('beti,ehi->beth', a, up_w)
        out = jnp.einsum('beth,bte->bth', expert_out, gate)
        return out

    def _L3_xattn_ref(Z, kv, decay, W_in, b_in, W_out, b_out, gamma, beta):
        import jax, jax.numpy as jnp
        import numpy as np
        from jax import lax
        LN_EPS = 1e-05
        B, T, D = kv.shape
        K = jax.nn.sigmoid(decay)
        x = jnp.einsum('btd,ed->bte', kv, W_in) + b_in

        def scan_fn(s, xt):
            s = K * s + xt
            return (s, s)
        s0 = jnp.zeros((B, D), dtype=kv.dtype)
        _, states = lax.scan(scan_fn, s0, jnp.swapaxes(x, 0, 1))
        states = jnp.swapaxes(states, 0, 1)
        proj = jnp.einsum('btd,ed->bte', states, W_out) + b_out
        summary = jnp.mean(proj, axis=1, keepdims=True)
        y = Z + summary
        mu = jnp.mean(y, axis=-1, keepdims=True)
        var = jnp.mean((y - mu) ** 2, axis=-1, keepdims=True)
        return (y - mu) / jnp.sqrt(var + LN_EPS) * gamma + beta

    def _L3_ffn_ref(x, Wq, keys, e_down, e_up):
        import jax, jax.numpy as jnp
        import numpy as np
        B, T, D = (2, 256, 512)
        H, K, DK = (4, 8, 64)
        E = 4096
        NK = 128
        b, t, d = x.shape
        q = (x @ Wq).reshape(b, t, H, 2, DK)
        q1, q2 = (q[..., 0, :], q[..., 1, :])
        sim1 = jnp.einsum('bthd,hkd->bthk', q1, keys[:, :, 0, :])
        sim2 = jnp.einsum('bthd,hkd->bthk', q2, keys[:, :, 1, :])
        s1, i1 = jax.lax.top_k(sim1, K)
        s2, i2 = jax.lax.top_k(sim2, K)
        all_scores = (s1[..., :, None] + s2[..., None, :]).reshape(b, t, H, K * K)
        all_indices = (i1[..., :, None] * NK + i2[..., None, :]).reshape(b, t, H, K * K)
        final_scores, pk_idx = jax.lax.top_k(all_scores, K)
        final_indices = jnp.take_along_axis(all_indices, pk_idx, axis=-1)
        w_down = e_down[final_indices]
        w_up = e_up[final_indices]
        hidden = jnp.einsum('btd,bthkd->bthk', x, w_down)
        hidden = jax.nn.silu(hidden)
        hidden = hidden * jax.nn.relu(final_scores)
        out = jnp.einsum('bthk,bthkd->btd', hidden, w_up)
        return out
    x = x + jnp.tanh(g_xattn[0]) * _L0_xattn_ref(8, 256, 512, L0_xattn_w, L0_xattn_u, _layernorm(x, axis=-1), ctx_2048)
    x = x + jnp.tanh(g_ffn[0]) * _L0_ffn_ref(_layernorm(x, axis=-1), L0_ffn_w_gate_up, L0_ffn_w_down, L0_ffn_norm_weight)
    x = x + jnp.tanh(g_xattn[1]) * _L1_xattn_ref(_layernorm(x, axis=-1), ctx_2048, L1_xattn_Wq, L1_xattn_Wg, L1_xattn_bg, L1_xattn_Wkv, L1_xattn_Wo)
    x = x + jnp.tanh(g_ffn[1]) * _L1_ffn_ref(_layernorm(x, axis=-1), L1_ffn_ln_gamma, L1_ffn_ln_beta, L1_ffn_spline_bases, L1_ffn_spline_slopes, L1_ffn_output_scale)
    x = x + jnp.tanh(g_xattn[2]) * _L2_xattn_ref(8, 256, 512, L2_xattn_time_decay, L2_xattn_time_first, _layernorm(x, axis=-1), ctx_2048)
    x = x + jnp.tanh(g_ffn[2]) * _L2_ffn_ref(_layernorm(x, axis=-1), L2_ffn_router_w, L2_ffn_down_w, L2_ffn_up_w)
    x = x + jnp.tanh(g_xattn[3]) * _L3_xattn_ref(_layernorm(x, axis=-1), ctx_2048, L3_xattn_decay, L3_xattn_W_in, L3_xattn_b_in, L3_xattn_W_out, L3_xattn_b_out, L3_xattn_gamma, L3_xattn_beta)
    x = x + jnp.tanh(g_ffn[3]) * _L3_ffn_ref(_layernorm(x, axis=-1), L3_ffn_Wq, L3_ffn_keys, L3_ffn_e_down, L3_ffn_e_up)
    return x

_drawn_inputs = setup_inputs


def setup_inputs(seed=0):
    import zlib

    import numpy as np

    out = dict(_drawn_inputs(seed))
    spreads = {'L0_ffn_norm_weight': (1.0, 0.6),
     'L1_xattn_bg': (1.0, 0.6),
     'L3_xattn_b_in': (0.0, 0.1),
     'L3_xattn_b_out': (0.0, 0.1),
     'L3_xattn_gamma': (1.0, 0.2),
     'L3_xattn_beta': (0.0, 0.1)}
    factors = {'L1_xattn_Wq': 5.108,
     'L1_ffn_ln_gamma': 8.0,
     'L1_ffn_ln_beta': 6.722,
     'L1_ffn_spline_bases': 7.588,
     'L1_ffn_spline_slopes': 8.0,
     'L1_ffn_output_scale': 8.0,
     'L3_ffn_Wq': 8.0,
     'L3_ffn_keys': 8.0,
     'L3_ffn_e_down': 8.0,
     'L3_ffn_e_up': 8.0}
    for name, (base, spread) in spreads.items():
        noise = np.random.default_rng([zlib.crc32(name.encode()), seed]).standard_normal(out[name].shape)
        drawn = base * np.exp(spread * noise) if base else spread * noise
        out[name] = jnp.asarray(drawn.astype(out[name].dtype))
    for name, factor in factors.items():
        out[name] = (out[name] * factor).astype(out[name].dtype)
    return out
```

```python
from contextlib import ExitStack

import concourse.bass as bass
from concourse import mybir

ALU = mybir.AluOpType
ACT = mybir.ActivationFunctionType
F32 = mybir.dt.float32
BF16 = mybir.dt.bfloat16
U32 = mybir.dt.uint32
AX = mybir.AxisListType

P = 128
B, T, D = 8, 256, 512
N = B * T
NT = N // P
DC = D // P
TB = T // P
LN_EPS = 1e-5
NEG = -1e38
EXP_MAX = 40.0
MAGIC = 1.5 * 2.0 ** 23


def here(i, h):
    return 2 * i + h + 3


def before(i, h):
    return 2 * i + h + 1


def both(i):
    return 2 * i + 4


class Phase:

    def __init__(self, nc, name):
        self.nc, self.name, self.ctx = nc, name, ExitStack()
        self.sems, self.pairs = [], []

    def sb(self, name, shape, dt=F32):
        return self.ctx.enter_context(self.nc.sbuf_tensor(f"{self.name}_{name}", shape, dt))

    def ps(self, name, shape, dt=F32):
        return self.ctx.enter_context(self.nc.psum_tensor(f"{self.name}_{name}", shape, dt))

    def sem(self, name):
        s = self.ctx.enter_context(self.nc.semaphore(f"{self.name}_{name}"))
        self.sems.append(s)
        return s

    def pair_sem(self, name):
        s = self.sem(name)
        self.pairs.append(s)
        return s

    def start(self):
        with self.nc.Block(no_gpsimd_drain=True) as block:
            @block.sync
            def _(sp):
                for s in self.sems:
                    sp.sem_clear(s)
                for s in self.pairs:
                    sp.sem_inc(s, 2)
        return self.ctx.enter_context(self.nc.Block(no_gpsimd_drain=True))

    def end(self):
        self.ctx.close()


def row_stats(dve, stats, m, var, w1, w2, step, at):
    dve.tensor_tensor(w1, stats[:, :, 1], stats[:, :, 4], ALU.add).then_inc(step, 1)
    dve.tensor_tensor(w2, stats[:, :, 1], stats[:, :, 4], ALU.subtract).then_inc(step, 1)
    dve.tensor_tensor(var, stats[:, :, 2], stats[:, :, 5], ALU.add).then_inc(step, 1)
    dve.wait_ge(step, at + 3)
    dve.tensor_scalar(m, w1, 0.5, None, ALU.mult).then_inc(step, 1)
    dve.scalar_tensor_tensor(w2, w2, 0.25, w2, ALU.mult, ALU.mult).then_inc(step, 1)
    dve.wait_ge(step, at + 5)
    dve.scalar_tensor_tensor(var, var, 1.0 / D, w2, ALU.mult, ALU.add).then_inc(step, 1)
    return at + 6


def rsqrt(dve, act_ask, act_said, asked, out, a, root, w, step, at):
    dve.wait_ge(step, at)
    dve.sem_inc(act_ask, 1)
    dve.wait_ge(act_said, asked)
    dve.reciprocal(out, root).then_inc(step, 1)
    dve.wait_ge(step, at + 1)
    dve.tensor_tensor(w, out, out, ALU.mult).then_inc(step, 1)
    dve.wait_ge(step, at + 2)
    dve.tensor_tensor(w, w, a, ALU.mult).then_inc(step, 1)
    dve.wait_ge(step, at + 3)
    dve.tensor_scalar(w, w, -0.5, 1.5, ALU.mult, ALU.add).then_inc(step, 1)
    dve.wait_ge(step, at + 4)
    dve.tensor_tensor(out, out, w, ALU.mult).then_inc(step, 1)
    return at + 5


def setup_phase(nc, R, A):
    ph = Phase(nc, "setup")
    g = ph.sb("g", [P, 8])
    x_in, g_in = [ph.sem(f"x_in{k}") for k in range(4)], ph.sem("g_in")
    zeroed, made, gated, stated = ph.sem("zeroed"), ph.sem("made"), ph.sem("gated"), ph.sem("stated")
    X, ident, identb, ones, tg, stats = R["X"], R["ident"], R["identb"], R["ones"], R["tg"], R["stats"]
    block = ph.start()
    QT = NT // 4

    @block.sync
    def _(sp):
        for k in range(4):
            sp.dma_start(X[:, k * QT:(k + 1) * QT, :],
                         A["x"].rearrange("(t p) c -> p t c", p=P)[:, k * QT:(k + 1) * QT, :]).then_inc(x_in[k], 16)
        sp.dma_start(g[:, 0:4], A["g_xattn"].partition_broadcast(P)).then_inc(g_in, 16)
        sp.dma_start(g[:, 4:8], A["g_ffn"].partition_broadcast(P)).then_inc(g_in, 16)

    @block.gpsimd
    def _(pool):
        pool.memset(ident[:, :], 0.0).then_inc(zeroed, 1)
        pool.memset(ones[:, :], 1.0).then_inc(made, 1)
        pool.memset(R["magic"][:, 0:1], MAGIC)
        pool.memset(R["magic"][:, 1:2], -MAGIC)
        pool.wait_ge(zeroed, 1)
        pool.affine_select(out=ident[:, :], in_=ident[:, :], compare_op=ALU.not_equal, fill=1.0, base=0,
                           pattern=[[-1, P]], channel_multiplier=1).then_inc(made, 1)

    @block.scalar
    def _(act):
        act.wait_ge(g_in, 32)
        act.activation(tg[:, :], g[:, :], ACT.Tanh).then_inc(gated, 1)

    @block.vector
    def _(dve):
        dve.wait_ge(made, 2)
        dve.tensor_copy(identb[:, :], ident[:, :]).then_inc(stated, 1)
        for k in range(4):
            dve.wait_ge(x_in[k], 16)
            with dve.Fori(k * QT, (k + 1) * QT) as t:
                dve.bn_stats(stats[:, t, :], X[:, t, :]).then_inc(stated, 1)

    ph.end()


def wkv_phase(nc, R, A, name, gate, w_name, u_name, negate_exp):
    ph = Phase(nc, name)
    X, ident, tg, stats = R["X"], R["ident"], R["tg"], R["stats"]
    NP = B // 2
    m, var, rstd, root, w1, w2 = (ph.sb(n, [P, NT]) for n in ("m", "var", "rstd", "root", "w1", "w2"))
    w, u = ph.sb("w", [P, DC]), ph.sb("u", [P, DC])

    def two(n, shape):
        return [ph.sb(f"{n}{h}", shape) for h in range(2)]

    xn = two("xn", [P, TB, D])
    kT, vT = two("kT", [P, DC, T]), two("vT", [P, DC, T])
    o, p, q = (two(n, [P, DC, T + 1]) for n in "opq")
    a, e, g = two("a", [P, DC, T]), two("e", [P, DC, T]), two("g", [P, DC, T])
    ev, num, r, tt = two("ev", [P, DC, T]), two("num", [P, DC, T]), two("r", [P, DC, T]), two("tt", [P, DC, T])
    k_ps = [ph.ps(f"k_ps{j}", [P, DC, P]) for j in range(4)]
    y_ps = [ph.ps(f"y_ps{j}", [P, DC, P]) for j in range(4)]

    wu_in, v_in = ph.sem("wu_in"), [ph.pair_sem(f"v_in{h}") for h in range(2)]
    step, asked, rooted, w_ready = ph.sem("step"), ph.sem("asked"), ph.sem("rooted"), ph.sem("w_ready")
    inited = ph.sem("inited")
    xn_ready, xn_used, k_ready = ph.pair_sem("xn_ready"), ph.pair_sem("xn_used"), ph.pair_sem("k_ready")
    o_ready, da_ready, de_ready, dg_ready, gc_ready = (ph.pair_sem(n) for n in ("o_ready", "da", "de", "dg", "gc"))
    a_ready, e_ready, g_ready, ev_ready = (ph.pair_sem(n) for n in ("a_ready", "e_ready", "g_ready", "ev_ready"))
    pq_ready, qv_ready, num_ready, den_ready = (ph.pair_sem(n) for n in ("pq", "qv", "num", "den"))
    ln_ready, r_ready, t_ready, r2_ready, yd_ready = (ph.pair_sem(n) for n in ("ln", "r", "t", "r2", "yd"))
    y_ready, yT_ready, x_ready, st_ready = (ph.pair_sem(n) for n in ("y", "yT", "x", "st"))
    block = ph.start()

    @block.sync
    def _(sp):
        sp.dma_start(w[:, :], A[w_name].rearrange("(c p) -> p c", p=P),
                     allow_slow_non_contiguous=True).then_inc(wu_in, 16)
        sp.dma_start(u[:, :], A[u_name].rearrange("(c p) -> p c", p=P),
                     allow_slow_non_contiguous=True).then_inc(wu_in, 16)
        ctxT = A["ctxT"].rearrange("(c p) n -> p c n", p=P)
        with sp.Fori(0, NP) as i:
            for h in range(2):
                sp.wait_ge(y_ready, before(i, h))
                sp.dma_start(vT[h][:, :, :], ctxT[:, :, bass.ds((2 * i + h) * T, T)]).then_inc(v_in[h], 16)

    @block.tensor
    def _(pe):
        with pe.Fori(0, NP) as i:
            for h in range(2):
                pe.wait_ge(xn_ready, here(i, h))
                pe.wait_ge(k_ready, before(i, h))
                for j in range(TB):
                    for c in range(DC):
                        last = pe.transpose(k_ps[2 * h + j][:, c, :], xn[h][:, j, c * P:(c + 1) * P], ident[:, :])
                last.then_inc(xn_used, 1)
            for h in range(2):
                pe.wait_ge(y_ready, here(i, h))
                pe.wait_ge(x_ready, before(i, h))
                for j in range(TB):
                    for c in range(DC):
                        last = pe.transpose(y_ps[2 * h + j][:, c, :], tt[h][:, c, j * P:(j + 1) * P], ident[:, :])
                last.then_inc(yT_ready, 1)

    @block.scalar
    def _(act):
        act.wait_ge(wu_in, 32)
        if negate_exp:
            act.activation(w[:, :], w[:, :], ACT.Exp).then_inc(w_ready, 1)
        act.wait_ge(asked, 1)
        act.activation(root[:, :], var[:, :], ACT.Sqrt).then_inc(rooted, 1)
        act.wait_ge(inited, 1)
        with act.Fori(0, NP) as i:
            for h in range(2):
                act.wait_ge(xn_used, here(i, h))
                act.wait_ge(g_ready, before(i, h))
                for j in range(TB):
                    last = act.activation(kT[h][:, :, j * P:(j + 1) * P], k_ps[2 * h + j][:, :, :], ACT.Copy)
                last.then_inc(k_ready, 1)
            for h in range(2):
                act.wait_ge(da_ready, here(i, h))
                for c in range(DC):
                    last = act.activation(a[h][:, c, :], a[h][:, c, :], ACT.Exp, bias=w[:, c:c + 1])
                last.then_inc(a_ready, 1)
                act.wait_ge(de_ready, here(i, h))
                act.activation(e[h][:, :, :], e[h][:, :, :], ACT.Exp).then_inc(e_ready, 1)
                act.wait_ge(gc_ready, here(i, h))
                act.activation(g[h][:, :, :], g[h][:, :, :], ACT.Exp).then_inc(g_ready, 1)
            for h in range(2):
                act.wait_ge(den_ready, here(i, h))
                act.wait_ge(yd_ready, before(i, h))
                act.activation(r[h][:, :, :], g[h][:, :, :], ACT.Ln).then_inc(ln_ready, 1)
                act.wait_ge(ln_ready, here(i, h))
                act.activation(r[h][:, :, :], r[h][:, :, :], ACT.Exp, scale=-1.0).then_inc(r_ready, 1)

    @block.gpsimd
    def _(pool):
        with pool.Fori(0, NP) as i:
            for h in range(2):
                pool.wait_ge(o_ready, here(i, h))
                pool.wait_ge(k_ready, here(i, h))
                pool.wait_ge(t_ready, before(i, h))
                pool.tensor_tensor(g[h][:, :, :], kT[h][:, :, :], o[h][:, :, 0:T], ALU.subtract).then_inc(dg_ready, 1)
            for h in range(2):
                pool.wait_ge(v_in[h], 16 * i + 18)
                pool.wait_ge(e_ready, here(i, h))
                pool.wait_ge(pq_ready, before(i, h))
                pool.tensor_tensor(ev[h][:, :, :], e[h][:, :, :], vT[h][:, :, :], ALU.mult).then_inc(ev_ready, 1)
            for h in range(2):
                pool.wait_ge(pq_ready, here(i, h))
                pool.wait_ge(yd_ready, before(i, h))
                pool.tensor_tensor(num[h][:, :, :], q[h][:, :, 0:T], vT[h][:, :, :], ALU.mult).then_inc(qv_ready, 1)
                pool.wait_ge(qv_ready, here(i, h))
                pool.tensor_tensor(num[h][:, :, :], p[h][:, :, 0:T], num[h][:, :, :], ALU.subtract).then_inc(num_ready, 1)

    @block.vector
    def _(dve):
        n = row_stats(dve, stats, m[:, :], var[:, :], w1[:, :], w2[:, :], step, 0)
        dve.wait_ge(step, n)
        dve.tensor_scalar(var[:, :], var[:, :], LN_EPS, None, ALU.add).then_inc(step, 1)
        n = rsqrt(dve, asked, rooted, 1, rstd[:, :], var[:, :], root[:, :], w1[:, :], step, n + 1)
        for h in range(2):
            dve.memset(o[h][:, :, 0:1], NEG).then_inc(step, 1)
            dve.memset(p[h][:, :, 0:1], 0.0).then_inc(step, 1)
            dve.memset(q[h][:, :, 0:1], 0.0).then_inc(step, 1)
        dve.wait_ge(wu_in, 32)
        if negate_exp:
            dve.wait_ge(w_ready, 1)
            dve.tensor_scalar(w[:, :], w[:, :], -1.0, None, ALU.mult).then_inc(step, 1)
        dve.wait_ge(step, n + 6 + int(negate_exp))
        dve.sem_inc(inited, 1)
        with dve.Fori(0, NP) as i:
            for h in range(2):
                dve.wait_ge(xn_used, before(i, h))
                for j in range(TB):
                    t = (2 * i + h) * TB + j
                    last = dve.tensor_scalar(xn[h][:, j, :], X[:, t, :], m[:, bass.ds(t, 1)], rstd[:, bass.ds(t, 1)],
                                             ALU.subtract, ALU.mult)
                last.then_inc(xn_ready, 1)
            for h in range(2):
                dve.wait_ge(k_ready, here(i, h))
                dve.wait_ge(dg_ready, before(i, h))
                for c in range(DC):
                    last = dve.tensor_tensor_scan(o[h][:, c, 1:T + 1], w[:, c:c + 1].to_broadcast([P, T]),
                                                  kT[h][:, c, :], NEG, ALU.add, ALU.max)
                last.then_inc(o_ready, 1)
            for h in range(2):
                dve.wait_ge(o_ready, here(i, h))
                dve.tensor_tensor(a[h][:, :, :], o[h][:, :, 0:T], o[h][:, :, 1:T + 1], ALU.subtract).then_inc(da_ready, 1)
                dve.tensor_tensor(e[h][:, :, :], kT[h][:, :, :], o[h][:, :, 1:T + 1], ALU.subtract).then_inc(de_ready, 1)
            for h in range(2):
                dve.wait_ge(dg_ready, here(i, h))
                for c in range(DC):
                    last = dve.tensor_scalar(g[h][:, c, :], g[h][:, c, :], u[:, c:c + 1], EXP_MAX, ALU.add, ALU.min)
                last.then_inc(gc_ready, 1)
            for h in range(2):
                dve.wait_ge(a_ready, here(i, h))
                dve.wait_ge(ev_ready, here(i, h))
                dve.wait_ge(num_ready, before(i, h))
                for c in range(DC):
                    dve.tensor_tensor_scan(p[h][:, c, 1:T + 1], a[h][:, c, :], ev[h][:, c, :], 0.0, ALU.mult, ALU.add)
                    last = dve.tensor_tensor_scan(q[h][:, c, 1:T + 1], a[h][:, c, :], e[h][:, c, :], 0.0, ALU.mult, ALU.add)
                last.then_inc(pq_ready, 1)
            for h in range(2):
                dve.wait_ge(pq_ready, here(i, h))
                dve.wait_ge(g_ready, here(i, h))
                dve.tensor_tensor(g[h][:, :, :], q[h][:, :, 0:T], g[h][:, :, :], ALU.add).then_inc(den_ready, 1)
            for h in range(2):
                dve.wait_ge(r_ready, here(i, h))
                dve.wait_ge(yT_ready, before(i, h))
                dve.tensor_tensor(tt[h][:, :, :], g[h][:, :, :], r[h][:, :, :], ALU.mult).then_inc(t_ready, 1)
            for h in range(2):
                dve.wait_ge(t_ready, here(i, h))
                dve.scalar_tensor_tensor(r[h][:, :, :], tt[h][:, :, :], -2.0, r[h][:, :, :], ALU.add, ALU.mult).then_inc(r2_ready, 1)
            for h in range(2):
                dve.wait_ge(r2_ready, here(i, h))
                dve.wait_ge(num_ready, here(i, h))
                dve.tensor_tensor(tt[h][:, :, :], num[h][:, :, :], r[h][:, :, :], ALU.mult).then_inc(yd_ready, 1)
            for h in range(2):
                dve.wait_ge(yd_ready, here(i, h))
                dve.wait_ge(v_in[h], 16 * i + 18)
                dve.tensor_tensor(tt[h][:, :, :], vT[h][:, :, :], tt[h][:, :, :], ALU.subtract).then_inc(y_ready, 1)
            for h in range(2):
                dve.wait_ge(yT_ready, here(i, h))
                for j in range(TB):
                    t = (2 * i + h) * TB + j
                    last = dve.scalar_tensor_tensor(X[:, t, :], y_ps[2 * h + j][:, :, :].rearrange("p c n -> p (c n)"),
                                                    tg[:, gate:gate + 1], X[:, t, :], ALU.mult, ALU.add)
                last.then_inc(x_ready, 1)
            for h in range(2):
                dve.wait_ge(x_ready, here(i, h))
                for j in range(TB):
                    t = (2 * i + h) * TB + j
                    last = dve.bn_stats(stats[:, t, :], X[:, t, :])
                last.then_inc(st_ready, 1)

    ph.end()


def ternary_phase(nc, R, A, wgu_q, wd_q, unit):
    ph = Phase(nc, "ternary")
    F = A["L0_ffn_w_downT"].shape[0]
    FC = F // P
    wgu, wd = ph.sb("wgu", [P, DC, 2 * F]), ph.sb("wd", [P, FC, D])
    junk = ph.sb("junk", [P, 2 * F], BF16)
    sums, tot, scale = ph.sb("sums", [P, DC + 1]), ph.sb("tot", [P, 2]), ph.sb("scale", [P, 2])
    s_ps = ph.ps("s_ps", [P, DC + 1])
    wgu_in, wd_in = [ph.sem(f"wgu_in{c}") for c in range(DC)], ph.sem("wd_in")
    summed, d_summed, added, step = ph.sem("summed"), ph.sem("d_summed"), ph.sem("added"), ph.sem("step")
    scaled, clipped, done = ph.sem("scaled"), ph.sem("clipped"), ph.sem("done")
    block = ph.start()
    parts = [(wgu[:, c, :], wgu_q[:, c, :], 0) for c in range(DC)] + [(wd[:, :, :], wd_q[:, :, :], 1)]

    @block.sync
    def _(sp):
        for c in range(DC):
            sp.dma_start(wgu[:, c, :], A["L0_ffn_w_gate_upT"][c * P:(c + 1) * P, :]).then_inc(wgu_in[c], 16)
        sp.dma_start(wd[:, :, :], A["L0_ffn_w_downT"].rearrange("(f p) n -> p f n", p=P)).then_inc(wd_in, 16)

    @block.tensor
    def _(pe):
        pe.wait_ge(summed, DC)
        pe.wait_ge(d_summed, 1)
        pe.matmul(s_ps[:, :], lhsT=R["ones"][:, :], rhs=sums[:, :], start=True, stop=True).then_inc(added, 1)

    @block.scalar
    def _(act):
        for c in range(DC):
            act.wait_ge(wgu_in[c], 16)
            if c:
                act.wait_ge(summed, c)
            act.activation(junk[:, :], wgu[:, c, :], ACT.Abs, accum_out=sums[:, c:c + 1]).then_inc(summed, 1)
        act.wait_ge(step, 5)
        for w, _, k in parts:
            act.activation(w, w, ACT.Identity, scale=scale[:, k:k + 1], bias=R["magic"][:, 0:1]).then_inc(scaled, 1)
        for n, (w, q, _) in enumerate(parts):
            act.wait_ge(clipped, n + 1)
            act.activation(q, w, ACT.Identity, bias=R["magic"][:, 1:2]).then_inc(done, 1)

    @block.gpsimd
    def _(pool):
        for n, (w, _, _) in enumerate(parts):
            pool.wait_ge(scaled, n + 1)
            pool.tensor_scalar(w, w, MAGIC + 1, MAGIC - 1, ALU.min, ALU.max).then_inc(clipped, 1)

    @block.vector
    def _(dve):
        dve.wait_ge(wd_in, 16)
        dve.tensor_reduce(sums[:, DC:DC + 1], wd[:, :, :].rearrange("p f n -> p (f n)"), AX.X, ALU.add,
                          apply_absolute_value=True).then_inc(d_summed, 1)
        dve.wait_ge(added, 1)
        dve.tensor_reduce(tot[:, 0:1], s_ps[:, 0:DC], AX.X, ALU.add).then_inc(step, 1)
        dve.tensor_copy(tot[:, 1:2], s_ps[:, DC:DC + 1]).then_inc(step, 1)
        dve.wait_ge(step, 2)
        dve.tensor_scalar(unit[:, 0:1], tot[:, 0:1], 1.0 / (2 * F * D), 1e-5, ALU.mult, ALU.max).then_inc(step, 1)
        dve.tensor_scalar(unit[:, 1:2], tot[:, 1:2], 1.0 / (F * D), 1e-5, ALU.mult, ALU.max).then_inc(step, 1)
        dve.wait_ge(step, 4)
        dve.reciprocal(scale[:, :], unit[:, 0:2]).then_inc(step, 1)

    ph.end()


def bitnet_phase(nc, R, A, wgu_q, wd_q, unit, gate):
    ph = Phase(nc, "L0f")
    X, identb, tg, stats, magic = R["X"], R["identb"], R["tg"], R["stats"], R["magic"]
    F = wd_q.shape[1] * P
    FC = F // P
    NP = NT // 2
    CH = [(j, min(512, F - j)) for j in range(0, F, 512)]
    NCH = len(CH)
    m, var, r1, r2, root, w1, w2 = (ph.sb(n, [P, NT]) for n in ("m", "var", "r1", "r2", "root", "w1", "w2"))
    nw = ph.sb("nw", [P, D])

    def two(n, shape, dt=F32):
        return [ph.sb(f"{n}{h}", shape, dt) for h in range(2)]

    xn, xq, xqT = two("xn", [P, D]), two("xq", [P, D], BF16), two("xqT", [P, DC, P], BF16)
    s = two("s", [P, 8])
    rl, hid = two("rl", [P, 512]), two("hid", [P, F])
    hq, hqT = two("hq", [P, F], BF16), two("hqT", [P, FC, P], BF16)
    x_ps = ph.ps("x_ps", [P, DC, P], BF16)
    g_ps, u_ps = [ph.ps(f"g_ps{k}", [P, 512]) for k in range(2)], [ph.ps(f"u_ps{k}", [P, 512]) for k in range(2)]
    h_ps = [ph.ps(f"h_ps{k}", [P, 8, P], BF16) for k in range(2)]
    o_ps = ph.ps("o_ps", [P, D])
    nw_in, step, asked, rooted = ph.sem("nw_in"), ph.sem("step"), ph.sem("asked"), ph.sem("rooted")
    xn_ready, xw_ready, am_ready, ac_ready, ar_ready, as_ready = (ph.pair_sem(n) for n in ("xn", "xw", "am", "ac", "ar", "as"))
    xm_ready, xq_ready, x_turned, xqT_ready = (ph.pair_sem(n) for n in ("xm", "xq", "x_turned", "xqT"))
    gu_ready, rl_ready, sq_ready, hid_ready = (ph.pair_sem(n) for n in ("gu", "rl", "sq", "hid"))
    hm_ready, c3_ready, hc_ready, hr_ready, hs_ready, hk_ready, hq_ready = (ph.pair_sem(n) for n in ("hm", "c3", "hc", "hr", "hs", "hk", "hq"))
    h_turned, hqT_ready, o_ready, x_ready, st_ready = (ph.pair_sem(n) for n in ("h_turned", "hqT", "o", "x", "st"))
    block = ph.start()

    @block.sync
    def _(sp):
        sp.dma_start(nw[:, :], A["L0_ffn_norm_weight"].partition_broadcast(P)).then_inc(nw_in, 16)

    @block.tensor
    def _(pe):
        def front(i):
            for h in range(2):
                pe.wait_ge(xq_ready, here(i, h))
                pe.wait_ge(xqT_ready, here(i, h) - 1)
                for c in range(DC):
                    last = pe.transpose(x_ps[:, c, :], xq[h][:, c * P:(c + 1) * P], identb[:, :])
                last.then_inc(x_turned, 1)

        def up(i, h):
            pe.wait_ge(xqT_ready, here(i, h))
            for j, (f0, fn) in enumerate(CH):
                k = NCH * h + j
                pe.wait_ge(hid_ready, 2 * NCH * i + k + 1)
                for c in range(DC):
                    pe.matmul(g_ps[k % 2][:, 0:fn], lhsT=xqT[h][:, c, :], rhs=wgu_q[:, c, f0:f0 + fn],
                              start=(c == 0), stop=(c == DC - 1))
                for c in range(DC):
                    last = pe.matmul(u_ps[k % 2][:, 0:fn], lhsT=xqT[h][:, c, :], rhs=wgu_q[:, c, F + f0:F + f0 + fn],
                                     start=(c == 0), stop=(c == DC - 1))
                last.then_inc(gu_ready, 1)

        def down(i, h):
            pe.wait_ge(hq_ready, here(i, h))
            pe.wait_ge(hqT_ready, here(i, h) - 1)
            for f in range(FC):
                last = pe.transpose(h_ps[f // 8][:, f % 8, :], hq[h][:, f * P:(f + 1) * P], identb[:, :])
            last.then_inc(h_turned, 1)
            pe.wait_ge(hqT_ready, here(i, h))
            pe.wait_ge(x_ready, here(i, h) - 1)
            for f in range(FC):
                last = pe.matmul(o_ps[:, :], lhsT=hqT[h][:, f, :], rhs=wd_q[:, f, :], start=(f == 0), stop=(f == FC - 1))
            last.then_inc(o_ready, 1)

        front(0)
        up(0, 0)
        up(0, 1)
        front(1)
        with pe.Fori(0, NP - 2) as i:
            up(i + 1, 0)
            down(i, 0)
            up(i + 1, 1)
            front(i + 2)
            down(i, 1)
        up(NP - 1, 0)
        down(NP - 2, 0)
        up(NP - 1, 1)
        down(NP - 2, 1)
        down(NP - 1, 0)
        down(NP - 1, 1)

    @block.scalar
    def _(act):
        for n in range(2):
            act.wait_ge(asked, n + 1)
            act.activation(root[:, :], var[:, :], ACT.Sqrt).then_inc(rooted, 1)

        def used(i, h):
            return 1 if isinstance(i, int) and i == 0 else 2 * NCH * i - NCH * (1 - h) + 2

        def front(i):
            for h in range(2):
                act.wait_ge(x_turned, here(i, h))
                act.wait_ge(gu_ready, used(i, h))
                act.activation(xqT[h][:, :, :], x_ps[:, :, :], ACT.Copy).then_inc(xqT_ready, 1)

        def up(i, h):
            for j, (f0, fn) in enumerate(CH):
                k = NCH * h + j
                act.wait_ge(gu_ready, 2 * NCH * i + k + 3)
                act.activation(rl[k % 2][:, 0:fn], g_ps[k % 2][:, 0:fn], ACT.Relu).then_inc(rl_ready, 1)
                act.wait_ge(rl_ready, 2 * NCH * i + k + 3)
                act.activation(rl[k % 2][:, 0:fn], rl[k % 2][:, 0:fn], ACT.Square).then_inc(sq_ready, 1)

        def down(i, h):
            act.wait_ge(h_turned, here(i, h))
            act.wait_ge(o_ready, before(i, h))
            act.activation(hqT[h][:, 0:8, :], h_ps[0][:, :, :], ACT.Copy)
            act.activation(hqT[h][:, 8:FC, :], h_ps[1][:, 0:FC - 8, :], ACT.Copy).then_inc(hqT_ready, 1)

        front(0)
        up(0, 0)
        up(0, 1)
        front(1)
        with act.Fori(0, NP - 2) as i:
            up(i + 1, 0)
            down(i, 0)
            up(i + 1, 1)
            front(i + 2)
            down(i, 1)
        up(NP - 1, 0)
        down(NP - 2, 0)
        up(NP - 1, 1)
        down(NP - 2, 1)
        down(NP - 1, 0)
        down(NP - 1, 1)

    @block.gpsimd
    def _(pool):
        def round_hidden(i, h):
            pool.wait_ge(hk_ready, here(i, h))
            pool.wait_ge(h_turned, before(i, h))
            pool.tensor_tensor(hq[h][:, :], hid[h][:, :], magic[:, 1:2].to_broadcast([P, F]), ALU.add).then_inc(hq_ready, 1)

        with pool.Fori(0, NP) as i:
            round_hidden(i, 0)
            round_hidden(i, 1)

    @block.vector
    def _(dve):
        n = row_stats(dve, stats, m[:, :], var[:, :], w1[:, :], w2[:, :], step, 0)
        dve.wait_ge(step, n)
        dve.tensor_scalar(w2[:, :], var[:, :], 1.0, None, ALU.mult).then_inc(step, 1)
        dve.wait_ge(step, n + 1)
        dve.tensor_scalar(var[:, :], var[:, :], LN_EPS, None, ALU.add).then_inc(step, 1)
        n = rsqrt(dve, asked, rooted, 1, r1[:, :], var[:, :], root[:, :], w1[:, :], step, n + 2)
        dve.wait_ge(step, n)
        dve.tensor_tensor(w2[:, :], w2[:, :], r1[:, :], ALU.mult).then_inc(step, 1)
        dve.wait_ge(step, n + 1)
        dve.tensor_tensor(w2[:, :], w2[:, :], r1[:, :], ALU.mult).then_inc(step, 1)
        dve.wait_ge(step, n + 2)
        dve.tensor_scalar(var[:, :], w2[:, :], LN_EPS, None, ALU.add).then_inc(step, 1)
        n = rsqrt(dve, asked, rooted, 2, r2[:, :], var[:, :], root[:, :], w1[:, :], step, n + 3)
        dve.wait_ge(step, n)
        dve.wait_ge(nw_in, 16)

        def front(i):
            for h in range(2):
                t = 2 * i + h
                dve.wait_ge(xm_ready, before(i, h))
                dve.tensor_scalar(xn[h][:, :], X[:, t, :], m[:, bass.ds(t, 1)], r1[:, bass.ds(t, 1)],
                                  ALU.subtract, ALU.mult).then_inc(xn_ready, 1)
            for h in range(2):
                dve.wait_ge(xn_ready, here(i, h))
                dve.tensor_tensor(xn[h][:, :], xn[h][:, :], nw[:, :], ALU.mult).then_inc(xw_ready, 1)
            for h in range(2):
                dve.wait_ge(xw_ready, here(i, h))
                dve.wait_ge(as_ready, before(i, h))
                dve.tensor_reduce(s[h][:, 0:1], xn[h][:, :], AX.X, ALU.max, apply_absolute_value=True).then_inc(am_ready, 1)
            for h in range(2):
                t = 2 * i + h
                dve.wait_ge(am_ready, here(i, h))
                dve.tensor_scalar(s[h][:, 0:1], s[h][:, 0:1], r2[:, bass.ds(t, 1)], 1e-5, ALU.mult, ALU.max).then_inc(ac_ready, 1)
            for h in range(2):
                dve.wait_ge(ac_ready, here(i, h))
                dve.reciprocal(s[h][:, 1:2], s[h][:, 0:1]).then_inc(ar_ready, 1)
            for h in range(2):
                t = 2 * i + h
                dve.wait_ge(ar_ready, here(i, h))
                dve.tensor_scalar(s[h][:, 1:2], s[h][:, 1:2], 127.0, r2[:, bass.ds(t, 1)], ALU.mult, ALU.mult).then_inc(as_ready, 1)
            for h in range(2):
                dve.wait_ge(as_ready, here(i, h))
                dve.tensor_scalar(xn[h][:, :], xn[h][:, :], s[h][:, 1:2], MAGIC, ALU.mult, ALU.add).then_inc(xm_ready, 1)
            for h in range(2):
                dve.wait_ge(xm_ready, here(i, h))
                dve.wait_ge(x_turned, before(i, h))
                dve.tensor_scalar(xq[h][:, :], xn[h][:, :], MAGIC, None, ALU.subtract).then_inc(xq_ready, 1)

        def scales(i, h):
            dve.wait_ge(c3_ready, before(i, h))
            dve.tensor_scalar(s[h][:, 2:3], s[h][:, 0:1], 1.0 / 127.0, unit[:, 0:1], ALU.mult, ALU.mult).then_inc(c3_ready, 1)

        def hidden(i, h):
            for j, (f0, fn) in enumerate(CH):
                k = NCH * h + j
                dve.wait_ge(sq_ready, 2 * NCH * i + k + 3)
                if j == 0:
                    dve.wait_ge(hq_ready, before(i, h))
                dve.tensor_tensor(hid[h][:, f0:f0 + fn], rl[k % 2][:, 0:fn], u_ps[k % 2][:, 0:fn], ALU.mult).then_inc(hid_ready, 1)

        def quantise(i, h):
            dve.wait_ge(hid_ready, 2 * NCH * i + NCH * h + NCH + 2)
            dve.tensor_reduce(s[h][:, 3:4], hid[h][:, :], AX.X, ALU.max, apply_absolute_value=True)
            dve.wait_ge(c3_ready, here(i, h))
            dve.tensor_scalar(s[h][:, 4:5], s[h][:, 2:3], s[h][:, 2:3], s[h][:, 2:3], ALU.mult, ALU.mult).then_inc(hm_ready, 1)
            dve.wait_ge(hm_ready, here(i, h))
            dve.tensor_scalar(s[h][:, 5:6], s[h][:, 3:4], s[h][:, 4:5], 1e-5, ALU.mult, ALU.max).then_inc(hc_ready, 1)
            dve.wait_ge(hc_ready, here(i, h))
            dve.reciprocal(s[h][:, 6:7], s[h][:, 5:6]).then_inc(hr_ready, 1)
            dve.tensor_scalar(s[h][:, 7:8], s[h][:, 5:6], 1.0 / 127.0, unit[:, 2:3], ALU.mult, ALU.mult)
            dve.wait_ge(hr_ready, here(i, h))
            dve.tensor_scalar(s[h][:, 6:7], s[h][:, 6:7], 127.0, s[h][:, 4:5], ALU.mult, ALU.mult).then_inc(hs_ready, 1)
            dve.wait_ge(hs_ready, here(i, h))
            dve.tensor_scalar(hid[h][:, :], hid[h][:, :], s[h][:, 6:7], MAGIC, ALU.mult, ALU.add).then_inc(hk_ready, 1)

        def out(i, h):
            t = 2 * i + h
            dve.wait_ge(o_ready, here(i, h))
            dve.scalar_tensor_tensor(X[:, bass.ds(t, 1), :], o_ps[:, :].unsqueeze(1), s[h][:, 7:8], X[:, bass.ds(t, 1), :],
                                     ALU.mult, ALU.add).then_inc(x_ready, 1)
            dve.wait_ge(x_ready, here(i, h))
            dve.bn_stats(stats[:, t, :], X[:, t, :]).then_inc(st_ready, 1)

        dve.tensor_scalar(unit[:, 2:3], unit[:, 1:2], tg[:, gate:gate + 1], None, ALU.mult).then_inc(step, 1)
        dve.wait_ge(step, n + 1)
        front(0)
        for h in range(2):
            scales(0, h)
        for h in range(2):
            hidden(0, h)
            quantise(0, h)
        front(1)
        with dve.Fori(0, NP - 2) as i:
            for h in range(2):
                scales(i + 1, h)
            hidden(i + 1, 0)
            out(i, 0)
            quantise(i + 1, 0)
            front(i + 2)
            hidden(i + 1, 1)
            out(i, 1)
            quantise(i + 1, 1)
        for h in range(2):
            scales(NP - 1, h)
        for h in range(2):
            hidden(NP - 1, h)
            out(NP - 2, h)
            quantise(NP - 1, h)
        for h in range(2):
            out(NP - 1, h)

    ph.end()


def summary_phase(nc, R, A, KV):
    ph = Phase(nc, "L1s")
    W = ph.sb("W", [P, DC, 2 * D])
    HD = 32
    mask = ph.sb("mask", [P, P // HD, HD])

    def two(n, shape, dt=F32):
        return [ph.sb(f"{n}{h}", shape, dt) for h in range(2)]

    ct, e, k, v = two("ct", [P, DC, P]), two("e", [P, D]), two("k", [P, D]), two("v", [P, DC, 2, P])
    k_ps, v_ps = [ph.ps(f"k_ps{h}", [P, D]) for h in range(2)], [ph.ps(f"v_ps{h}", [P, D]) for h in range(2)]
    s_ps = [ph.ps(f"s_ps{g}", [P, 2, 2, P]) for g in range(2)]
    w_in, c_in = ph.sem("w_in"), [ph.sem(f"c_in{h}") for h in range(2)]
    masked, filled = ph.sem("masked"), ph.sem("filled")
    kv_ready, r_ready, e_ready, k_ready, v_ready, s_ready = (ph.pair_sem(n) for n in ("kv", "r", "e", "k", "v", "s"))
    KV_ready = ph.pair_sem("KV")
    block = ph.start()

    @block.sync
    def _(sp):
        sp.dma_start(W[:, :, :], A["L1_xattn_WkvT"].rearrange("(c p) n -> p c n", p=P)).then_inc(w_in, 16)
        ctxT = A["ctxT"].rearrange("(c p) n -> p c n", p=P)
        with sp.Fori(0, B) as i:
            for h in range(2):
                sp.wait_ge(kv_ready, before(i, h))
                sp.dma_start(ct[h][:, :, :], ctxT[:, :, bass.ds((TB * i + h) * P, P)]).then_inc(c_in[h], 16)

    @block.gpsimd
    def _(pool):
        pool.memset(mask[:, :, :], 1.0).then_inc(masked, 1)
        pool.wait_ge(masked, 1)
        pool.affine_select(out=mask[:, :, :], in_=mask[:, :, :], compare_op=ALU.is_ge, fill=0.0, base=0,
                           pattern=[[-HD, P // HD], [0, HD]], channel_multiplier=1).then_inc(masked, 1)
        pool.wait_ge(masked, 2)
        pool.affine_select(out=mask[:, :, :], in_=mask[:, :, :], compare_op=ALU.is_ge, fill=0.0, base=HD - 1,
                           pattern=[[HD, P // HD], [0, HD]], channel_multiplier=-1).then_inc(masked, 1)
        for h in range(2):
            pool.memset(v[h][:, :, 1, :], 1.0).then_inc(filled, 1)

    @block.tensor
    def _(pe):
        pe.wait_ge(w_in, 16)
        pe.wait_ge(filled, 2)
        with pe.Fori(0, B) as i:
            for h in range(2):
                pe.wait_ge(c_in[h], 16 * i + 16)
                pe.wait_ge(k_ready, before(i, h))
                pe.wait_ge(v_ready, before(i, h))
                for c in range(DC):
                    pe.matmul(k_ps[h][:, :], lhsT=ct[h][:, c, :], rhs=W[:, c, 0:D], start=(c == 0), stop=(c == DC - 1))
                for c in range(DC):
                    last = pe.matmul(v_ps[h][:, :], lhsT=ct[h][:, c, :], rhs=W[:, c, D:2 * D], start=(c == 0), stop=(c == DC - 1))
                last.then_inc(kv_ready, 1)
            for h in range(2):
                pe.wait_ge(k_ready, here(i, h))
                pe.wait_ge(v_ready, here(i, h))
            pe.wait_ge(KV_ready, before(i, 1))
            for g in range(DC):
                for h in range(2):
                    last = pe.matmul(s_ps[g // 2][:, g % 2, :, :], lhsT=k[h][:, g * P:(g + 1) * P], rhs=v[h][:, g, :, :],
                                     start=(h == 0), stop=(h == 1))
                if g % 2:
                    last.then_inc(s_ready, 1)

    @block.scalar
    def _(act):
        with act.Fori(0, B) as i:
            for h in range(2):
                act.wait_ge(kv_ready, here(i, h))
                act.wait_ge(k_ready, before(i, h))
                act.activation(e[h][:, :], k_ps[h][:, :], ACT.Relu, scale=-1.0).then_inc(r_ready, 1)
                act.wait_ge(s_ready, before(i, 1))
                act.activation(v[h][:, :, 0, :], v_ps[h][:, :].rearrange("p (g e) -> p g e", g=DC), ACT.Copy).then_inc(v_ready, 1)
                act.wait_ge(r_ready, here(i, h))
                act.activation(e[h][:, :], e[h][:, :], ACT.Exp, scale=-1.0).then_inc(e_ready, 1)

    @block.vector
    def _(dve):
        dve.wait_ge(masked, 3)
        with dve.Fori(0, B) as i:
            for h in range(2):
                dve.wait_ge(e_ready, here(i, h))
                dve.wait_ge(s_ready, before(i, 1))
                dve.scalar_tensor_tensor(k[h][:, :], k_ps[h][:, :], 0.0, e[h][:, :], ALU.max, ALU.add).then_inc(k_ready, 1)
            for g in range(2):
                dve.wait_ge(s_ready, here(i, g))
                dve.tensor_tensor(KV[:, bass.ds(4 * i + 2 * g, 2), :].rearrange("p a (b n) -> p (a b) n", b=2),
                                  s_ps[g][:, :, :, :].rearrange("p a b n -> p (a b) n"),
                                  mask[:, :, :].rearrange("p a b -> p (a b)").unsqueeze(1).to_broadcast([P, 4, P]),
                                  ALU.mult).then_inc(KV_ready, 1)

    ph.end()


def linear_attention_phase(nc, R, A, KV, gate):
    ph = Phase(nc, "L1x")
    X, ident, tg, stats = R["X"], R["ident"], R["tg"], R["stats"]
    NP = B // 2
    EPS = 1e-6
    Wq, Wg, Wo = (ph.sb(n, [P, DC, D]) for n in ("Wq", "Wg", "Wo"))
    bg, eps = ph.sb("bg", [P, DC]), ph.sb("eps", [P, 1])
    m, var, rstd, root, w1, w2 = (ph.sb(n, [P, NT]) for n in ("m", "var", "rstd", "root", "w1", "w2"))

    def two(n, shape, dt=F32):
        return [ph.sb(f"{n}{h}", shape, dt) for h in range(2)]

    xn, xT, kv = two("xn", [P, TB, D]), two("xT", [P, DC, T]), two("kv", [P, DC, 2, P])
    e, q, sg, dn, ag = two("e", [P, DC, T]), two("q", [P, DC, T]), two("sg", [P, DC, T]), two("dn", [P, DC, T]), two("ag", [P, DC, T])
    t_ps = [ph.ps(f"t_ps{j}", [P, DC, P]) for j in range(TB)]
    q_ps, g_ps, n_ps = (ph.ps(n, [P, DC, T]) for n in ("q_ps", "g_ps", "n_ps"))
    w_in, step, asked, rooted = ph.sem("w_in"), ph.sem("step"), ph.sem("asked"), ph.sem("rooted")
    xn_ready, x_turned, xT_ready, kv_ready = (ph.pair_sem(n) for n in ("xn", "x_turned", "xT", "kv"))
    qp_ready, gp_ready, r_ready, e_ready, q_ready, sg_ready = (ph.pair_sem(n) for n in ("qp", "gp", "r", "e", "q", "sg"))
    nd_ready, dn_ready, ng_ready, rd_ready, ag_ready = (ph.pair_sem(n) for n in ("nd", "dn", "ng", "rd", "ag"))
    o_ready, x_ready, st_ready = (ph.pair_sem(n) for n in ("o", "x", "st"))
    block = ph.start()

    @block.sync
    def _(sp):
        for w, n in ((Wq, "L1_xattn_WqT"), (Wg, "L1_xattn_WgT"), (Wo, "L1_xattn_WoT")):
            sp.dma_start(w[:, :, :], A[n].rearrange("(c p) n -> p c n", p=P)).then_inc(w_in, 16)
        sp.dma_start(bg[:, :], A["L1_xattn_bg"].rearrange("(c p) -> p c", p=P), allow_slow_non_contiguous=True).then_inc(w_in, 16)

    @block.gpsimd
    def _(pool):
        with pool.Fori(0, NP) as i:
            for h in range(2):
                pool.wait_ge(nd_ready, before(i, h))
                pool.tensor_copy(kv[h][:, :, :, :].rearrange("p g a n -> p g (a n)"),
                                 KV[:, bass.ds((2 * i + h) * DC, DC), :]).then_inc(kv_ready, 1)

    @block.tensor
    def _(pe):
        def turn(i, h):
            pe.wait_ge(xn_ready, here(i, h))
            for j in range(TB):
                for c in range(DC):
                    last = pe.transpose(t_ps[j][:, c, :], xn[h][:, j, c * P:(c + 1) * P], ident[:, :])
            last.then_inc(x_turned, 1)

        def project(i, h):
            pe.wait_ge(xT_ready, here(i, h))
            pe.wait_ge(dn_ready, here(i, h) - 1)
            for o in range(DC):
                for c in range(DC):
                    last = pe.matmul(q_ps[:, o, :], lhsT=Wq[:, c, o * P:(o + 1) * P], rhs=xT[h][:, c, :],
                                     start=(c == 0), stop=(c == DC - 1))
            last.then_inc(qp_ready, 1)
            pe.wait_ge(sg_ready, here(i, h) - 1)
            for o in range(DC):
                for c in range(DC):
                    last = pe.matmul(g_ps[:, o, :], lhsT=Wg[:, c, o * P:(o + 1) * P], rhs=xT[h][:, c, :],
                                     start=(c == 0), stop=(c == DC - 1))
            last.then_inc(gp_ready, 1)

        def attend(i, h):
            pe.wait_ge(q_ready, here(i, h))
            pe.wait_ge(kv_ready, here(i, h))
            pe.wait_ge(ng_ready, here(i, h) - 1)
            for g in range(DC):
                pe.matmul(q_ps[:, g, :], lhsT=kv[h][:, g, 1, :], rhs=q[h][:, g, :], start=True, stop=True)
            for g in range(DC):
                last = pe.matmul(n_ps[:, g, :], lhsT=kv[h][:, g, 0, :], rhs=q[h][:, g, :], start=True, stop=True)
            last.then_inc(nd_ready, 1)

        def out(i, h):
            pe.wait_ge(ag_ready, here(i, h))
            for j in range(TB):
                for c in range(DC):
                    last = pe.matmul(t_ps[j][:, :, :], lhsT=ag[h][:, c, j * P:(j + 1) * P], rhs=Wo[:, c, :],
                                     start=(c == 0), stop=(c == DC - 1))
            last.then_inc(o_ready, 1)

        def unit(now, prev, nxt):
            project(*now)
            if prev:
                pe.wait_ge(xT_ready, here(*now))
                out(*prev)
            if nxt:
                if prev:
                    pe.wait_ge(x_ready, here(*prev))
                turn(*nxt)
            attend(*now)

        pe.wait_ge(w_in, 64)
        turn(0, 0)
        unit((0, 0), None, (0, 1))
        with pe.Fori(0, NP - 1) as i:
            unit((i, 1), (i, 0), (i + 1, 0))
            unit((i + 1, 0), (i, 1), (i + 1, 1))
        unit((NP - 1, 1), (NP - 1, 0), None)
        out(NP - 1, 1)

    @block.scalar
    def _(act):
        def turned(i, h):
            act.wait_ge(x_turned, here(i, h))
            act.wait_ge(gp_ready, before(i, h))
            for j in range(TB):
                last = act.activation(xT[h][:, :, j * P:(j + 1) * P], t_ps[j][:, :, :], ACT.Copy)
            last.then_inc(xT_ready, 1)

        def unit(now, nxt):
            i, h = now
            act.wait_ge(qp_ready, here(i, h))
            act.wait_ge(q_ready, before(i, h))
            act.activation(e[h][:, :, :], q_ps[:, :, :], ACT.Relu, scale=-1.0).then_inc(r_ready, 1)
            act.wait_ge(r_ready, here(i, h))
            act.activation(e[h][:, :, :], e[h][:, :, :], ACT.Exp, scale=-1.0).then_inc(e_ready, 1)
            act.wait_ge(gp_ready, here(i, h))
            act.wait_ge(ng_ready, before(i, h))
            for c in range(DC):
                last = act.activation(sg[h][:, c, :], g_ps[:, c, :], ACT.Sigmoid, bias=bg[:, c:c + 1])
            last.then_inc(sg_ready, 1)
            if nxt:
                turned(*nxt)
            act.wait_ge(nd_ready, here(i, h))
            act.wait_ge(ag_ready, before(i, h))
            act.activation(dn[h][:, :, :], q_ps[:, :, :], ACT.Identity, bias=eps[:, 0:1]).then_inc(dn_ready, 1)

        act.wait_ge(asked, 1)
        act.activation(root[:, :], var[:, :], ACT.Sqrt).then_inc(rooted, 1)
        act.wait_ge(w_in, 64)
        act.wait_ge(step, 1)
        turned(0, 0)
        unit((0, 0), (0, 1))
        with act.Fori(0, NP - 1) as i:
            unit((i, 1), (i + 1, 0))
            unit((i + 1, 0), (i + 1, 1))
        unit((NP - 1, 1), None)

    @block.vector
    def _(dve):
        dve.memset(eps[:, :], EPS).then_inc(step, 1)
        n = row_stats(dve, stats, m[:, :], var[:, :], w1[:, :], w2[:, :], step, 1)
        dve.wait_ge(step, n)
        dve.tensor_scalar(var[:, :], var[:, :], LN_EPS, None, ALU.add).then_inc(step, 1)
        n = rsqrt(dve, asked, rooted, 1, rstd[:, :], var[:, :], root[:, :], w1[:, :], step, n + 1)
        dve.wait_ge(step, n)

        def normalise(i, h):
            dve.wait_ge(x_turned, before(i, h))
            for j in range(TB):
                t = (2 * i + h) * TB + j
                last = dve.tensor_scalar(xn[h][:, j, :], X[:, t, :], m[:, bass.ds(t, 1)], rstd[:, bass.ds(t, 1)],
                                         ALU.subtract, ALU.mult)
            last.then_inc(xn_ready, 1)

        def out(i, h):
            dve.wait_ge(o_ready, here(i, h))
            for j in range(TB):
                t = (2 * i + h) * TB + j
                last = dve.scalar_tensor_tensor(X[:, t, :], t_ps[j][:, :, :].rearrange("p c n -> p (c n)"),
                                                tg[:, gate:gate + 1], X[:, t, :], ALU.mult, ALU.add)
            last.then_inc(x_ready, 1)
            dve.wait_ge(x_ready, here(i, h))
            for j in range(TB):
                t = (2 * i + h) * TB + j
                last = dve.bn_stats(stats[:, t, :], X[:, t, :])
            last.then_inc(st_ready, 1)

        def unit(now, prev, nxt):
            i, h = now
            if nxt:
                normalise(*nxt)
            dve.wait_ge(e_ready, here(i, h))
            dve.wait_ge(nd_ready, before(i, h))
            dve.scalar_tensor_tensor(q[h][:, :, :], q_ps[:, :, :], 0.0, e[h][:, :, :], ALU.max, ALU.add).then_inc(q_ready, 1)
            if prev:
                out(*prev)
            dve.wait_ge(nd_ready, here(i, h))
            dve.wait_ge(sg_ready, here(i, h))
            dve.wait_ge(o_ready, before(i, h))
            dve.tensor_tensor(ag[h][:, :, :], n_ps[:, :, :], sg[h][:, :, :], ALU.mult).then_inc(ng_ready, 1)
            dve.wait_ge(dn_ready, here(i, h))
            dve.reciprocal(dn[h][:, :, :], dn[h][:, :, :]).then_inc(rd_ready, 1)
            dve.wait_ge(rd_ready, here(i, h))
            dve.tensor_tensor(ag[h][:, :, :], ag[h][:, :, :], dn[h][:, :, :], ALU.mult).then_inc(ag_ready, 1)

        normalise(0, 0)
        unit((0, 0), None, (0, 1))
        with dve.Fori(0, NP - 1) as i:
            unit((i, 1), (i, 0), (i + 1, 0))
            unit((i + 1, 0), (i, 1), (i + 1, 1))
        unit((NP - 1, 1), (NP - 1, 0), None)
        out(NP - 1, 1)

    ph.end()


def linker(eng, sem, at=0):
    count = [at]

    def link(ins):
        count[0] += 1
        ins.then_inc(sem, 1)
        eng.wait_ge(sem, count[0])
        return count[0]

    return link


def spline_phase(nc, R, A, gate):
    ph = Phase(nc, "L1f")
    X, ident, ones, tg, stats = R["X"], R["ident"], R["ones"], R["tg"], R["stats"]
    NTL, NCL, SL, GR = 64, 8, 8, 16
    NP = NT // 2
    BIG = 1e30
    TW = 2 * SL * GR + 3
    m, var, v0, r1, r2, root, w1, w2 = (ph.sb(n, [P, NT]) for n in ("m", "var", "v0", "r1", "r2", "root", "w1", "w2"))
    keep, shift = ph.sb("keep", [P, NT]), ph.sb("shift", [P, NT])
    gamma, beta, srow = ph.sb("gamma", [P, D]), ph.sb("beta", [P, D]), ph.sb("srow", [P, D])
    slopes, ss, sb_ = ph.sb("slopes", [P, DC, GR]), ph.sb("ss", [P, 3, DC]), ph.sb("sb", [P, DC, P])
    XF = ph.sb("XF", [P, NT, D])
    sg = [ph.sb(f"sg{h}", [P, D]) for h in range(2)]
    TS, OH, W1 = ph.sb("TS", [P, NT, NTL]), ph.sb("OH", [P, NT, NTL]), ph.sb("W1", [P, NT, NTL])
    CS, KM = ph.sb("CS", [P, NT, NCL]), ph.sb("KM", [P, NT])
    cio, tio, kio = ph.sb("cio", [P, NCL]), ph.sb("tio", [P, NCL, SL]), ph.sb("kio", [P, GR])
    XS, XM, MM = ph.sb("XS", [P, NT, SL]), ph.sb("XM", [P, 2, NT]), ph.sb("MM", [P, 2, NTL])
    TAB, OHT, LUT = ph.sb("TAB", [NTL, TW]), ph.sb("OHT", [NTL, NT, P]), ph.sb("LUT", [P, NT, TW])
    U, GI, Z, DL = (ph.sb(n, [P, NT, SL]) for n in ("U", "GI", "Z", "DL"))
    RG = ph.sb("RG", [P, NT])
    KN, KW = ph.sb("KN", [P, NT * SL, GR]), ph.sb("KW", [P, NT, SL * GR])
    s_ps, mm_ps = ph.ps("s_ps", [P, D]), ph.ps("mm_ps", [NTL, 2, P])
    oh_ps = [ph.ps(f"oh_ps{h}", [NTL, P]) for h in range(2)]
    l_ps = [ph.ps(f"l_ps{h}", [P, TW]) for h in range(2)]
    row_in, sl_in, tab_in, io_made = ph.sem("row_in"), ph.sem("sl_in"), ph.sem("tab_in"), ph.sem("io_made")
    step, chain, asked, rooted = ph.sem("step"), ph.sem("chain"), ph.sem("asked"), ph.sem("rooted")
    sgn_made, s_spread = ph.sem("sgn_made"), ph.sem("s_spread")
    xf_ready, xg_ready, xb_ready, sg_ready, sp_ready, ts_ready, gone = (ph.pair_sem(n) for n in ("xf", "xg", "xb", "sg", "sp", "ts", "gone"))
    xm_ready, xs_ready = ph.pair_sem("xm"), ph.pair_sem("xs")
    oh_made, oh_turned, oht_ready = ph.sem("oh_made"), ph.pair_sem("oh_turned"), ph.pair_sem("oht")
    mm_made, mm_turned, tab_ready = ph.sem("mm_made"), ph.sem("mm_turned"), ph.sem("tab_ready")
    l_ready, lut_ready, dl_made = ph.pair_sem("l"), ph.pair_sem("lut"), ph.sem("dl_made")
    put_ready, x_ready, st_ready = ph.pair_sem("put"), ph.pair_sem("x"), ph.pair_sem("st")
    block = ph.start()

    @block.sync
    def _(sp):
        sp.dma_start(slopes[:, :, :], A["L1_ffn_spline_slopes"].rearrange("a b g -> (a b) g").rearrange("(c p) g -> p c g", p=P)).then_inc(sl_in, 16)
        sp.dma_start(gamma[:, :], A["L1_ffn_ln_gamma"].partition_broadcast(P)).then_inc(row_in, 16)
        sp.dma_start(beta[:, :], A["L1_ffn_ln_beta"].partition_broadcast(P)).then_inc(row_in, 16)
        sp.dma_start(TAB[:, 0:SL * GR], A["L1_ffn_spline_bases"].rearrange("a b g -> a (b g)")).then_inc(tab_in, 16)
        sp.dma_start(TAB[:, SL * GR:2 * SL * GR], A["L1_ffn_spline_slopes"].rearrange("a b g -> a (b g)")).then_inc(tab_in, 16)
        sp.dma_start(TAB[:, TW - 1:TW], A["L1_ffn_output_scale"].unsqueeze(1)).then_inc(tab_in, 16)

    @block.gpsimd
    def _(pool):
        pool.iota(cio[:, :], pattern=[[-1, NCL]], base=0, channel_multiplier=0, allow_small_or_imprecise_dtypes=True).then_inc(io_made, 1)
        pool.iota(tio[:, :, :], pattern=[[0, NCL], [-1, SL]], base=0, channel_multiplier=0, allow_small_or_imprecise_dtypes=True).then_inc(io_made, 1)
        pool.iota(kio[:, :], pattern=[[1, GR]], base=0, channel_multiplier=0, allow_small_or_imprecise_dtypes=True).then_inc(io_made, 1)
        pool.wait_ge(dl_made, 1)
        with pool.Fori(0, NP) as i:
            for h in range(2):
                pool.wait_ge(x_ready, before(i, h))
                pool.tensor_tensor(sg[h][:, :].rearrange("p (a b) -> p a b", b=SL),
                                   OH[:, bass.ds(2 * i + h, 1), :].rearrange("p a b -> p (a b)").unsqueeze(2).to_broadcast([P, NTL, SL]),
                                   DL[:, bass.ds(2 * i + h, 1), :].to_broadcast([P, NTL, SL]), ALU.mult).then_inc(put_ready, 1)

    @block.tensor
    def _(pe):
        pe.wait_ge(sgn_made, DC)
        for c in range(DC):
            last = pe.matmul(s_ps[:, c * P:(c + 1) * P], lhsT=sb_[:, c, :], rhs=ident[:, :], start=True, stop=True)
        last.then_inc(s_spread, 1)
        pe.wait_ge(oh_made, 1)
        for t in range(NT):
            i, h = t // 2, t % 2
            pe.wait_ge(oht_ready, before(i, h))
            pe.transpose(oh_ps[h][:, :], OH[:, t, :], ident[:, :]).then_inc(oh_turned, 1)
        pe.wait_ge(mm_made, 1)
        for k in range(2):
            last = pe.transpose(mm_ps[:, k, :], MM[:, k, :], ident[:, :])
        last.then_inc(mm_turned, 1)
        pe.wait_ge(tab_ready, 1)
        for t in range(NT):
            i, h = t // 2, t % 2
            pe.wait_ge(oht_ready, here(i, h))
            pe.wait_ge(lut_ready, before(i, h))
            pe.matmul(l_ps[h][:, :], lhsT=OHT[:, t, :], rhs=TAB[:, :], start=True, stop=True).then_inc(l_ready, 1)

    @block.scalar
    def _(act):
        for n in range(2):
            act.wait_ge(asked, n + 1)
            act.activation(root[:, :], var[:, :], ACT.Sqrt).then_inc(rooted, 1)
        with act.Fori(0, NP) as i:
            for h in range(2):
                act.wait_ge(xb_ready, here(i, h))
                act.wait_ge(ts_ready, before(i, h))
                act.activation(sg[h][:, :], XF[:, 2 * i + h, :], ACT.Sign).then_inc(sg_ready, 1)
        with act.Fori(0, NP) as i:
            for h in range(2):
                act.wait_ge(oh_turned, here(i, h))
                act.activation(OHT[:, 2 * i + h, :], oh_ps[h][:, :], ACT.Copy).then_inc(oht_ready, 1)
        with act.Fori(0, NP) as i:
            for h in range(2):
                act.wait_ge(l_ready, here(i, h))
                act.activation(LUT[:, 2 * i + h, :], l_ps[h][:, :], ACT.Copy).then_inc(lut_ready, 1)

    @block.vector
    def _(dve):
        n = row_stats(dve, stats, m[:, :], v0[:, :], w1[:, :], w2[:, :], step, 0)
        dve.wait_ge(step, n)
        dve.tensor_scalar(var[:, :], v0[:, :], LN_EPS, None, ALU.add).then_inc(step, 1)
        n = rsqrt(dve, asked, rooted, 1, r1[:, :], var[:, :], root[:, :], w1[:, :], step, n + 1)
        dve.wait_ge(step, n)
        link = linker(dve, chain)
        link(dve.tensor_tensor(w2[:, :], v0[:, :], r1[:, :], ALU.mult))
        link(dve.tensor_tensor(w2[:, :], w2[:, :], r1[:, :], ALU.mult))
        link(dve.tensor_scalar(var[:, :], w2[:, :], LN_EPS, None, ALU.add))
        n = rsqrt(dve, asked, rooted, 2, r2[:, :], var[:, :], root[:, :], w1[:, :], step, n)
        dve.wait_ge(step, n)
        link(dve.tensor_tensor(r2[:, :], r2[:, :], r1[:, :], ALU.mult))
        link(dve.tensor_scalar(keep[:, :], r1[:, :], tg[:, gate:gate + 1], 1.0, ALU.mult, ALU.add))
        link(dve.tensor_tensor(shift[:, :], m[:, :], r1[:, :], ALU.mult))
        link(dve.tensor_scalar(shift[:, :], shift[:, :], tg[:, gate:gate + 1], -1.0, ALU.mult, ALU.mult))
        dve.wait_ge(sl_in, 16)
        link(dve.tensor_reduce(ss[:, 0, :], slopes[:, :, :], AX.X, ALU.add))
        link(dve.tensor_scalar(ss[:, 1, :], ss[:, 0, :], 0.0, None, ALU.is_gt))
        link(dve.tensor_scalar(ss[:, 2, :], ss[:, 0, :], 0.0, None, ALU.is_lt))
        link(dve.tensor_tensor(ss[:, 0, :], ss[:, 1, :], ss[:, 2, :], ALU.subtract))
        for c in range(DC):
            dve.tensor_scalar(sb_[:, c, :], ones[:, :], ss[:, 0, c:c + 1], None, ALU.mult).then_inc(sgn_made, 1)
        dve.wait_ge(s_spread, 1)
        link(dve.tensor_copy(srow[:, :], s_ps[:, :]))
        dve.wait_ge(row_in, 32)
        with dve.Fori(0, NP) as i:
            for h in range(2):
                t = 2 * i + h
                dve.tensor_scalar(XF[:, t, :], X[:, t, :], m[:, bass.ds(t, 1)], r2[:, bass.ds(t, 1)],
                                  ALU.subtract, ALU.mult).then_inc(xf_ready, 1)
            for h in range(2):
                t = 2 * i + h
                dve.wait_ge(xf_ready, here(i, h))
                dve.tensor_tensor(XF[:, t, :], XF[:, t, :], gamma[:, :], ALU.mult).then_inc(xg_ready, 1)
            for h in range(2):
                t = 2 * i + h
                dve.wait_ge(xg_ready, here(i, h))
                dve.tensor_tensor(XF[:, t, :], XF[:, t, :], beta[:, :], ALU.add).then_inc(xb_ready, 1)
            for h in range(2):
                t = 2 * i + h
                dve.tensor_scalar(X[:, t, :], X[:, t, :], keep[:, bass.ds(t, 1)], shift[:, bass.ds(t, 1)],
                                  ALU.mult, ALU.add).then_inc(gone, 1)
            for h in range(2):
                dve.wait_ge(sg_ready, here(i, h))
                dve.tensor_tensor(sg[h][:, :], sg[h][:, :], srow[:, :], ALU.mult).then_inc(sp_ready, 1)
            for h in range(2):
                t = 2 * i + h
                dve.wait_ge(sp_ready, here(i, h))
                dve.tensor_reduce(TS[:, t, :], sg[h][:, :].rearrange("p (a b) -> p a b", b=SL), AX.X, ALU.add).then_inc(ts_ready, 1)
        dve.wait_ge(ts_ready, 2 * NP + 2)
        dve.wait_ge(io_made, 3)
        link(dve.tensor_reduce(CS[:, :, :], TS[:, :, :].rearrange("p t (c a) -> p (t c) a", a=SL), AX.X, ALU.add))
        link(dve.scalar_tensor_tensor(CS[:, :, :], CS[:, :, :], 8.0, cio[:, :].unsqueeze(1).to_broadcast([P, NT, NCL]), ALU.mult, ALU.add))
        link(dve.scalar_tensor_tensor(TS[:, :, :], TS[:, :, :], 8.0,
                                      tio[:, :, :].rearrange("p a b -> p (a b)").unsqueeze(1).to_broadcast([P, NT, NTL]), ALU.mult, ALU.add))
        link(dve.scalar_tensor_tensor(TS[:, :, :].rearrange("p t (c a) -> p (t c) a", a=SL),
                                      CS[:, :, :].rearrange("p t c -> p (t c)").unsqueeze(2).to_broadcast([P, NT * NCL, SL]), 256.0,
                                      TS[:, :, :].rearrange("p t (c a) -> p (t c) a", a=SL), ALU.mult, ALU.add))
        link(dve.tensor_reduce(KM[:, :], TS[:, :, :], AX.X, ALU.max))
        dve.tensor_tensor(OH[:, :, :], TS[:, :, :], KM[:, :].unsqueeze(2).to_broadcast([P, NT, NTL]), ALU.is_equal).then_inc(oh_made, 1)
        dve.wait_ge(oh_made, 1)
        with dve.Fori(0, NP) as i:
            for h in range(2):
                t = 2 * i + h
                dve.wait_ge(xs_ready, before(i, h))
                dve.tensor_tensor(sg[h][:, :].rearrange("p (a b) -> p a b", b=SL),
                                  XF[:, bass.ds(t, 1), :].rearrange("p t (a b) -> p (t a) b", b=SL),
                                  OH[:, bass.ds(t, 1), :].rearrange("p a b -> p (a b)").unsqueeze(2).to_broadcast([P, NTL, SL]),
                                  ALU.mult).then_inc(xm_ready, 1)
            for h in range(2):
                dve.wait_ge(xm_ready, here(i, h))
                dve.tensor_reduce(XS[:, 2 * i + h, :], sg[h][:, :].rearrange("p (a b) -> p b a", b=SL), AX.X, ALU.add).then_inc(xs_ready, 1)
        dve.wait_ge(xs_ready, 2 * NP + 2)
        link(dve.tensor_reduce(XM[:, 0, :], XS[:, :, :], AX.X, ALU.max))
        link(dve.tensor_reduce(XM[:, 1, :], XS[:, :, :], AX.X, ALU.min, negate=True))
        link(dve.tensor_scalar(W1[:, :, :], OH[:, :, :], -1.0, BIG, ALU.add, ALU.mult))
        for k in range(2):
            link(dve.tensor_tensor(TS[:, :, :], OH[:, :, :], XM[:, k, :].unsqueeze(2).to_broadcast([P, NT, NTL]), ALU.mult))
            link(dve.tensor_tensor(TS[:, :, :], TS[:, :, :], W1[:, :, :], ALU.add))
            link(dve.tensor_reduce(MM[:, k, :], TS[:, :, :].rearrange("p t a -> p a t"), AX.X, ALU.max))
        dve.sem_inc(mm_made, 1)
        dve.wait_ge(mm_turned, 1)
        dve.wait_ge(tab_in, 48)
        dve.tensor_reduce(TAB[:, TW - 3:TW - 1], mm_ps[:, :, :], AX.X, ALU.max).then_inc(tab_ready, 1)
        dve.wait_ge(lut_ready, 2 * NP + 2)
        link(dve.tensor_tensor(RG[:, :], LUT[:, :, TW - 3], LUT[:, :, TW - 2], ALU.add))
        link(dve.tensor_scalar(RG[:, :], RG[:, :], 1e-8, None, ALU.add))
        link(dve.reciprocal(RG[:, :], RG[:, :]))
        link(dve.tensor_tensor(U[:, :, :], XS[:, :, :], LUT[:, :, TW - 2:TW - 1].to_broadcast([P, NT, SL]), ALU.add))
        link(dve.tensor_tensor(U[:, :, :], U[:, :, :], RG[:, :].unsqueeze(2).to_broadcast([P, NT, SL]), ALU.mult))
        link(dve.tensor_scalar(U[:, :, :], U[:, :, :], 0.0, 1.0 - 1e-6, ALU.max, ALU.min))
        link(dve.tensor_scalar(U[:, :, :], U[:, :, :], float(GR), None, ALU.mult))
        link(dve.tensor_scalar(GI[:, :, :], U[:, :, :], MAGIC, -MAGIC, ALU.add, ALU.add))
        link(dve.tensor_tensor(Z[:, :, :], GI[:, :, :], U[:, :, :], ALU.is_gt))
        link(dve.tensor_tensor(GI[:, :, :], GI[:, :, :], Z[:, :, :], ALU.subtract))
        link(dve.tensor_tensor(U[:, :, :], U[:, :, :], GI[:, :, :], ALU.subtract))
        link(dve.tensor_tensor(KN[:, :, :], kio[:, :].unsqueeze(1).to_broadcast([P, NT * SL, GR]),
                               GI[:, :, :].rearrange("p t j -> p (t j)").unsqueeze(2).to_broadcast([P, NT * SL, GR]), ALU.is_equal))
        for k, dst in ((0, Z), (1, DL)):
            link(dve.tensor_tensor(KW[:, :, :], KN[:, :, :].rearrange("p (t j) g -> p t (j g)", j=SL),
                                   LUT[:, :, k * SL * GR:(k + 1) * SL * GR], ALU.mult))
            link(dve.tensor_reduce(dst[:, :, :].rearrange("p t j -> p (t j)"),
                                   KW[:, :, :].rearrange("p t (j g) -> p (t j) g", g=GR), AX.X, ALU.add))
        link(dve.tensor_tensor(DL[:, :, :], DL[:, :, :], U[:, :, :], ALU.mult))
        link(dve.tensor_tensor(DL[:, :, :], DL[:, :, :], Z[:, :, :], ALU.add))
        link(dve.tensor_tensor(DL[:, :, :], DL[:, :, :], LUT[:, :, TW - 1:TW].to_broadcast([P, NT, SL]), ALU.mult))
        dve.tensor_scalar(DL[:, :, :], DL[:, :, :], tg[:, gate:gate + 1], None, ALU.mult).then_inc(dl_made, 1)
        with dve.Fori(0, NP) as i:
            for h in range(2):
                t = 2 * i + h
                dve.wait_ge(put_ready, here(i, h))
                dve.tensor_tensor(X[:, t, :], X[:, t, :], sg[h][:, :], ALU.add).then_inc(x_ready, 1)
            for h in range(2):
                t = 2 * i + h
                dve.wait_ge(x_ready, here(i, h))
                dve.bn_stats(stats[:, t, :], X[:, t, :]).then_inc(st_ready, 1)

    ph.end()


def experts_phase(nc, R, A, gate):
    ph = Phase(nc, "L2f")
    X, ident, tg, stats = R["X"], R["ident"], R["tg"], R["stats"]
    E, I = 8, 16
    EI = E * I
    NP = NT // 2
    m, var, rstd, root, w1, w2 = (ph.sb(n, [P, NT]) for n in ("m", "var", "rstd", "root", "w1", "w2"))
    W, up = ph.sb("W", [P, DC, EI + E]), ph.sb("up", [P, D])
    H, LG = ph.sb("H", [P, NT, EI]), ph.sb("LG", [P, NT, E])
    MX, WT, FI, K1, MK, RM = ph.sb("MX", [P, NT]), ph.sb("WT", [P, NT, E]), ph.sb("FI", [P, E]), ph.sb("K1", [P, NT, E]), ph.sb("MK", [P, NT, E]), ph.sb("RM", [P, NT, E])

    def two(n, shape):
        return [ph.sb(f"{n}{h}", shape) for h in range(2)]

    xn, xT, a, aT = two("xn", [P, D]), two("xT", [P, DC, P]), two("a", [P, EI]), two("aT", [P, P])
    t_ps = [ph.ps(f"t_ps{h}", [P, DC, P]) for h in range(2)]
    h_ps = [ph.ps(f"h_ps{h}", [P, EI + E]) for h in range(2)]
    a_ps = [ph.ps(f"a_ps{h}", [P, P]) for h in range(2)]
    o_ps = [ph.ps(f"o_ps{h}", [P, D]) for h in range(2)]
    w_in, step, chain, asked, rooted, iota_made = (ph.sem(n) for n in ("w_in", "step", "chain", "asked", "rooted", "iota"))
    xn_ready, turned, xT_ready, h_ready, H_ready, LG_ready = (ph.pair_sem(n) for n in ("xn", "turned", "xT", "h", "H", "LG"))
    ex_asked, ex_ready = ph.sem("ex_asked"), ph.sem("ex")
    a_ready, a_turned, aT_ready, o_ready, x_ready, st_ready = (ph.pair_sem(n) for n in ("a", "a_turned", "aT", "o", "x", "st"))
    block = ph.start()

    @block.sync
    def _(sp):
        sp.dma_start(W[:, :, 0:EI], A["L2_ffn_downT"].rearrange("(c p) n -> p c n", p=P)).then_inc(w_in, 16)
        sp.dma_start(W[:, :, EI:EI + E], A["L2_ffn_routerT"].rearrange("(c p) n -> p c n", p=P)).then_inc(w_in, 16)
        sp.dma_start(up[:, :], A["L2_ffn_up"]).then_inc(w_in, 16)

    @block.gpsimd
    def _(pool):
        pool.iota(FI[:, :], pattern=[[-1, E]], base=E, channel_multiplier=0, allow_small_or_imprecise_dtypes=True).then_inc(iota_made, 1)

    @block.tensor
    def _(pe):
        pe.wait_ge(w_in, 48)
        with pe.Fori(0, NP) as i:
            for h in range(2):
                pe.wait_ge(xn_ready, here(i, h))
                pe.wait_ge(xT_ready, before(i, h))
                for c in range(DC):
                    last = pe.transpose(t_ps[h][:, c, :], xn[h][:, c * P:(c + 1) * P], ident[:, :])
                last.then_inc(turned, 1)
            for h in range(2):
                pe.wait_ge(xT_ready, here(i, h))
                pe.wait_ge(H_ready, before(i, h))
                pe.wait_ge(LG_ready, before(i, h))
                for c in range(DC):
                    last = pe.matmul(h_ps[h][:, :], lhsT=xT[h][:, c, :], rhs=W[:, c, :], start=(c == 0), stop=(c == DC - 1))
                last.then_inc(h_ready, 1)
        with pe.Fori(0, NP) as i:
            for h in range(2):
                pe.wait_ge(a_ready, here(i, h))
                pe.wait_ge(aT_ready, before(i, h))
                pe.transpose(a_ps[h][:, :], a[h][:, :], ident[:, :]).then_inc(a_turned, 1)
            for h in range(2):
                pe.wait_ge(aT_ready, here(i, h))
                pe.wait_ge(x_ready, before(i, h))
                pe.matmul(o_ps[h][:, :], lhsT=aT[h][:, :], rhs=up[:, :], start=True, stop=True).then_inc(o_ready, 1)

    @block.scalar
    def _(act):
        act.wait_ge(asked, 1)
        act.activation(root[:, :], var[:, :], ACT.Sqrt).then_inc(rooted, 1)
        with act.Fori(0, NP) as i:
            for h in range(2):
                act.wait_ge(turned, here(i, h))
                act.wait_ge(h_ready, before(i, h))
                act.activation(xT[h][:, :, :], t_ps[h][:, :, :], ACT.Copy).then_inc(xT_ready, 1)
            for h in range(2):
                act.wait_ge(h_ready, here(i, h))
                act.activation(H[:, 2 * i + h, :], h_ps[h][:, 0:EI], ACT.Silu).then_inc(H_ready, 1)
                act.activation(LG[:, 2 * i + h, :], h_ps[h][:, EI:EI + E], ACT.Copy).then_inc(LG_ready, 1)
        act.wait_ge(ex_asked, 1)
        act.activation(LG[:, :, :], LG[:, :, :], ACT.Exp).then_inc(ex_ready, 1)
        with act.Fori(0, NP) as i:
            for h in range(2):
                act.wait_ge(a_turned, here(i, h))
                act.wait_ge(o_ready, before(i, h))
                act.activation(aT[h][:, :], a_ps[h][:, :], ACT.Copy).then_inc(aT_ready, 1)

    @block.vector
    def _(dve):
        n = row_stats(dve, stats, m[:, :], var[:, :], w1[:, :], w2[:, :], step, 0)
        dve.wait_ge(step, n)
        dve.tensor_scalar(var[:, :], var[:, :], LN_EPS, None, ALU.add).then_inc(step, 1)
        n = rsqrt(dve, asked, rooted, 1, rstd[:, :], var[:, :], root[:, :], w1[:, :], step, n + 1)
        dve.wait_ge(step, n)
        with dve.Fori(0, NP) as i:
            for h in range(2):
                t = 2 * i + h
                dve.wait_ge(turned, before(i, h))
                dve.tensor_scalar(xn[h][:, :], X[:, t, :], m[:, bass.ds(t, 1)], rstd[:, bass.ds(t, 1)],
                                  ALU.subtract, ALU.mult).then_inc(xn_ready, 1)
        dve.wait_ge(LG_ready, 2 * NP + 2)
        link = linker(dve, chain)
        link(dve.tensor_reduce(MX[:, :], LG[:, :, :], AX.X, ALU.max))
        dve.tensor_tensor(LG[:, :, :], LG[:, :, :], MX[:, :].unsqueeze(2).to_broadcast([P, NT, E]), ALU.subtract).then_inc(ex_asked, 1)
        dve.wait_ge(ex_ready, 1)
        link(dve.tensor_reduce(MX[:, :], LG[:, :, :], AX.X, ALU.add))
        link(dve.reciprocal(MX[:, :], MX[:, :]))
        link(dve.tensor_tensor(WT[:, :, :], LG[:, :, :], MX[:, :].unsqueeze(2).to_broadcast([P, NT, E]), ALU.mult))
        link(dve.tensor_copy(RM[:, :, :], WT[:, :, :]))
        dve.wait_ge(iota_made, 1)
        for k in range(2):
            link(dve.tensor_reduce(MX[:, :], RM[:, :, :], AX.X, ALU.max))
            link(dve.tensor_tensor(K1[:, :, :], RM[:, :, :], MX[:, :].unsqueeze(2).to_broadcast([P, NT, E]), ALU.is_equal))
            link(dve.tensor_tensor(K1[:, :, :], K1[:, :, :], FI[:, :].unsqueeze(1).to_broadcast([P, NT, E]), ALU.mult))
            link(dve.tensor_reduce(MX[:, :], K1[:, :, :], AX.X, ALU.max))
            link(dve.tensor_tensor(K1[:, :, :], K1[:, :, :], MX[:, :].unsqueeze(2).to_broadcast([P, NT, E]), ALU.is_equal))
            if k == 0:
                link(dve.tensor_copy(MK[:, :, :], K1[:, :, :]))
                link(dve.scalar_tensor_tensor(RM[:, :, :], K1[:, :, :], -2.0, RM[:, :, :], ALU.mult, ALU.add))
            else:
                link(dve.tensor_tensor(MK[:, :, :], MK[:, :, :], K1[:, :, :], ALU.add))
        link(dve.tensor_tensor(WT[:, :, :], WT[:, :, :], MK[:, :, :], ALU.mult))
        dve.wait_ge(H_ready, 2 * NP + 2)
        with dve.Fori(0, NP) as i:
            for h in range(2):
                t = 2 * i + h
                dve.wait_ge(a_turned, before(i, h))
                dve.tensor_tensor(a[h][:, :].rearrange("p (e k) -> p e k", k=I),
                                  H[:, bass.ds(t, 1), :].rearrange("p t (e k) -> p (t e) k", k=I),
                                  WT[:, bass.ds(t, 1), :].rearrange("p a b -> p (a b)").unsqueeze(2).to_broadcast([P, E, I]),
                                  ALU.mult).then_inc(a_ready, 1)
            for h in range(2):
                t = 2 * i + h
                dve.wait_ge(o_ready, here(i, h))
                dve.scalar_tensor_tensor(X[:, t, :], o_ps[h][:, :], tg[:, gate:gate + 1], X[:, t, :], ALU.mult, ALU.add).then_inc(x_ready, 1)
            for h in range(2):
                t = 2 * i + h
                dve.wait_ge(x_ready, here(i, h))
                dve.bn_stats(stats[:, t, :], X[:, t, :]).then_inc(st_ready, 1)

    ph.end()


def decay_phase(nc, R, A, gate, x_dram):
    ph = Phase(nc, "L3x")
    X, ident, ones, tg, stats = R["X"], R["ident"], R["ones"], R["tg"], R["stats"]
    NP = NT // 2
    m, var, rstd, root, w1, w2 = (ph.sb(n, [P, NT]) for n in ("m", "var", "rstd", "root", "w1", "w2"))
    C = ph.sb("C", [P, NT, D])
    Y = ph.sb("Y", [P, NT, D])
    st2 = ph.sb("st2", [P, NT, 6])
    Wi, Wo = ph.sb("Wi", [P, DC, D]), ph.sb("Wo", [P, DC, D])
    K, rr, rt, wc = ph.sb("K", [P, 2]), ph.sb("rr", [P, T]), ph.sb("rt", [P, T]), ph.sb("wc", [P, TB + 1])
    wsel, sel = ph.sb("wsel", [P, NT, B]), ph.sb("sel", [B, B, P])
    gamma, beta, bo, bi = ph.sb("gamma", [P, D]), ph.sb("beta", [P, D]), ph.sb("bo", [B, D]), ph.sb("bi", [P, DC])
    s8, sT, mT, pr, SB = ph.sb("s8", [B, D]), ph.sb("sT", [P, DC, B]), ph.sb("mT", [P, DC, B]), ph.sb("pr", [B, D]), ph.sb("SB", [P, B, D])
    z = [ph.sb(f"z{h}", [P, D]) for h in range(2)]
    s_ps, t_ps, m_ps, p_ps = ph.ps("s_ps", [B, D]), ph.ps("t_ps", [P, DC, B]), ph.ps("m_ps", [P, DC, B]), ph.ps("p_ps", [B, D])
    b_ps = [ph.ps(f"b_ps{h}", [P, D]) for h in range(2)]
    c_in, w_in, v_in, d_in = [ph.sem(f"c_in{k}") for k in range(2)], ph.sem("w_in"), ph.sem("v_in"), ph.sem("d_in")
    step, chain, asked, rooted, kept, sel_made, wsel_made = (ph.sem(n) for n in ("step", "chain", "asked", "rooted", "kept", "sel", "wsel"))
    summed, copied, turned, turned_back, mixed, mixed_back, proj, proj_back = (ph.sem(n) for n in ("summed", "copied", "turned", "turned_back", "mixed", "mixed_back", "proj", "proj_back"))
    spread, SB_ready = ph.pair_sem("spread"), ph.pair_sem("SB")
    y_ready, y_stat, z_ready, zg_ready, xb_ready, x_ready = (ph.pair_sem(n) for n in ("y", "y_stat", "z", "zg", "xb", "x"))
    stored = ph.sem("stored")
    row_made = ph.sem("row_made")
    block = ph.start()

    @block.sync
    def _(sp):
        sp.dma_start(K[:, 0:1], A["L3_xattn_decay"].partition_broadcast(P)).then_inc(d_in, 16)
        for k in range(2):
            sp.dma_start(C[:, k * NT // 2:(k + 1) * NT // 2, :],
                         A["ctx"].rearrange("(t p) c -> p t c", p=P)[:, k * NT // 2:(k + 1) * NT // 2, :]).then_inc(c_in[k], 16)
        for w, n in ((Wi, "L3_xattn_W_inT"), (Wo, "L3_xattn_W_outT")):
            sp.dma_start(w[:, :, :], A[n].rearrange("(c p) n -> p c n", p=P)).then_inc(w_in, 16)
        sp.dma_start(gamma[:, :], A["L3_xattn_gamma"].partition_broadcast(P)).then_inc(v_in, 16)
        sp.dma_start(beta[:, :], A["L3_xattn_beta"].partition_broadcast(P)).then_inc(v_in, 16)
        sp.dma_start(bo[:, :], A["L3_xattn_b_out"].partition_broadcast(B)).then_inc(v_in, 16)
        sp.dma_start(bi[:, :], A["L3_xattn_b_in"].rearrange("(c p) -> p c", p=P), allow_slow_non_contiguous=True).then_inc(v_in, 16)
        xd = x_dram.rearrange("(t p) c -> p t c", p=P)
        with sp.Fori(0, NP) as i:
            sp.wait_ge(x_ready, both(i))
            sp.dma_start(xd[:, bass.ds(2 * i, 2), :], X[:, bass.ds(2 * i, 2), :]).then_inc(stored, 16)
        sp.wait_ge(stored, 16 * NP)

    @block.gpsimd
    def _(pool):
        pool.memset(sel[:, :, :], 0.0).then_inc(sel_made, 1)
        pool.wait_ge(sel_made, 1)
        pool.affine_select(out=sel[:, :, :], in_=sel[:, :, :], compare_op=ALU.not_equal, fill=1.0, base=0,
                           pattern=[[-1, B], [0, P]], channel_multiplier=1).then_inc(sel_made, 1)
        pool.wait_ge(row_made, 2)
        with pool.Fori(0, NP) as i:
            for h in range(2):
                pool.wait_ge(y_ready, here(i, h))
                pool.tensor_tensor(X[:, 2 * i + h, :], X[:, 2 * i + h, :], beta[:, :], ALU.add).then_inc(xb_ready, 1)

    @block.tensor
    def _(pe):
        pe.wait_ge(wsel_made, 1)
        for t in range(NT):
            if t % (NT // 2) == 0:
                pe.wait_ge(c_in[t // (NT // 2)], 16)
            last = pe.matmul(s_ps[:, :], lhsT=wsel[:, t, :], rhs=C[:, t, :], start=(t == 0), stop=(t == NT - 1))
        last.then_inc(summed, 1)
        pe.wait_ge(copied, 1)
        for c in range(DC):
            last = pe.transpose(t_ps[:, c, :], s8[:, c * P:(c + 1) * P], ident[0:B, 0:B])
        last.then_inc(turned, 1)
        pe.wait_ge(turned_back, 1)
        pe.wait_ge(w_in, 32)
        for o in range(DC):
            for c in range(DC):
                last = pe.matmul(m_ps[:, o, :], lhsT=Wi[:, c, o * P:(o + 1) * P], rhs=sT[:, c, :], start=(c == 0), stop=(c == DC - 1))
        last.then_inc(mixed, 1)
        pe.wait_ge(mixed_back, 1)
        for c in range(DC):
            last = pe.matmul(p_ps[:, :], lhsT=mT[:, c, :], rhs=Wo[:, c, :], start=(c == 0), stop=(c == DC - 1))
        last.then_inc(proj, 1)
        pe.wait_ge(proj_back, 1)
        pe.wait_ge(sel_made, 2)
        for b in range(B):
            pe.wait_ge(SB_ready, before(b // 2, b % 2))
            pe.matmul(b_ps[b % 2][:, :], lhsT=sel[:, b, :], rhs=pr[:, :], start=True, stop=True).then_inc(spread, 1)

    @block.scalar
    def _(act):
        act.wait_ge(d_in, 16)
        act.activation(K[:, 1:2], K[:, 0:1], ACT.Sigmoid).then_inc(kept, 1)
        for n in range(2):
            act.wait_ge(asked, n + 1)
            act.activation(root[:, :], var[:, :], ACT.Sqrt).then_inc(rooted, 1)
            if n == 0:
                for b in range(B):
                    act.wait_ge(spread, here(b // 2, b % 2))
                    act.activation(SB[:, b, :], b_ps[b % 2][:, :], ACT.Copy).then_inc(SB_ready, 1)

    @block.vector
    def _(dve):
        link = linker(dve, chain)
        dve.wait_ge(kept, 1)
        link(dve.tensor_copy(rt[:, :], ones[:, 0:1].to_broadcast([P, T])))
        link(dve.tensor_tensor_scan(rr[:, :], K[:, 1:2].to_broadcast([P, T]), rt[:, :], 0.0, ALU.mult, ALU.add))
        link(dve.tensor_reduce(wc[:, TB:TB + 1], rr[:, :], AX.X, ALU.add))
        link(dve.tensor_copy(rt[:, :], rr[:, ::-1]))
        for j in range(TB):
            link(dve.tensor_tensor(rr[:, 0:P], rt[:, j * P:(j + 1) * P], ident[:, :], ALU.mult))
            link(dve.tensor_reduce(wc[:, j:j + 1], rr[:, 0:P], AX.X, ALU.add))
        link(dve.tensor_scalar(wc[:, :], wc[:, :], 1.0 / T, None, ALU.mult))
        link(dve.memset(wsel[:, :, :], 0.0))
        for b in range(B):
            last = dve.tensor_copy(wsel[:, TB * b:TB * (b + 1), b], wc[:, 0:TB])
        last.then_inc(wsel_made, 1)
        dve.wait_ge(v_in, 64)
        dve.tensor_scalar(gamma[:, :], gamma[:, :], tg[:, gate:gate + 1], None, ALU.mult).then_inc(row_made, 1)
        dve.tensor_scalar(beta[:, :], beta[:, :], tg[:, gate:gate + 1], None, ALU.mult).then_inc(row_made, 1)
        n = row_stats(dve, stats, m[:, :], var[:, :], w1[:, :], w2[:, :], step, 0)
        dve.wait_ge(step, n)
        dve.tensor_scalar(var[:, :], var[:, :], LN_EPS, None, ALU.add).then_inc(step, 1)
        n = rsqrt(dve, asked, rooted, 1, rstd[:, :], var[:, :], root[:, :], w1[:, :], step, n + 1)
        dve.wait_ge(step, n)
        dve.wait_ge(summed, 1)
        dve.tensor_copy(s8[:, :], s_ps[:, :]).then_inc(copied, 1)
        dve.wait_ge(turned, 1)
        dve.tensor_copy(sT[:, :, :], t_ps[:, :, :]).then_inc(turned_back, 1)
        dve.wait_ge(mixed, 1)
        link(dve.tensor_scalar(bi[:, :], bi[:, :], wc[:, TB:TB + 1], None, ALU.mult))
        dve.tensor_tensor(mT[:, :, :], m_ps[:, :, :], bi[:, :].unsqueeze(2).to_broadcast([P, DC, B]), ALU.add).then_inc(mixed_back, 1)
        dve.wait_ge(proj, 1)
        dve.tensor_tensor(pr[:, :], p_ps[:, :], bo[:, :], ALU.add).then_inc(proj_back, 1)
        dve.wait_ge(SB_ready, B + 2)
        with dve.Fori(0, NP) as i:
            for h in range(2):
                t = 2 * i + h
                dve.scalar_tensor_tensor(Y[:, t, :], X[:, t, :], rstd[:, bass.ds(t, 1)], SB[:, i, :], ALU.mult, ALU.add).then_inc(y_ready, 1)
            for h in range(2):
                t = 2 * i + h
                dve.wait_ge(y_ready, here(i, h))
                dve.bn_stats(st2[:, t, :], Y[:, t, :]).then_inc(y_stat, 1)
        dve.wait_ge(y_stat, 2 * NP + 2)
        n = row_stats(dve, st2, m[:, :], var[:, :], w1[:, :], w2[:, :], step, n)
        dve.wait_ge(step, n)
        dve.tensor_scalar(var[:, :], var[:, :], LN_EPS, None, ALU.add).then_inc(step, 1)
        n = rsqrt(dve, asked, rooted, 2, rstd[:, :], var[:, :], root[:, :], w1[:, :], step, n + 1)
        dve.wait_ge(step, n)
        dve.wait_ge(row_made, 2)
        with dve.Fori(0, NP) as i:
            for h in range(2):
                t = 2 * i + h
                dve.wait_ge(x_ready, before(i, h))
                dve.tensor_scalar(z[h][:, :], Y[:, t, :], m[:, bass.ds(t, 1)], rstd[:, bass.ds(t, 1)],
                                  ALU.subtract, ALU.mult).then_inc(z_ready, 1)
            for h in range(2):
                dve.wait_ge(z_ready, here(i, h))
                dve.tensor_tensor(z[h][:, :], z[h][:, :], gamma[:, :], ALU.mult).then_inc(zg_ready, 1)
            for h in range(2):
                t = 2 * i + h
                dve.wait_ge(zg_ready, here(i, h))
                dve.wait_ge(xb_ready, here(i, h))
                dve.tensor_tensor(X[:, t, :], X[:, t, :], z[h][:, :], ALU.add).then_inc(x_ready, 1)

    ph.end()


def route_phase(nc, R, A, name, x_dram, xT, TR):
    ph = Phase(nc, name)
    ident, ones = R["ident"], R["ones"]
    NP = NT // 2
    HD, NK, KB = 4, 128, 8
    S = HD * KB
    E1 = A["L3_ffn_e_down"].shape[0]
    X8, stats = ph.sb("X8", [P, NT, D]), ph.sb("stats", [P, NT, 6])
    m, var, rstd, root, w1, w2 = (ph.sb(n, [P, NT]) for n in ("m", "var", "rstd", "root", "w1", "w2"))
    Wq, Kd = ph.sb("Wq", [P, DC, D]), ph.sb("Kd", [P, HD, 2 * NK])

    def two(n, shape, dt=F32):
        return [ph.sb(f"{n}{h}", shape, dt) for h in range(2)]

    xn, qT, sims = two("xn", [P, D]), two("qT", [P, HD, P]), two("sims", [P, 2 * HD, NK])
    best, at = two("best", [P, 2 * HD, KB]), two("at", [P, 2 * HD, KB], U32)
    sums, fin, pk = two("sums", [P, HD, KB, KB]), two("fin", [P, HD, KB]), two("pk", [P, HD, KB], U32)
    I, FW, PK = ph.sb("I", [P, 2, NT, S]), ph.sb("FW", [P, NT, S]), ph.sb("PK", [P, NT, S])
    PH = ph.sb("PH", [P, NT, S])
    kio, sec, M = ph.sb("kio", [P, KB]), ph.sb("sec", [P, 1]), ph.sb("M", [P, NT * S, KB])
    t_ps = [ph.ps(f"t_ps{h}", [P, DC, P]) for h in range(2)]
    q_ps = [ph.ps(f"q_ps{h}", [P, HD, P]) for h in range(2)]
    s_ps = [ph.ps(f"s_ps{h}", [P, 2 * HD, NK]) for h in range(2)]
    x_in, w_in, k_in, zeroed, io_made = [ph.sem(f"x_in{k}") for k in range(4)], ph.sem("w_in"), ph.sem("k_in"), ph.sem("zeroed"), ph.sem("io")
    step, chain, asked, rooted = ph.sem("step"), ph.sem("chain"), ph.sem("asked"), ph.sem("rooted")
    xn_ready, turned, xT_ready, q_ready, qT_ready, s_ready, sims_ready = (ph.pair_sem(n) for n in ("xn", "turned", "xT", "q", "qT", "s", "sims"))
    best_ready, at_ready, sums_ready, fin_ready, pk_ready, kept = (ph.pair_sem(n) for n in ("best", "at", "sums", "fin", "pk", "kept"))
    block = ph.start()

    @block.sync
    def _(sp):
        for q in range(4):
            for a in range(4):
                r = (q * 4 + a) * P
                sp.dma_start(X8[a * 32:(a + 1) * 32, q * 4:(q + 1) * 4, :],
                             x_dram[r:r + P, :].rearrange("(t g) c -> g t c", g=32)).then_inc(x_in[q], 16)
            if q == 0:
                sp.dma_start(Wq[:, :, :], A["L3_ffn_Wq"].rearrange("(c p) n -> p c n", p=P)).then_inc(w_in, 16)
                sp.wait_ge(zeroed, 1)
                for j in range(2):
                    sp.dma_start(Kd[j * 64:(j + 1) * 64, :, j * NK:(j + 1) * NK],
                                 A["L3_ffn_keys"][j].rearrange("d h k -> d h k")).then_inc(k_in, 16)

    @block.gpsimd
    def _(pool):
        pool.memset(Kd[:, :, :], 0.0).then_inc(zeroed, 1)
        pool.iota(kio[:, :], pattern=[[1, KB]], base=0, channel_multiplier=0, allow_small_or_imprecise_dtypes=True).then_inc(io_made, 1)

    @block.tensor
    def _(pe):
        pe.wait_ge(w_in, 16)
        pe.wait_ge(k_in, 32)
        with pe.Fori(0, NP) as i:
            for h in range(2):
                pe.wait_ge(xn_ready, here(i, h))
                pe.wait_ge(xT_ready, before(i, h))
                for c in range(DC):
                    last = pe.transpose(t_ps[h][:, c, :], xn[h][:, c * P:(c + 1) * P], ident[:, :])
                last.then_inc(turned, 1)
            for h in range(2):
                pe.wait_ge(xT_ready, here(i, h))
                pe.wait_ge(qT_ready, before(i, h))
                for n in range(HD):
                    for c in range(DC):
                        last = pe.matmul(q_ps[h][:, n, :], lhsT=Wq[:, c, n * P:(n + 1) * P], rhs=xT[:, c, :, bass.ds((2 * i + h) * 32, 32)],
                                         start=(c == 0), stop=(c == DC - 1))
                last.then_inc(q_ready, 1)
            for h in range(2):
                pe.wait_ge(qT_ready, here(i, h))
                pe.wait_ge(sims_ready, before(i, h))
                for n in range(HD):
                    last = pe.matmul(s_ps[h][:, 2 * n:2 * n + 2, :], lhsT=qT[h][:, n, :], rhs=Kd[:, n, :], start=True, stop=True)
                last.then_inc(s_ready, 1)

    @block.scalar
    def _(act):
        act.wait_ge(asked, 1)
        act.activation(root[:, :], var[:, :], ACT.Sqrt).then_inc(rooted, 1)
        with act.Fori(0, NP) as i:
            for h in range(2):
                t = 2 * i + h
                act.wait_ge(turned, here(i, h))
                act.activation(xT[:, :, :, bass.ds(t * 32, 32)], t_ps[h][:, :, :].rearrange("p c (a g) -> p c a g", g=32),
                               ACT.Copy).then_inc(xT_ready, 1)
            for h in range(2):
                act.wait_ge(q_ready, here(i, h))
                act.wait_ge(s_ready, before(i, h))
                act.activation(qT[h][:, :, :], q_ps[h][:, :, :], ACT.Copy).then_inc(qT_ready, 1)
            for h in range(2):
                act.wait_ge(s_ready, here(i, h))
                act.wait_ge(at_ready, before(i, h))
                act.activation(sims[h][:, :, :], s_ps[h][:, :, :], ACT.Copy).then_inc(sims_ready, 1)

    @block.vector
    def _(dve):
        for k in range(4):
            dve.wait_ge(x_in[k], 64)
            for t in range(4 * k, 4 * k + 4):
                last = dve.bn_stats(stats[:, t, :], X8[:, t, :])
        last.then_inc(step, 1)
        dve.wait_ge(step, 1)
        n = row_stats(dve, stats, m[:, :], var[:, :], w1[:, :], w2[:, :], step, 1)
        dve.wait_ge(step, n)
        dve.tensor_scalar(var[:, :], var[:, :], LN_EPS, None, ALU.add).then_inc(step, 1)
        n = rsqrt(dve, asked, rooted, 1, rstd[:, :], var[:, :], root[:, :], w1[:, :], step, n + 1)
        dve.wait_ge(step, n)
        def normalise(t, h):
            dve.tensor_scalar(xn[h][:, :], X8[:, t, :], m[:, bass.ds(t, 1)], rstd[:, bass.ds(t, 1)],
                              ALU.subtract, ALU.mult).then_inc(xn_ready, 1)

        def choose(i, more):
            for h in range(2):
                dve.wait_ge(sims_ready, here(i, h))
                if more:
                    dve.wait_ge(turned, here(i, h))
                    normalise(2 * i + 2 + h, h)
                for n in range(2 * HD):
                    last = dve.max(out=best[h][:, n, :], in_=sims[h][:, n, :])
                last.then_inc(best_ready, 1)
            for h in range(2):
                dve.wait_ge(best_ready, here(i, h))
                bh = best[h][:, :, :].rearrange("p (n two) k -> p n two k", two=2)
                dve.tensor_tensor(sums[h][:, :, :, :], bh[:, :, 0, :].unsqueeze(3).to_broadcast([P, HD, KB, KB]),
                                  bh[:, :, 1, :].unsqueeze(2).to_broadcast([P, HD, KB, KB]), ALU.add).then_inc(sums_ready, 1)
                for n in range(2 * HD):
                    last = dve.max_index(out=at[h][:, n, :], in_max=best[h][:, n, :], in_values=sims[h][:, n, :])
                last.then_inc(at_ready, 1)
            for h in range(2):
                t = 2 * i + h
                dve.wait_ge(sums_ready, here(i, h))
                dve.wait_ge(at_ready, here(i, h))
                ah = at[h][:, :, :].rearrange("p (n two) k -> p two n k", two=2)
                for j in range(2):
                    dve.tensor_copy(I[:, j, bass.ds(t, 1), :].rearrange("p a (n k) -> p (a n) k", k=KB), ah[:, j, :, :])
                for n in range(HD):
                    last = dve.max(out=fin[h][:, n, :], in_=sums[h][:, n, :, :].rearrange("p a b -> p (a b)"))
                last.then_inc(fin_ready, 1)
            for h in range(2):
                t = 2 * i + h
                dve.wait_ge(fin_ready, here(i, h))
                dve.tensor_scalar(FW[:, bass.ds(t, 1), :].rearrange("p a (n k) -> p (a n) k", k=KB), fin[h][:, :, :], 0.0, None, ALU.max)
                for n in range(HD):
                    last = dve.max_index(out=pk[h][:, n, :], in_max=fin[h][:, n, :], in_values=sums[h][:, n, :, :].rearrange("p a b -> p (a b)"))
                last.then_inc(pk_ready, 1)
            for h in range(2):
                t = 2 * i + h
                dve.wait_ge(pk_ready, here(i, h))
                dve.tensor_copy(PK[:, bass.ds(t, 1), :].rearrange("p a (n k) -> p (a n) k", k=KB), pk[h][:, :, :]).then_inc(kept, 1)

        for h in range(2):
            normalise(h, h)
        with dve.Fori(0, NP - 1) as i:
            choose(i, True)
        choose(NP - 1, False)
        dve.wait_ge(kept, 2 * NP + 2)
        dve.wait_ge(io_made, 1)
        link = linker(dve, chain)
        for a in range(4):
            link(dve.memset(sec[a * 32:(a + 1) * 32, :], 32.0 * a))
        link(dve.tensor_scalar(PH[:, :, :], PK[:, :, :], 1.0 / KB, -(KB - 1) / (2 * KB), ALU.mult, ALU.add))
        link(dve.tensor_scalar(PH[:, :, :], PH[:, :, :], MAGIC, None, ALU.add))
        link(dve.tensor_scalar(PH[:, :, :], PH[:, :, :], -MAGIC, None, ALU.add))
        link(dve.scalar_tensor_tensor(PK[:, :, :], PH[:, :, :], -float(KB), PK[:, :, :], ALU.mult, ALU.add))
        for j, r in ((0, PH), (1, PK)):
            link(dve.tensor_tensor(M[:, :, :], r[:, :, :].rearrange("p t s -> p (t s)").unsqueeze(2).to_broadcast([P, NT * S, KB]),
                                   kio[:, :].unsqueeze(1).to_broadcast([P, NT * S, KB]), ALU.is_equal))
            M4 = M[:, :, :].rearrange("p (a s) k -> p a s k", s=KB)
            link(dve.tensor_tensor(M4, M4, I[:, j, :, :].rearrange("p t (n k) -> p (t n) k", k=KB).unsqueeze(2).to_broadcast([P, NT * HD, KB, KB]), ALU.mult))
            link(dve.tensor_reduce(r[:, :, :].rearrange("p t s -> p (t s)"), M[:, :, :], AX.X, ALU.add))
        link(dve.tensor_scalar(M[:, 0:NT * S // KB, :].rearrange("p a k -> p (a k)"), PH[:, :, :].rearrange("p t s -> p (t s)"), float(E1), float(NK - 1), ALU.is_ge, ALU.mult))
        link(dve.tensor_tensor(PK[:, :, :].rearrange("p t s -> p (t s)"), PK[:, :, :].rearrange("p t s -> p (t s)"), M[:, 0:NT * S // KB, :].rearrange("p a k -> p (a k)"), ALU.max))
        link(dve.tensor_scalar(PH[:, :, :], PH[:, :, :], float(E1 - 1), None, ALU.min))
        for j, r in ((0, PH), (1, PK), (2, FW)):
            link(dve.transpose(TR[:, j, :], r[:, :, :].rearrange("p t s -> p (t s)")))
        link(dve.tensor_scalar(TR[:, 0, :], TR[:, 0, :], sec[:, 0:1], None, ALU.add))
        W3 = M[:, :, :].rearrange("p a k -> p (a k)").bitcast(BF16)
        for k in range(2, 5):
            link(dve.tensor_copy(W3[:, 0:NT * S], TR[:, k, :]))
            if k < 4:
                link(dve.tensor_tensor(TR[:, k + 1, :], TR[:, k, :], W3[:, 0:NT * S], ALU.subtract))
            link(dve.tensor_copy(TR[:, k, :], W3[:, 0:NT * S]))

    ph.end()


def retrieve_phase(nc, R, A, name, x_dram, xT, TR, gate, out):
    ph = Phase(nc, name)
    tg = R["tg"]
    NQ, CH = N // 512, 512
    EB = A["L3_ffn_e_down"].shape[0]
    NP = EB // 2
    GR = CH // 4 // EB

    def two(n, shape, dt=F32):
        return [ph.sb(f"{n}{h}", shape, dt) for h in range(2)]

    G = ph.sb("G", [P, 2, EB, CH])
    ed, eu, sl, at = two("ed", [P, DC, P]), two("eu", [P, D]), two("sl", [P, CH]), two("at", [P, CH])
    oh2, oh1 = two("oh2", [P, GR, P], BF16), two("oh1", [P, 3, GR, P], BF16)
    xr, io, iob, zero = ph.sb("xr", [P, 4, D]), ph.sb("io", [P, P]), ph.sb("iob", [P, P], BF16), ph.sb("zero", [P, CH], BF16)
    h_ps = [ph.ps(f"h_ps{h}", [P, CH]) for h in range(2)]
    g_ps = [ph.ps(f"g_ps{h}", [P, GR, P]) for h in range(2)]
    o_ps = [ph.ps(f"o_ps{a}", [P, D]) for a in range(4)]
    io_made, zeroed, iob_made = ph.sem("io"), ph.sem("zeroed"), ph.sem("iob")
    ed_in, eu_in = [ph.pair_sem(f"ed_in{h}") for h in range(2)], [ph.pair_sem(f"eu_in{h}") for h in range(2)]
    h_ready, sl_ready, at_ready, used = (ph.pair_sem(n) for n in ("h", "sl", "at", "used"))
    oh_ready, g_ready, G_ready = (ph.pair_sem(n) for n in ("oh", "g", "G"))
    xr_in, summed, y_ready, stored = ph.sem("xr_in"), ph.sem("summed"), ph.sem("y"), ph.sem("stored")
    block = ph.start()

    @block.sync
    def _(sp):
        for q in range(NQ):
            with sp.Fori(0, NP) as k:
                i = q * NP + k
                for h in range(2):
                    e = 2 * k + h
                    sp.wait_ge(h_ready, before(i, h))
                    sp.dma_start(ed[h][:, :, :], A["L3_ffn_e_down"][bass.ds(e, 1)].rearrange("e p c k -> p (e c) k")).then_inc(ed_in[h], 16)
                    sp.wait_ge(used, before(i, h))
                    sp.dma_start(eu[h][:, :], A["L3_ffn_e_up"][bass.ds(e, 1)].rearrange("e p c -> p (e c)")).then_inc(eu_in[h], 16)

    @block.gpsimd
    def _(pool):
        pool.iota(io[:, :], pattern=[[1, P]], base=0, channel_multiplier=0, allow_small_or_imprecise_dtypes=True).then_inc(io_made, 1)
        pool.memset(zero[:, :], 0.0).then_inc(zeroed, 1)
        for q in range(NQ):
            rows = slice(q * CH, (q + 1) * CH)
            if q:
                pool.wait_ge(stored, 16 * q)
            pool.dma_start(xr[:, :, :], x_dram[rows, :].rearrange("(a p) c -> p a c", p=P)).then_inc(xr_in, 16)
            pool.wait_ge(y_ready, 4 * (q + 1))
            pool.dma_start(out[rows, :].rearrange("(a p) c -> p a c", p=P), xr[:, :, :]).then_inc(stored, 16)
        pool.wait_ge(stored, 16 * NQ)

    def weigh(pe, i, h):
        pe.wait_ge(oh_ready, here(i, h))
        pe.wait_ge(G_ready, before(i, h))
        for g in range(GR):
            for k in range(3):
                last = pe.matmul(g_ps[h][:, g, :], lhsT=oh2[h][:, g, :], rhs=oh1[h][:, k, g, :], start=(k == 0), stop=(k == 2))
        last.then_inc(g_ready, 1)

    @block.tensor
    def _(pe):
        pe.wait_ge(zeroed, 1)
        with pe.Fori(0, NP) as i:
            for h in range(2):
                weigh(pe, i, h)
        for q in range(NQ):
            if q:
                pe.wait_ge(y_ready, 4 * q)
            for a in range(4):
                pe.matmul(o_ps[a][:, :], lhsT=zero[:, 0:P], rhs=zero[:, :], start=True, stop=False)
            with pe.Fori(0, NP) as k:
                i = q * NP + k
                for h in range(2):
                    pe.wait_ge(ed_in[h], 16 * i + 18)
                    pe.wait_ge(sl_ready, before(i, h))
                    for c in range(DC):
                        last = pe.matmul(h_ps[h][:, :], lhsT=ed[h][:, c, :], rhs=xT[:, c, :, q * P:(q + 1) * P], start=(c == 0), stop=(c == DC - 1))
                    last.then_inc(h_ready, 1)
                if q < NQ - 1:
                    for h in range(2):
                        weigh(pe, i + NP, h)
                for h in range(2):
                    pe.wait_ge(eu_in[h], 16 * i + 18)
                    pe.wait_ge(at_ready, here(i, h))
                    for a in range(4):
                        last = pe.matmul(o_ps[a][:, :], lhsT=at[h][:, a * P:(a + 1) * P], rhs=eu[h][:, :], start=False, stop=False)
                    last.then_inc(used, 1)
            for a in range(4):
                last = pe.matmul(o_ps[a][:, :], lhsT=zero[:, 0:P], rhs=zero[:, :], start=False, stop=True)
            last.then_inc(summed, 1)

    def keep(act, i, q, k, h):
        act.wait_ge(g_ready, here(i, h))
        act.activation(G[:, q % 2, :, :].rearrange("p e (a l) -> p a e l", a=4)[:, :, :, bass.ds((2 * k + h) * GR, GR)],
                       g_ps[h][:, :, :].rearrange("p g (a e) -> p a e g", a=4), ACT.Copy).then_inc(G_ready, 1)

    @block.scalar
    def _(act):
        with act.Fori(0, NP) as i:
            for h in range(2):
                keep(act, i, 0, i, h)
        for q in range(NQ):
            with act.Fori(0, NP) as k:
                i = q * NP + k
                for h in range(2):
                    act.wait_ge(h_ready, here(i, h))
                    act.wait_ge(at_ready, before(i, h))
                    act.activation(sl[h][:, :], h_ps[h][:, :], ACT.Silu).then_inc(sl_ready, 1)
                if q < NQ - 1:
                    for h in range(2):
                        keep(act, i + NP, q + 1, k, h)

    def one_hots(dve, i, q, k, h):
        dve.wait_ge(g_ready, before(i, h))
        for g in range(GR):
            def col(j):
                return TR[:, j, bass.ds(q * P + (2 * k + h) * GR + g, 1)]
            dve.tensor_scalar(oh2[h][:, g, :], iob[:, :], col(1), None, ALU.is_equal)
            for j in range(3):
                last = dve.tensor_scalar(oh1[h][:, j, g, :], iob[:, :], col(0), col(2 + j), ALU.is_equal, ALU.mult)
        last.then_inc(oh_ready, 1)

    @block.vector
    def _(dve):
        dve.wait_ge(io_made, 1)
        dve.tensor_copy(iob[:, :], io[:, :]).then_inc(iob_made, 1)
        dve.wait_ge(iob_made, 1)
        with dve.Fori(0, NP) as i:
            for h in range(2):
                one_hots(dve, i, 0, i, h)
        for q in range(NQ):
            dve.wait_ge(G_ready, here(q * NP + NP - 1, 1))
            with dve.Fori(0, NP) as k:
                i = q * NP + k
                for h in range(2):
                    dve.wait_ge(sl_ready, here(i, h))
                    dve.wait_ge(used, before(i, h))
                    dve.tensor_tensor(at[h][:, :], sl[h][:, :], G[:, q % 2, 2 * k + h, :], ALU.mult).then_inc(at_ready, 1)
                if q < NQ - 1:
                    for h in range(2):
                        one_hots(dve, i + NP, q + 1, k, h)
            dve.wait_ge(summed, q + 1)
            dve.wait_ge(xr_in, 16 * (q + 1))
            for a in range(4):
                dve.scalar_tensor_tensor(xr[:, a, :], o_ps[a][:, :], tg[:, gate:gate + 1], xr[:, a, :], ALU.mult, ALU.add).then_inc(y_ready, 1)

    ph.end()


def build(nc, A, out):
    with ExitStack() as ctx:
        def sb(name, shape, dt=F32):
            return ctx.enter_context(nc.sbuf_tensor(name, shape, dt))

        R = {"ident": sb("ident", [P, P]), "identb": sb("identb", [P, P], BF16), "ones": sb("ones", [P, P]),
             "tg": sb("tg", [P, 8]), "stats": sb("stats", [P, NT, 6]), "magic": sb("magic", [P, 2])}
        x7 = nc.dram_tensor("x7", (N, D), F32, kind="Internal").ap()
        F = A["L0_ffn_w_downT"].shape[0]
        with nc.sbuf_tensor("X", [P, NT, D], F32) as X:
            R["X"] = X
            setup_phase(nc, R, A)
            wkv_phase(nc, R, A, "L0x", 0, "L0_xattn_w", "L0_xattn_u", False)
            with nc.sbuf_tensor("wgu_q", [P, DC, 2 * F], BF16) as wgu_q, nc.sbuf_tensor("wd_q", [P, F // P, D], BF16) as wd_q, \
                    nc.sbuf_tensor("unit", [P, 3], F32) as unit:
                ternary_phase(nc, R, A, wgu_q, wd_q, unit)
                bitnet_phase(nc, R, A, wgu_q, wd_q, unit, 4)
            with nc.sbuf_tensor("KV", [P, B * DC, 2 * P], F32) as KV:
                summary_phase(nc, R, A, KV)
                linear_attention_phase(nc, R, A, KV, 1)
            spline_phase(nc, R, A, 5)
            wkv_phase(nc, R, A, "L2x", 2, "L2_xattn_time_decay", "L2_xattn_time_first", True)
            experts_phase(nc, R, A, 6)
            decay_phase(nc, R, A, 3, x7)
        with nc.sbuf_tensor("xT", [P, DC, 4, NT * 32], F32) as xT, nc.sbuf_tensor("TR", [P, 5, NT * 32], F32) as TR:
            route_phase(nc, R, A, "L3r", x7, xT, TR)
            retrieve_phase(nc, R, A, "L3f", x7, xT, TR, 7, out)


def kernel(**inputs):
    import numpy as np
    import concourse.bacc as bacc
    from concourse.bass_utils import run_bass_kernel_spmd

    def rows(name, n):
        return np.ascontiguousarray(inputs[name]).reshape(n, -1)

    def turned(name, n):
        return np.ascontiguousarray(rows(name, n).T)

    laid = {
        "x": rows("x", N),
        "ctxT": turned("ctx_2048", N),
        "g_xattn": inputs["g_xattn"], "g_ffn": inputs["g_ffn"],
        "L0_ffn_w_gate_upT": turned("L0_ffn_w_gate_up", 2816), "L0_ffn_w_downT": turned("L0_ffn_w_down", 512),
        "L0_ffn_norm_weight": inputs["L0_ffn_norm_weight"],
        "L1_xattn_WqT": turned("L1_xattn_Wq", D), "L1_xattn_WgT": turned("L1_xattn_Wg", D),
        "L1_xattn_WkvT": turned("L1_xattn_Wkv", 2 * D), "L1_xattn_WoT": turned("L1_xattn_Wo", D),
        "L1_xattn_bg": inputs["L1_xattn_bg"],
        **{n: inputs[n] for n in ("L1_ffn_ln_gamma", "L1_ffn_ln_beta", "L1_ffn_spline_bases", "L1_ffn_spline_slopes",
                                  "L1_ffn_output_scale", "L2_xattn_time_decay", "L2_xattn_time_first")},
        "L2_ffn_downT": turned("L2_ffn_down_w", 128), "L2_ffn_routerT": turned("L2_ffn_router_w", 8),
        "L2_ffn_up": np.transpose(inputs["L2_ffn_up_w"], (0, 2, 1)).reshape(128, D),
        "ctx": rows("ctx_2048", N),
        "L3_xattn_decay": np.asarray(inputs["L3_xattn_decay"]).reshape(1),
        "L3_xattn_W_inT": turned("L3_xattn_W_in", D), "L3_xattn_W_outT": turned("L3_xattn_W_out", D),
        **{n: inputs[n] for n in ("L3_xattn_b_in", "L3_xattn_b_out", "L3_xattn_gamma", "L3_xattn_beta")},
        "L3_ffn_Wq": inputs["L3_ffn_Wq"],
        "L3_ffn_keys": np.transpose(inputs["L3_ffn_keys"], (2, 3, 0, 1)),
        "L3_ffn_e_down": np.transpose(np.reshape(inputs["L3_ffn_e_down"], (32, P, DC, P)), (0, 3, 2, 1)),
        "L3_ffn_e_up": np.reshape(inputs["L3_ffn_e_up"], (32, P, D)),
        "L0_xattn_w": inputs["L0_xattn_w"], "L0_xattn_u": inputs["L0_xattn_u"],
    }
    nc = bacc.Bacc("TRN2", target_bir_lowering=False, num_devices=1)
    arrays, A = {}, {}
    for name, a in laid.items():
        a = np.ascontiguousarray(a)
        arrays[f"in_{name}"] = a
        A[name] = nc.dram_tensor(f"in_{name}", a.shape, mybir.dt.from_np(a.dtype), kind="ExternalInput").ap()
    out = nc.dram_tensor("out", (N, D), F32, kind="ExternalOutput").ap()
    build(nc, A, out)
    r = run_bass_kernel_spmd(nc, [arrays], core_ids=[0])
    return r.results[0]["out"].reshape(B, T, D)
```

```python
from contextlib import ExitStack

import concourse.bass as bass
from concourse import mybir

ALU = mybir.AluOpType
ACT = mybir.ActivationFunctionType
F32 = mybir.dt.float32
BF16 = mybir.dt.bfloat16
F32R = mybir.dt.float32r
U32 = mybir.dt.uint32
AX = mybir.AxisListType

P = 128
B, T, D = 8, 256, 512
N = B * T
NT = N // P
DC = D // P
TB = T // P
LN_EPS = 1e-5
NEG = -1e38
EXP_MAX = 40.0
MAGIC = 1.5 * 2.0 ** 23


def here(i, h):
    return 2 * i + h + 3


def before(i, h):
    return 2 * i + h + 1


def both(i):
    return 2 * i + 4


class Phase:

    def __init__(self, nc, name):
        self.nc, self.name, self.ctx = nc, name, ExitStack()
        self.sems, self.pairs = [], []

    def sb(self, name, shape, dt=F32):
        return self.ctx.enter_context(self.nc.sbuf_tensor(f"{self.name}_{name}", shape, dt))

    def ps(self, name, shape, dt=F32):
        return self.ctx.enter_context(self.nc.psum_tensor(f"{self.name}_{name}", shape, dt))

    def sem(self, name):
        s = self.ctx.enter_context(self.nc.semaphore(f"{self.name}_{name}"))
        self.sems.append(s)
        return s

    def pair_sem(self, name):
        s = self.sem(name)
        self.pairs.append(s)
        return s

    def start(self):
        with self.nc.Block(no_gpsimd_drain=True) as block:
            @block.sync
            def _(sp):
                for s in self.sems:
                    sp.sem_clear(s)
                for s in self.pairs:
                    sp.sem_inc(s, 2)
        return self.ctx.enter_context(self.nc.Block(no_gpsimd_drain=True))

    def end(self):
        self.ctx.close()


def row_stats(dve, stats, m, var, w1, w2, step, at):
    dve.tensor_tensor(w1, stats[:, :, 1], stats[:, :, 4], ALU.add).then_inc(step, 1)
    dve.tensor_tensor(w2, stats[:, :, 1], stats[:, :, 4], ALU.subtract).then_inc(step, 1)
    dve.tensor_tensor(var, stats[:, :, 2], stats[:, :, 5], ALU.add).then_inc(step, 1)
    dve.wait_ge(step, at + 3)
    dve.tensor_scalar(m, w1, 0.5, None, ALU.mult).then_inc(step, 1)
    dve.scalar_tensor_tensor(w2, w2, 0.25, w2, ALU.mult, ALU.mult).then_inc(step, 1)
    dve.wait_ge(step, at + 5)
    dve.scalar_tensor_tensor(var, var, 1.0 / D, w2, ALU.mult, ALU.add).then_inc(step, 1)
    return at + 6


def rsqrt(dve, act_ask, act_said, asked, out, a, root, w, step, at):
    dve.wait_ge(step, at)
    dve.sem_inc(act_ask, 1)
    dve.wait_ge(act_said, asked)
    dve.reciprocal(out, root).then_inc(step, 1)
    dve.wait_ge(step, at + 1)
    dve.tensor_tensor(w, out, out, ALU.mult).then_inc(step, 1)
    dve.wait_ge(step, at + 2)
    dve.tensor_tensor(w, w, a, ALU.mult).then_inc(step, 1)
    dve.wait_ge(step, at + 3)
    dve.tensor_scalar(w, w, -0.5, 1.5, ALU.mult, ALU.add).then_inc(step, 1)
    dve.wait_ge(step, at + 4)
    dve.tensor_tensor(out, out, w, ALU.mult).then_inc(step, 1)
    return at + 5


def setup_phase(nc, R, A):
    ph = Phase(nc, "setup")
    g = ph.sb("g", [P, 8])
    x_in, g_in = [ph.sem(f"x_in{k}") for k in range(4)], ph.sem("g_in")
    zeroed, made, gated, stated = ph.sem("zeroed"), ph.sem("made"), ph.sem("gated"), ph.sem("stated")
    X, ident, identb, ones, tg, stats = R["X"], R["ident"], R["identb"], R["ones"], R["tg"], R["stats"]
    block = ph.start()
    QT = NT // 4

    @block.sync
    def _(sp):
        for k in range(4):
            sp.dma_start(X[:, k * QT:(k + 1) * QT, :],
                         A["x"].rearrange("(t p) c -> p t c", p=P)[:, k * QT:(k + 1) * QT, :]).then_inc(x_in[k], 16)
        sp.dma_start(g[:, 0:4], A["g_xattn"].partition_broadcast(P)).then_inc(g_in, 16)
        sp.dma_start(g[:, 4:8], A["g_ffn"].partition_broadcast(P)).then_inc(g_in, 16)

    @block.gpsimd
    def _(pool):
        pool.memset(ident[:, :], 0.0).then_inc(zeroed, 1)
        pool.memset(ones[:, :], 1.0).then_inc(made, 1)
        pool.memset(R["magic"][:, 0:1], MAGIC)
        pool.memset(R["magic"][:, 1:2], -MAGIC)
        pool.wait_ge(zeroed, 1)
        pool.affine_select(out=ident[:, :], in_=ident[:, :], compare_op=ALU.not_equal, fill=1.0, base=0,
                           pattern=[[-1, P]], channel_multiplier=1).then_inc(made, 1)

    @block.scalar
    def _(act):
        act.wait_ge(g_in, 32)
        act.activation(tg[:, :], g[:, :], ACT.Tanh).then_inc(gated, 1)

    @block.vector
    def _(dve):
        dve.wait_ge(made, 2)
        dve.tensor_copy(identb[:, :], ident[:, :]).then_inc(stated, 1)
        for k in range(4):
            dve.wait_ge(x_in[k], 16)
            with dve.Fori(k * QT, (k + 1) * QT) as t:
                dve.bn_stats(stats[:, t, :], X[:, t, :]).then_inc(stated, 1)

    ph.end()


def wkv_phase(nc, R, A, name, gate, w_name, u_name, negate_exp, KV=None):
    ph = Phase(nc, name)
    X, ident, tg, stats = R["X"], R["ident"], R["tg"], R["stats"]
    NP = B // 2
    HD = 32
    m, var, rstd, root, w1, w2 = (ph.sb(n, [P, NT]) for n in ("m", "var", "rstd", "root", "w1", "w2"))
    w, u = ph.sb("w", [P, DC]), ph.sb("u", [P, DC])

    def two(n, shape):
        return [ph.sb(f"{n}{h}", shape) for h in range(2)]

    xn = ph.sb("xn", [P, TB, D])
    V = ph.sb("V", [P, 4, DC, T])
    kT = two("kT", [P, DC, T])
    o, p, q = (two(n, [P, DC, T + 1]) for n in "opq")
    a, e, g = two("a", [P, DC, T]), two("e", [P, DC, T]), two("g", [P, DC, T])
    den, num, r = two("den", [P, DC, T]), two("num", [P, DC, T]), two("r", [P, DC, T])
    t_ps = [ph.ps(f"t_ps{j}", [P, DC, P]) for j in range(TB)]

    wu_in, v_in = ph.sem("wu_in"), [ph.pair_sem(f"v_in{h}") for h in range(2)]
    step, asked, rooted, w_ready = ph.sem("step"), ph.sem("asked"), ph.sem("rooted"), ph.sem("w_ready")
    inited = ph.sem("inited")
    xn_ready, xn_used, k_ready = ph.pair_sem("xn_ready"), ph.pair_sem("xn_used"), ph.pair_sem("k_ready")
    o_ready, da_ready, de_ready, dg_ready, gc_ready = (ph.pair_sem(n) for n in ("o_ready", "da", "de", "dg", "gc"))
    a_ready, e_ready, g_ready, ev_ready = (ph.pair_sem(n) for n in ("a_ready", "e_ready", "g_ready", "ev_ready"))
    pq_ready, qv_ready, num_ready, den_ready = (ph.pair_sem(n) for n in ("pq", "qv", "num", "den"))
    ln_ready, r_ready, t_ready, r2_ready, yd_ready = (ph.pair_sem(n) for n in ("ln", "r", "t", "r2", "yd"))
    y_ready, yT_ready, x_ready, st_ready = (ph.pair_sem(n) for n in ("y", "yT", "x", "st"))
    if KV is not None:
        W, mask = ph.sb("W", [P, DC, 2 * D]), ph.sb("mask", [P, P // HD, HD])
        ct, se, sk, sv = two("ct", [P, DC, P]), two("se", [P, D]), two("sk", [P, D]), two("sv", [P, DC, 2, P])
        k_ps, v_ps = [ph.ps(f"k_ps{h}", [P, D]) for h in range(2)], [ph.ps(f"v_ps{h}", [P, D]) for h in range(2)]
        s_ps = [ph.ps(f"s_ps{g}", [P, 2, 2, P]) for g in range(2)]
        W_in, c_in = ph.sem("W_in"), [ph.sem(f"c_in{h}") for h in range(2)]
        masked, filled = ph.sem("masked"), ph.sem("filled")
        kv_ready, sr_ready, se_ready, sk_ready, sv_ready, s_ready = (ph.pair_sem(n) for n in ("kv", "sr", "se", "sk", "sv", "s"))
        KV_ready = ph.pair_sem("KV")
    block = ph.start()

    def slot(i, h):
        return (i % 2) * 2 + h

    @block.sync
    def _(sp):
        sp.dma_start(w[:, :], A[w_name].rearrange("(c p) -> p c", p=P),
                     allow_slow_non_contiguous=True).then_inc(wu_in, 16)
        sp.dma_start(u[:, :], A[u_name].rearrange("(c p) -> p c", p=P),
                     allow_slow_non_contiguous=True).then_inc(wu_in, 16)
        ctxT = A["ctxT"].rearrange("(c p) n -> p c n", p=P)

        def load_v(i, h):
            sp.dma_start(V[:, slot(i, h), :, :], ctxT[:, :, bass.ds((2 * i + h) * T, T)]).then_inc(v_in[h], 16)

        def load_ct(b, j):
            sp.wait_ge(kv_ready, before(b, j))
            sp.dma_start(ct[j][:, :, :], ctxT[:, :, bass.ds((TB * b + j) * P, P)]).then_inc(c_in[j], 16)

        for h in range(2):
            load_v(0, h)
        if KV is not None:
            sp.dma_start(W[:, :, :], A["L1_xattn_WkvT"].rearrange("(c p) n -> p c n", p=P)).then_inc(W_in, 16)
        with sp.Fori(0, NP - 1) as i:
            for h in range(2):
                if KV is not None:
                    load_ct(2 * i, h)
            for h in range(2):
                sp.wait_ge(y_ready, before(i, h))
                sp.wait_ge(v_in[h], 16 * i + 18)
                load_v(i + 1, h)
            for h in range(2):
                if KV is not None:
                    load_ct(2 * i + 1, h)
        if KV is not None:
            for b in (B - 2, B - 1):
                for j in range(TB):
                    load_ct(b, j)

    @block.tensor
    def _(pe):
        def turn(i, h, again):
            pe.wait_ge(xn_ready, here(i, h))
            pe.wait_ge(k_ready, here(i, h) - 1)
            pe.wait_ge(x_ready, 2 * i if again else 2)
            for j in range(TB):
                for c in range(DC):
                    last = pe.transpose(t_ps[j][:, c, :], xn[:, j, c * P:(c + 1) * P], ident[:, :])
            last.then_inc(xn_used, 1)

        def turn_back(i, fronts):
            for h in range(2):
                pe.wait_ge(y_ready, here(i, h))
                pe.wait_ge(k_ready, both(fronts))
                pe.wait_ge(x_ready, here(i, h) - 1)
                for j in range(TB):
                    for c in range(DC):
                        last = pe.transpose(t_ps[j][:, c, :], num[h][:, c, j * P:(j + 1) * P], ident[:, :])
                last.then_inc(yT_ready, 1)

        def project(b, j):
            if KV is None:
                return
            pe.wait_ge(c_in[j], 16 * b + 16)
            pe.wait_ge(sk_ready, before(b, j))
            pe.wait_ge(sv_ready, before(b, j))
            for c in range(DC):
                pe.matmul(k_ps[j][:, :], lhsT=ct[j][:, c, :], rhs=W[:, c, 0:D], start=(c == 0), stop=(c == DC - 1))
            for c in range(DC):
                last = pe.matmul(v_ps[j][:, :], lhsT=ct[j][:, c, :], rhs=W[:, c, D:2 * D], start=(c == 0), stop=(c == DC - 1))
            last.then_inc(kv_ready, 1)

        def add_up(b):
            if KV is None:
                return
            for j in range(2):
                pe.wait_ge(sk_ready, here(b, j))
                pe.wait_ge(sv_ready, here(b, j))
            pe.wait_ge(KV_ready, before(b, 1))
            for g_ in range(DC):
                for j in range(2):
                    last = pe.matmul(s_ps[g_ // 2][:, g_ % 2, :, :], lhsT=sk[j][:, g_ * P:(g_ + 1) * P], rhs=sv[j][:, g_, :, :],
                                     start=(j == 0), stop=(j == 1))
                if g_ % 2:
                    last.then_inc(s_ready, 1)

        def finish(i, fronts):
            project(2 * i, 1)
            project(2 * i + 1, 0)
            add_up(2 * i)
            project(2 * i + 1, 1)
            turn_back(i, fronts)
            add_up(2 * i + 1)

        if KV is not None:
            pe.wait_ge(W_in, 16)
            pe.wait_ge(filled, 2)
        for h in range(2):
            turn(0, h, False)
        with pe.Fori(0, NP - 1) as i:
            turn(i + 1, 0, True)
            project(2 * i, 0)
            turn(i + 1, 1, True)
            finish(i, i + 1)
        project(B - 2, 0)
        finish(NP - 1, NP - 1)

    @block.scalar
    def _(act):
        def take(i):
            for h in range(2):
                act.wait_ge(xn_used, here(i, h))
                act.wait_ge(pq_ready, before(i, h))
                for j in range(TB):
                    last = act.activation(kT[h][:, :, j * P:(j + 1) * P], t_ps[j][:, :, :], ACT.Copy)
                last.then_inc(k_ready, 1)

        def weigh(i):
            for h in range(2):
                act.wait_ge(da_ready, here(i, h))
                for c in range(DC):
                    last = act.activation(a[h][:, c, :], a[h][:, c, :], ACT.Exp, bias=w[:, c:c + 1])
                last.then_inc(a_ready, 1)
                act.wait_ge(de_ready, here(i, h))
                act.activation(e[h][:, :, :], e[h][:, :, :], ACT.Exp).then_inc(e_ready, 1)
                act.wait_ge(gc_ready, here(i, h))
                act.activation(g[h][:, :, :], g[h][:, :, :], ACT.Exp).then_inc(g_ready, 1)

        def invert(i):
            for h in range(2):
                act.wait_ge(den_ready, here(i, h))
                act.wait_ge(yd_ready, before(i, h))
                act.activation(r[h][:, :, :], den[h][:, :, :], ACT.Ln).then_inc(ln_ready, 1)
            for h in range(2):
                act.wait_ge(ln_ready, here(i, h))
                act.activation(r[h][:, :, :], r[h][:, :, :], ACT.Exp, scale=-1.0).then_inc(r_ready, 1)

        def context(b, j):
            if KV is None:
                return
            act.wait_ge(kv_ready, here(b, j))
            act.wait_ge(sk_ready, before(b, j))
            act.activation(se[j][:, :], k_ps[j][:, :], ACT.Relu, scale=-1.0).then_inc(sr_ready, 1)
            act.wait_ge(s_ready, before(b, 1))
            act.activation(sv[j][:, :, 0, :], v_ps[j][:, :].rearrange("p (g e) -> p g e", g=DC), ACT.Copy).then_inc(sv_ready, 1)
            act.wait_ge(sr_ready, here(b, j))
            act.activation(se[j][:, :], se[j][:, :], ACT.Exp, scale=-1.0).then_inc(se_ready, 1)

        act.wait_ge(wu_in, 32)
        if negate_exp:
            act.activation(w[:, :], w[:, :], ACT.Exp).then_inc(w_ready, 1)
        act.wait_ge(asked, 1)
        act.activation(root[:, :], var[:, :], ACT.Sqrt).then_inc(rooted, 1)
        act.wait_ge(inited, 1)
        take(0)
        weigh(0)
        with act.Fori(0, NP - 1) as i:
            take(i + 1)
            invert(i)
            context(2 * i, 0)
            context(2 * i, 1)
            weigh(i + 1)
            context(2 * i + 1, 0)
            context(2 * i + 1, 1)
        context(B - 2, 0)
        invert(NP - 1)
        context(B - 2, 1)
        context(B - 1, 0)
        context(B - 1, 1)

    @block.gpsimd
    def _(pool):
        if KV is not None:
            pool.memset(mask[:, :, :], 1.0).then_inc(masked, 1)
            pool.wait_ge(masked, 1)
            pool.affine_select(out=mask[:, :, :], in_=mask[:, :, :], compare_op=ALU.is_ge, fill=0.0, base=0,
                               pattern=[[-HD, P // HD], [0, HD]], channel_multiplier=1).then_inc(masked, 1)
            pool.wait_ge(masked, 2)
            pool.affine_select(out=mask[:, :, :], in_=mask[:, :, :], compare_op=ALU.is_ge, fill=0.0, base=HD - 1,
                               pattern=[[HD, P // HD], [0, HD]], channel_multiplier=-1).then_inc(masked, 1)
            for h in range(2):
                pool.memset(sv[h][:, :, 1, :], 1.0).then_inc(filled, 1)

        def bonus(i):
            for h in range(2):
                pool.wait_ge(o_ready, here(i, h))
                pool.wait_ge(k_ready, here(i, h))
                pool.tensor_tensor(g[h][:, :, :], kT[h][:, :, :], o[h][:, :, 0:T], ALU.subtract).then_inc(dg_ready, 1)

        def add_v(i):
            for h in range(2):
                pool.wait_ge(v_in[h], 16 * i + 18)
                pool.wait_ge(e_ready, here(i, h))
                pool.wait_ge(gc_ready, here(i, h))
                pool.tensor_tensor(kT[h][:, :, :].unsqueeze(1), e[h][:, :, :].unsqueeze(1), V[:, bass.ds(slot(i, h), 1), :, :],
                                   ALU.mult).then_inc(ev_ready, 1)

        def numerator(i, h):
            pool.wait_ge(pq_ready, here(i, h))
            pool.wait_ge(yT_ready, before(i, h))
            pool.tensor_tensor(num[h][:, :, :].unsqueeze(1), q[h][:, :, 0:T].unsqueeze(1), V[:, bass.ds(slot(i, h), 1), :, :],
                               ALU.mult).then_inc(qv_ready, 1)
            pool.wait_ge(qv_ready, here(i, h))
            pool.tensor_tensor(num[h][:, :, :], p[h][:, :, 0:T], num[h][:, :, :], ALU.subtract).then_inc(num_ready, 1)

        bonus(0)
        add_v(0)
        with pool.Fori(0, NP - 1) as i:
            numerator(i, 0)
            bonus(i + 1)
            numerator(i, 1)
            add_v(i + 1)
        numerator(NP - 1, 0)
        numerator(NP - 1, 1)

    @block.vector
    def _(dve):
        n = row_stats(dve, stats, m[:, :], var[:, :], w1[:, :], w2[:, :], step, 0)
        dve.wait_ge(step, n)
        dve.tensor_scalar(var[:, :], var[:, :], LN_EPS, None, ALU.add).then_inc(step, 1)
        n = rsqrt(dve, asked, rooted, 1, rstd[:, :], var[:, :], root[:, :], w1[:, :], step, n + 1)
        for h in range(2):
            dve.memset(o[h][:, :, 0:1], NEG).then_inc(step, 1)
            dve.memset(p[h][:, :, 0:1], 0.0).then_inc(step, 1)
            dve.memset(q[h][:, :, 0:1], 0.0).then_inc(step, 1)
        dve.wait_ge(wu_in, 32)
        if negate_exp:
            dve.wait_ge(w_ready, 1)
            dve.tensor_scalar(w[:, :], w[:, :], -1.0, None, ALU.mult).then_inc(step, 1)
        dve.wait_ge(step, n + 6 + int(negate_exp))
        dve.sem_inc(inited, 1)

        def normalise(i, h):
            dve.wait_ge(xn_used, here(i, h) - 1)
            for j in range(TB):
                t = (2 * i + h) * TB + j
                last = dve.tensor_scalar(xn[:, j, :], X[:, t, :], m[:, bass.ds(t, 1)], rstd[:, bass.ds(t, 1)],
                                         ALU.subtract, ALU.mult)
            last.then_inc(xn_ready, 1)

        def front(i):
            for h in range(2):
                dve.wait_ge(k_ready, here(i, h))
                for c in range(DC):
                    last = dve.tensor_tensor_scan(o[h][:, c, 1:T + 1], w[:, c:c + 1].to_broadcast([P, T]),
                                                  kT[h][:, c, :], NEG, ALU.add, ALU.max)
                last.then_inc(o_ready, 1)
            for h in range(2):
                dve.wait_ge(o_ready, here(i, h))
                dve.tensor_tensor(a[h][:, :, :], o[h][:, :, 0:T], o[h][:, :, 1:T + 1], ALU.subtract).then_inc(da_ready, 1)
                dve.tensor_tensor(e[h][:, :, :], kT[h][:, :, :], o[h][:, :, 1:T + 1], ALU.subtract).then_inc(de_ready, 1)
            for h in range(2):
                dve.wait_ge(dg_ready, here(i, h))
                for c in range(DC):
                    last = dve.tensor_scalar(g[h][:, c, :], g[h][:, c, :], u[:, c:c + 1], EXP_MAX, ALU.add, ALU.min)
                last.then_inc(gc_ready, 1)

        def sums(i):
            for h in range(2):
                dve.wait_ge(a_ready, here(i, h))
                dve.wait_ge(ev_ready, here(i, h))
                dve.wait_ge(num_ready, before(i, h))
                for c in range(DC):
                    dve.tensor_tensor_scan(p[h][:, c, 1:T + 1], a[h][:, c, :], kT[h][:, c, :], 0.0, ALU.mult, ALU.add)
                    last = dve.tensor_tensor_scan(q[h][:, c, 1:T + 1], a[h][:, c, :], e[h][:, c, :], 0.0, ALU.mult, ALU.add)
                last.then_inc(pq_ready, 1)

        def denominator(i):
            for h in range(2):
                dve.wait_ge(pq_ready, here(i, h))
                dve.wait_ge(g_ready, here(i, h))
                dve.tensor_tensor(den[h][:, :, :], q[h][:, :, 0:T], g[h][:, :, :], ALU.add).then_inc(den_ready, 1)

        def invert(i):
            for h in range(2):
                dve.wait_ge(r_ready, here(i, h))
                dve.tensor_tensor(den[h][:, :, :], den[h][:, :, :], r[h][:, :, :], ALU.mult).then_inc(t_ready, 1)
            for h in range(2):
                dve.wait_ge(t_ready, here(i, h))
                dve.scalar_tensor_tensor(r[h][:, :, :], den[h][:, :, :], -2.0, r[h][:, :, :], ALU.add, ALU.mult).then_inc(r2_ready, 1)

        def result(i):
            for h in range(2):
                dve.wait_ge(r2_ready, here(i, h))
                dve.wait_ge(num_ready, here(i, h))
                dve.tensor_tensor(num[h][:, :, :], num[h][:, :, :], r[h][:, :, :], ALU.mult).then_inc(yd_ready, 1)
            for h in range(2):
                dve.wait_ge(yd_ready, here(i, h))
                dve.wait_ge(v_in[h], 16 * i + 18)
                dve.tensor_tensor(num[h][:, :, :].unsqueeze(1), V[:, bass.ds(slot(i, h), 1), :, :],
                                  num[h][:, :, :].unsqueeze(1), ALU.subtract).then_inc(y_ready, 1)

        def add_to_x(i):
            for h in range(2):
                dve.wait_ge(yT_ready, here(i, h))
                for j in range(TB):
                    t = (2 * i + h) * TB + j
                    last = dve.scalar_tensor_tensor(X[:, t, :], t_ps[j][:, :, :].rearrange("p c n -> p (c n)"),
                                                    tg[:, gate:gate + 1], X[:, t, :], ALU.mult, ALU.add)
                last.then_inc(x_ready, 1)
                dve.wait_ge(x_ready, here(i, h))
                for j in range(TB):
                    t = (2 * i + h) * TB + j
                    last = dve.bn_stats(stats[:, t, :], X[:, t, :])
                last.then_inc(st_ready, 1)

        def context(b, j):
            if KV is None:
                return
            dve.wait_ge(se_ready, here(b, j))
            dve.wait_ge(s_ready, before(b, 1))
            dve.scalar_tensor_tensor(sk[j][:, :], k_ps[j][:, :], 0.0, se[j][:, :], ALU.max, ALU.add).then_inc(sk_ready, 1)

        def keep(b):
            if KV is None:
                return
            for g_ in range(2):
                dve.wait_ge(s_ready, here(b, g_))
                dve.tensor_tensor(KV[:, bass.ds(4 * b + 2 * g_, 2), :].rearrange("p a (b n) -> p (a b) n", b=2),
                                  s_ps[g_][:, :, :, :].rearrange("p a b n -> p (a b) n"),
                                  mask[:, :, :].rearrange("p a b -> p (a b)").unsqueeze(1).to_broadcast([P, 4, P]),
                                  ALU.mult).then_inc(KV_ready, 1)

        if KV is not None:
            dve.wait_ge(masked, 3)
        for h in range(2):
            normalise(0, h)
        front(0)
        with dve.Fori(0, NP - 1) as i:
            normalise(i + 1, 0)
            sums(i)
            normalise(i + 1, 1)
            denominator(i)
            front(i + 1)
            context(2 * i, 0)
            context(2 * i, 1)
            invert(i)
            context(2 * i + 1, 0)
            result(i)
            keep(2 * i)
            context(2 * i + 1, 1)
            add_to_x(i)
            keep(2 * i + 1)
        sums(NP - 1)
        denominator(NP - 1)
        context(B - 2, 0)
        context(B - 2, 1)
        invert(NP - 1)
        context(B - 1, 0)
        result(NP - 1)
        keep(B - 2)
        context(B - 1, 1)
        add_to_x(NP - 1)
        keep(B - 1)

    ph.end()


def ternary_phase(nc, R, A, wgu_q, wd_q, unit):
    ph = Phase(nc, "ternary")
    F = A["L0_ffn_w_downT"].shape[0]
    FC = F // P
    wgu, wd = ph.sb("wgu", [P, DC, 2 * F]), ph.sb("wd", [P, FC, D])
    junk = ph.sb("junk", [P, 2 * F], BF16)
    sums, tot, scale = ph.sb("sums", [P, DC + 1]), ph.sb("tot", [P, 2]), ph.sb("scale", [P, 2])
    s_ps = ph.ps("s_ps", [P, DC + 1])
    wgu_in, wd_in = [ph.sem(f"wgu_in{c}") for c in range(DC)], ph.sem("wd_in")
    summed, d_summed, added, step = ph.sem("summed"), ph.sem("d_summed"), ph.sem("added"), ph.sem("step")
    scaled, clipped, rounded, done = ph.sem("scaled"), ph.sem("clipped"), ph.sem("rounded"), ph.sem("done")
    block = ph.start()
    wd1, wd1_q = wd[:, :, :].rearrange("p f n -> p (f n)"), wd_q[:, :, :].rearrange("p f n -> p (f n)")
    parts = [(wgu[:, c, :], wgu_q[:, c, :], 0) for c in range(DC)]
    parts += [(wd1[:, k:k + 2 * F], wd1_q[:, k:k + 2 * F], 1) for k in range(0, FC * D, 2 * F)]
    own = 3

    @block.sync
    def _(sp):
        for c in range(DC):
            sp.dma_start(wgu[:, c, :], A["L0_ffn_w_gate_upT"][c * P:(c + 1) * P, :]).then_inc(wgu_in[c], 16)
        sp.dma_start(wd[:, :, :], A["L0_ffn_w_downT"].rearrange("(f p) n -> p f n", p=P)).then_inc(wd_in, 16)

    @block.tensor
    def _(pe):
        pe.wait_ge(summed, DC)
        pe.wait_ge(d_summed, 1)
        pe.matmul(s_ps[:, :], lhsT=R["ones"][:, :], rhs=sums[:, :], start=True, stop=True).then_inc(added, 1)

    @block.scalar
    def _(act):
        for c in range(DC):
            act.wait_ge(wgu_in[c], 16)
            if c:
                act.wait_ge(summed, c)
            act.activation(junk[:, :], wgu[:, c, :], ACT.Abs, accum_out=sums[:, c:c + 1]).then_inc(summed, 1)
        act.wait_ge(step, 5)
        for w, _, k in parts[own:]:
            act.activation(w, w, ACT.Identity, scale=scale[:, k:k + 1], bias=R["magic"][:, 0:1]).then_inc(scaled, 1)
        for n, (w, q, _) in enumerate(parts[own:]):
            act.wait_ge(clipped, n + 1)
            act.activation(q, w, ACT.Identity, bias=R["magic"][:, 1:2]).then_inc(done, 1)

    @block.vector
    def _(dve):
        dve.wait_ge(wd_in, 16)
        dve.tensor_reduce(sums[:, DC:DC + 1], wd[:, :, :].rearrange("p f n -> p (f n)"), AX.X, ALU.add,
                          apply_absolute_value=True).then_inc(d_summed, 1)
        dve.wait_ge(added, 1)
        dve.tensor_reduce(tot[:, 0:1], s_ps[:, 0:DC], AX.X, ALU.add).then_inc(step, 1)
        dve.tensor_copy(tot[:, 1:2], s_ps[:, DC:DC + 1]).then_inc(step, 1)
        dve.wait_ge(step, 2)
        dve.tensor_scalar(unit[:, 0:1], tot[:, 0:1], 1.0 / (2 * F * D), 1e-5, ALU.mult, ALU.max).then_inc(step, 1)
        dve.tensor_scalar(unit[:, 1:2], tot[:, 1:2], 1.0 / (F * D), 1e-5, ALU.mult, ALU.max).then_inc(step, 1)
        dve.wait_ge(step, 4)
        dve.reciprocal(scale[:, :], unit[:, 0:2]).then_inc(step, 1)
        dve.wait_ge(step, 5)
        for n, (w, q, k) in enumerate(parts[:own]):
            dve.tensor_scalar(w, w, scale[:, k:k + 1], MAGIC, ALU.mult, ALU.add).then_inc(rounded, 1)
            dve.wait_ge(scaled, n + 1)
            dve.tensor_scalar(parts[own + n][0], parts[own + n][0], MAGIC + 1, MAGIC - 1, ALU.min, ALU.max).then_inc(clipped, 1)
            dve.wait_ge(rounded, 2 * n + 1)
            dve.tensor_scalar(w, w, MAGIC + 1, MAGIC - 1, ALU.min, ALU.max).then_inc(rounded, 1)
            dve.wait_ge(rounded, 2 * n + 2)
            dve.tensor_scalar(q, w, MAGIC, None, ALU.subtract)

    ph.end()


def bitnet_phase(nc, R, A, wgu_q, wd_q, unit, gate):
    ph = Phase(nc, "L0f")
    X, identb, tg, stats, magic = R["X"], R["identb"], R["tg"], R["stats"], R["magic"]
    F = wd_q.shape[1] * P
    FC = F // P
    CH = [(j, min(512, F - j)) for j in range(0, F, 512)]
    NCH = len(CH)
    m, var, r1, r2, root, w1, w2 = (ph.sb(n, [P, NT]) for n in ("m", "var", "r1", "r2", "root", "w1", "w2"))
    nw = ph.sb("nw", [P, D])

    def two(n, shape, dt=F32):
        return [ph.sb(f"{n}{h}", shape, dt) for h in range(2)]

    xn, xq, xqT = two("xn", [P, D]), two("xq", [P, D], BF16), two("xqT", [P, DC, P], BF16)
    s = ph.sb("s", [P, NT, 8])
    rl, hid = two("rl", [P, 512]), two("hid", [P, F])
    hq, hqT = two("hq", [P, F], BF16), two("hqT", [P, FC, P], BF16)
    x_ps = ph.ps("x_ps", [P, DC, P], BF16)
    g_ps, u_ps = [ph.ps(f"g_ps{k}", [P, 512]) for k in range(2)], [ph.ps(f"u_ps{k}", [P, 512]) for k in range(2)]
    h_ps = [ph.ps(f"h_ps{k}", [P, 8, P], BF16) for k in range(2)]
    o_ps = ph.ps("o_ps", [P, D])
    nw_in, step, asked, rooted = ph.sem("nw_in"), ph.sem("step"), ph.sem("asked"), ph.sem("rooted")
    xn_ready, am_ready, ac_ready, ar_ready, as_ready = (ph.pair_sem(n) for n in ("xn", "am", "ac", "ar", "as"))
    xm_ready, xq_ready, x_turned, xqT_ready = (ph.pair_sem(n) for n in ("xm", "xq", "x_turned", "xqT"))
    gu_ready, rl_ready, sq_ready, hid_ready = (ph.pair_sem(n) for n in ("gu", "rl", "sq", "hid"))
    hm_ready, hc_ready, hr_ready, hs_ready, hk_ready, hq_ready = (ph.pair_sem(n) for n in ("hm", "hc", "hr", "hs", "hk", "hq"))
    h_turned, hqT_ready, o_ready, x_ready, st_ready = (ph.pair_sem(n) for n in ("h_turned", "hqT", "o", "x", "st"))
    block = ph.start()

    def steps(eng, one):
        for n in range(2):
            one(n, n)
        with eng.Fori(1, NT // 2 - 2) as i:
            for h in range(2):
                one(2 * i + h, h)
        for n in range(NT - 4, NT):
            one(n, n % 2)

    def within(n, ahead):
        return not isinstance(n, int) or 0 <= n + ahead < NT

    @block.sync
    def _(sp):
        sp.dma_start(nw[:, :], A["L0_ffn_norm_weight"].partition_broadcast(P)).then_inc(nw_in, 16)

    @block.tensor
    def _(pe):
        def turn(n, h):
            pe.wait_ge(xq_ready, n + 3)
            pe.wait_ge(xqT_ready, n + 2)
            for c in range(DC):
                last = pe.transpose(x_ps[:, c, :], xq[h][:, c * P:(c + 1) * P], identb[:, :])
            last.then_inc(x_turned, 1)

        def up(n, h, j):
            f0, fn = CH[j]
            k = (h + j) % 2 if NCH % 2 else j % 2
            if j == 0:
                pe.wait_ge(xqT_ready, n + 3)
            pe.wait_ge(hid_ready, NCH * n + j + 1)
            for c in range(DC):
                pe.matmul(g_ps[k][:, 0:fn], lhsT=xqT[h][:, c, :], rhs=wgu_q[:, c, f0:f0 + fn],
                          start=(c == 0), stop=(c == DC - 1))
            for c in range(DC):
                last = pe.matmul(u_ps[k][:, 0:fn], lhsT=xqT[h][:, c, :], rhs=wgu_q[:, c, F + f0:F + f0 + fn],
                                 start=(c == 0), stop=(c == DC - 1))
            last.then_inc(gu_ready, 1)

        def turn_hidden(n, h):
            pe.wait_ge(hq_ready, n + 3)
            pe.wait_ge(hqT_ready, n + 2)
            for f in range(FC):
                last = pe.transpose(h_ps[f // 8][:, f % 8, :], hq[h][:, f * P:(f + 1) * P], identb[:, :])
            last.then_inc(h_turned, 1)

        def down(n, h):
            pe.wait_ge(hqT_ready, n + 3)
            pe.wait_ge(x_ready, n + 2)
            for f in range(FC):
                last = pe.matmul(o_ps[:, :], lhsT=hqT[h][:, f, :], rhs=wd_q[:, f, :], start=(f == 0), stop=(f == FC - 1))
            last.then_inc(o_ready, 1)

        def one(n, h):
            turn_hidden(n, h)
            for j in range(NCH):
                if within(n, 2):
                    up(n + 2, h, j)
            if within(n, 3):
                turn(n + 3, 1 - h)
            down(n, h)

        turn(0, 0)
        turn(1, 1)
        for j in range(NCH):
            up(0, 0, j)
        turn(2, 0)
        for j in range(NCH):
            up(1, 1, j)
        steps(pe, one)

    @block.scalar
    def _(act):
        for n in range(2):
            act.wait_ge(asked, n + 1)
            act.activation(root[:, :], var[:, :], ACT.Sqrt).then_inc(rooted, 1)

        def round_tokens(n, h):
            act.wait_ge(xm_ready, n + 3)
            act.wait_ge(x_turned, n + 1)
            act.activation(xq[h][:, :], xn[h][:, :], ACT.Identity, bias=magic[:, 1:2]).then_inc(xq_ready, 1)

        def turned(n, h):
            act.wait_ge(x_turned, n + 3)
            act.wait_ge(gu_ready, NCH * (n - 2) + NCH + 2 if not isinstance(n, int) or n >= 2 else 2)
            act.activation(xqT[h][:, :, :], x_ps[:, :, :], ACT.Copy).then_inc(xqT_ready, 1)

        def up(n, h, j):
            fn = CH[j][1]
            k = (h + j) % 2 if NCH % 2 else j % 2
            act.wait_ge(gu_ready, NCH * n + j + 3)
            act.activation(rl[k][:, 0:fn], g_ps[k][:, 0:fn], ACT.Relu).then_inc(rl_ready, 1)
            act.wait_ge(rl_ready, NCH * n + j + 3)
            act.activation(rl[k][:, 0:fn], rl[k][:, 0:fn], ACT.Square).then_inc(sq_ready, 1)

        def hidden_turned(n, h):
            act.wait_ge(h_turned, n + 3)
            act.wait_ge(o_ready, n + 1)
            act.activation(hqT[h][:, 0:8, :], h_ps[0][:, :, :], ACT.Copy)
            act.activation(hqT[h][:, 8:FC, :], h_ps[1][:, 0:FC - 8, :], ACT.Copy).then_inc(hqT_ready, 1)

        def one(n, h):
            hidden_turned(n, h)
            for j in range(NCH):
                if within(n, 2):
                    up(n + 2, h, j)
                if j == 1 and within(n, 3):
                    round_tokens(n + 3, 1 - h)
            if within(n, 3):
                turned(n + 3, 1 - h)

        for n in range(2):
            round_tokens(n, n)
            turned(n, n)
        for j in range(NCH):
            up(0, 0, j)
        round_tokens(2, 0)
        turned(2, 0)
        for j in range(NCH):
            up(1, 1, j)
        steps(act, one)

    @block.gpsimd
    def _(pool):
        with pool.Fori(0, NT // 2) as i:
            for h in range(2):
                n = 2 * i + h
                pool.wait_ge(hk_ready, n + 3)
                pool.wait_ge(h_turned, n + 1)
                pool.tensor_tensor(hq[h][:, :], hid[h][:, :], magic[:, 1:2].to_broadcast([P, F]), ALU.add).then_inc(hq_ready, 1)

    @block.vector
    def _(dve):
        n = row_stats(dve, stats, m[:, :], var[:, :], w1[:, :], w2[:, :], step, 0)
        dve.wait_ge(step, n)
        dve.tensor_scalar(w2[:, :], var[:, :], 1.0, None, ALU.mult).then_inc(step, 1)
        dve.wait_ge(step, n + 1)
        dve.tensor_scalar(var[:, :], var[:, :], LN_EPS, None, ALU.add).then_inc(step, 1)
        n = rsqrt(dve, asked, rooted, 1, r1[:, :], var[:, :], root[:, :], w1[:, :], step, n + 2)
        dve.wait_ge(step, n)
        dve.tensor_tensor(w2[:, :], w2[:, :], r1[:, :], ALU.mult).then_inc(step, 1)
        dve.wait_ge(step, n + 1)
        dve.tensor_tensor(w2[:, :], w2[:, :], r1[:, :], ALU.mult).then_inc(step, 1)
        dve.wait_ge(step, n + 2)
        dve.tensor_scalar(var[:, :], w2[:, :], LN_EPS, None, ALU.add).then_inc(step, 1)
        n = rsqrt(dve, asked, rooted, 2, r2[:, :], var[:, :], root[:, :], w1[:, :], step, n + 3)
        dve.wait_ge(step, n)
        dve.tensor_tensor(r2[:, :], r2[:, :], r1[:, :], ALU.mult).then_inc(step, 1)
        dve.tensor_scalar(unit[:, 2:3], unit[:, 1:2], tg[:, gate:gate + 1], None, ALU.mult).then_inc(step, 1)
        dve.wait_ge(step, n + 2)
        dve.wait_ge(nw_in, 16)

        def at(a, n, k=None):
            return a[:, bass.ds(n, 1)] if k is None else a[:, bass.ds(n, 1), k]

        def front(n, h):
            dve.wait_ge(xq_ready, n + 1)
            dve.scalar_tensor_tensor(xn[h][:, :], X[:, n, :], at(m, n), nw[:, :], ALU.subtract, ALU.mult).then_inc(xn_ready, 1)
            dve.wait_ge(xn_ready, n + 3)
            dve.tensor_reduce(at(s, n, 0), xn[h][:, :], AX.X, ALU.max, apply_absolute_value=True).then_inc(am_ready, 1)

        def scale(n, h):
            dve.wait_ge(am_ready, n + 3)
            dve.tensor_scalar(at(s, n, 0), at(s, n, 0), at(r2, n), 1e-5, ALU.mult, ALU.max).then_inc(ac_ready, 1)
            dve.wait_ge(ac_ready, n + 3)
            dve.reciprocal(at(s, n, 1), at(s, n, 0)).then_inc(ar_ready, 1)
            dve.tensor_scalar(at(s, n, 2), at(s, n, 0), 1.0 / 127.0, unit[:, 0:1], ALU.mult, ALU.mult)
            dve.wait_ge(ar_ready, n + 3)
            dve.tensor_scalar(at(s, n, 1), at(s, n, 1), 127.0, at(r2, n), ALU.mult, ALU.mult).then_inc(as_ready, 1)
            dve.wait_ge(as_ready, n + 3)
            dve.tensor_scalar(xn[h][:, :], xn[h][:, :], at(s, n, 1), MAGIC, ALU.mult, ALU.add).then_inc(xm_ready, 1)

        def hidden(n, h, j):
            f0, fn = CH[j]
            k = (h + j) % 2 if NCH % 2 else j % 2
            dve.wait_ge(sq_ready, NCH * n + j + 3)
            if j == 0:
                dve.wait_ge(hq_ready, n + 1)
            dve.tensor_tensor(hid[h][:, f0:f0 + fn], rl[k][:, 0:fn], u_ps[k][:, 0:fn], ALU.mult).then_inc(hid_ready, 1)

        def quantise(n, h):
            dve.wait_ge(hid_ready, NCH * n + NCH + 2)
            dve.tensor_reduce(at(s, n, 3), hid[h][:, :], AX.X, ALU.max, apply_absolute_value=True)
            dve.tensor_scalar(at(s, n, 4), at(s, n, 2), at(s, n, 2), at(s, n, 2), ALU.mult, ALU.mult).then_inc(hm_ready, 1)
            dve.wait_ge(hm_ready, n + 3)
            dve.tensor_scalar(at(s, n, 5), at(s, n, 3), at(s, n, 4), 1e-5, ALU.mult, ALU.max).then_inc(hc_ready, 1)
            dve.wait_ge(hc_ready, n + 3)
            dve.reciprocal(at(s, n, 6), at(s, n, 5)).then_inc(hr_ready, 1)
            dve.tensor_scalar(at(s, n, 7), at(s, n, 5), 1.0 / 127.0, unit[:, 2:3], ALU.mult, ALU.mult)
            dve.wait_ge(hr_ready, n + 3)
            dve.tensor_scalar(at(s, n, 6), at(s, n, 6), 127.0, at(s, n, 4), ALU.mult, ALU.mult).then_inc(hs_ready, 1)
            dve.wait_ge(hs_ready, n + 3)
            dve.tensor_scalar(hid[h][:, :], hid[h][:, :], at(s, n, 6), MAGIC, ALU.mult, ALU.add).then_inc(hk_ready, 1)

        def out(n, h):
            dve.wait_ge(o_ready, n + 3)
            dve.scalar_tensor_tensor(X[:, n, :], o_ps[:, :], at(s, n, 7), X[:, n, :], ALU.mult, ALU.add).then_inc(x_ready, 1)

        def measure(n, h):
            dve.wait_ge(x_ready, n + 3)
            dve.bn_stats(stats[:, n, :], X[:, n, :]).then_inc(st_ready, 1)

        def one(n, h):
            if within(n, 3):
                front(n + 3, 1 - h)
            if within(n, 2):
                hidden(n + 2, h, 0)
            if within(n, 3):
                scale(n + 3, 1 - h)
            if within(n, -1):
                out(n - 1, 1 - h)
            for j in range(1, NCH):
                if within(n, 2):
                    hidden(n + 2, h, j)
                if j == 1 and within(n, -1):
                    measure(n - 1, 1 - h)
            if within(n, 2):
                quantise(n + 2, h)

        for n in range(2):
            front(n, n)
            scale(n, n)
        for n in range(2):
            for j in range(NCH):
                hidden(n, n, j)
                if n == 0 and j == 0:
                    front(2, 0)
                    scale(2, 0)
            quantise(n, n)
        steps(dve, one)
        out(NT - 1, 1)
        measure(NT - 1, 1)

    ph.end()


def linear_attention_phase(nc, R, A, KV, gate):
    ph = Phase(nc, "L1x")
    X, ident, tg, stats = R["X"], R["ident"], R["tg"], R["stats"]
    NP = B // 2
    EPS = 1e-6
    Wq, Wg, Wo = (ph.sb(n, [P, DC, D]) for n in ("Wq", "Wg", "Wo"))
    bg, eps = ph.sb("bg", [P, DC]), ph.sb("eps", [P, 1])
    m, var, rstd, root, w1, w2 = (ph.sb(n, [P, NT]) for n in ("m", "var", "rstd", "root", "w1", "w2"))

    def two(n, shape, dt=F32):
        return [ph.sb(f"{n}{h}", shape, dt) for h in range(2)]

    xn, xT, kv = two("xn", [P, TB, D]), two("xT", [P, DC, T]), two("kv", [P, DC, 2, P])
    e, q, sg, dn, ag = two("e", [P, DC, T]), two("q", [P, DC, T]), two("sg", [P, DC, T]), two("dn", [P, DC, T]), two("ag", [P, DC, T])
    t_ps = [ph.ps(f"t_ps{j}", [P, DC, P]) for j in range(TB)]
    q_ps, g_ps, n_ps = (ph.ps(n, [P, DC, T]) for n in ("q_ps", "g_ps", "n_ps"))
    w_in, step, asked, rooted = ph.sem("w_in"), ph.sem("step"), ph.sem("asked"), ph.sem("rooted")
    xn_ready, x_turned, xT_ready, kv_ready = (ph.pair_sem(n) for n in ("xn", "x_turned", "xT", "kv"))
    qp_ready, gp_ready, r_ready, e_ready, q_ready, sg_ready = (ph.pair_sem(n) for n in ("qp", "gp", "r", "e", "q", "sg"))
    nd_ready, dn_ready, ng_ready, rd_ready, ag_ready = (ph.pair_sem(n) for n in ("nd", "dn", "ng", "rd", "ag"))
    o_ready, x_ready, st_ready = (ph.pair_sem(n) for n in ("o", "x", "st"))
    block = ph.start()

    @block.sync
    def _(sp):
        for w, n in ((Wq, "L1_xattn_WqT"), (Wg, "L1_xattn_WgT"), (Wo, "L1_xattn_WoT")):
            sp.dma_start(w[:, :, :], A[n].rearrange("(c p) n -> p c n", p=P)).then_inc(w_in, 16)
        sp.dma_start(bg[:, :], A["L1_xattn_bg"].rearrange("(c p) -> p c", p=P), allow_slow_non_contiguous=True).then_inc(w_in, 16)

    @block.gpsimd
    def _(pool):
        with pool.Fori(0, NP) as i:
            for h in range(2):
                pool.wait_ge(nd_ready, before(i, h))
                pool.tensor_copy(kv[h][:, :, :, :].rearrange("p g a n -> p g (a n)"),
                                 KV[:, bass.ds((2 * i + h) * DC, DC), :]).then_inc(kv_ready, 1)

    @block.tensor
    def _(pe):
        def turn(i, h):
            pe.wait_ge(xn_ready, here(i, h))
            for j in range(TB):
                for c in range(DC):
                    last = pe.transpose(t_ps[j][:, c, :], xn[h][:, j, c * P:(c + 1) * P], ident[:, :])
            last.then_inc(x_turned, 1)

        def project(i, h):
            pe.wait_ge(xT_ready, here(i, h))
            pe.wait_ge(dn_ready, here(i, h) - 1)
            for o in range(DC):
                for c in range(DC):
                    last = pe.matmul(q_ps[:, o, :], lhsT=Wq[:, c, o * P:(o + 1) * P], rhs=xT[h][:, c, :],
                                     start=(c == 0), stop=(c == DC - 1))
            last.then_inc(qp_ready, 1)
            pe.wait_ge(sg_ready, here(i, h) - 1)
            for o in range(DC):
                for c in range(DC):
                    last = pe.matmul(g_ps[:, o, :], lhsT=Wg[:, c, o * P:(o + 1) * P], rhs=xT[h][:, c, :],
                                     start=(c == 0), stop=(c == DC - 1))
            last.then_inc(gp_ready, 1)

        def attend(i, h):
            pe.wait_ge(q_ready, here(i, h))
            pe.wait_ge(kv_ready, here(i, h))
            pe.wait_ge(ng_ready, here(i, h) - 1)
            for g in range(DC):
                pe.matmul(q_ps[:, g, :], lhsT=kv[h][:, g, 1, :], rhs=q[h][:, g, :], start=True, stop=True)
            for g in range(DC):
                last = pe.matmul(n_ps[:, g, :], lhsT=kv[h][:, g, 0, :], rhs=q[h][:, g, :], start=True, stop=True)
            last.then_inc(nd_ready, 1)

        def out(i, h):
            pe.wait_ge(ag_ready, here(i, h))
            for j in range(TB):
                for c in range(DC):
                    last = pe.matmul(t_ps[j][:, :, :], lhsT=ag[h][:, c, j * P:(j + 1) * P], rhs=Wo[:, c, :],
                                     start=(c == 0), stop=(c == DC - 1))
            last.then_inc(o_ready, 1)

        def unit(now, prev, nxt):
            project(*now)
            if nxt:
                if prev:
                    pe.wait_ge(x_ready, here(*prev) - 1)
                turn(*nxt)
            attend(*now)
            if prev:
                if nxt:
                    pe.wait_ge(xT_ready, here(*nxt))
                out(*prev)

        pe.wait_ge(w_in, 64)
        turn(0, 0)
        unit((0, 0), None, (0, 1))
        with pe.Fori(0, NP - 1) as i:
            unit((i, 1), (i, 0), (i + 1, 0))
            unit((i + 1, 0), (i, 1), (i + 1, 1))
        unit((NP - 1, 1), (NP - 1, 0), None)
        pe.wait_ge(x_ready, here(NP - 1, 0))
        out(NP - 1, 1)

    @block.scalar
    def _(act):
        def turned(i, h):
            act.wait_ge(x_turned, here(i, h))
            act.wait_ge(gp_ready, before(i, h))
            for j in range(TB):
                last = act.activation(xT[h][:, :, j * P:(j + 1) * P], t_ps[j][:, :, :], ACT.Copy)
            last.then_inc(xT_ready, 1)

        def unit(now, nxt):
            i, h = now
            act.wait_ge(qp_ready, here(i, h))
            act.wait_ge(q_ready, before(i, h))
            act.activation(e[h][:, :, :], q_ps[:, :, :], ACT.Relu, scale=-1.0).then_inc(r_ready, 1)
            act.wait_ge(r_ready, here(i, h))
            act.activation(e[h][:, :, :], e[h][:, :, :], ACT.Exp, scale=-1.0).then_inc(e_ready, 1)
            act.wait_ge(gp_ready, here(i, h))
            act.wait_ge(ng_ready, before(i, h))
            for c in range(DC):
                last = act.activation(sg[h][:, c, :], g_ps[:, c, :], ACT.Sigmoid, bias=bg[:, c:c + 1])
            last.then_inc(sg_ready, 1)
            if nxt:
                turned(*nxt)
            act.wait_ge(nd_ready, here(i, h))
            act.wait_ge(ag_ready, before(i, h))
            act.activation(dn[h][:, :, :], q_ps[:, :, :], ACT.Identity, bias=eps[:, 0:1]).then_inc(dn_ready, 1)

        act.wait_ge(asked, 1)
        act.activation(root[:, :], var[:, :], ACT.Sqrt).then_inc(rooted, 1)
        act.wait_ge(w_in, 64)
        act.wait_ge(step, 1)
        turned(0, 0)
        unit((0, 0), (0, 1))
        with act.Fori(0, NP - 1) as i:
            unit((i, 1), (i + 1, 0))
            unit((i + 1, 0), (i + 1, 1))
        unit((NP - 1, 1), None)

    @block.vector
    def _(dve):
        dve.memset(eps[:, :], EPS).then_inc(step, 1)
        n = row_stats(dve, stats, m[:, :], var[:, :], w1[:, :], w2[:, :], step, 1)
        dve.wait_ge(step, n)
        dve.tensor_scalar(var[:, :], var[:, :], LN_EPS, None, ALU.add).then_inc(step, 1)
        n = rsqrt(dve, asked, rooted, 1, rstd[:, :], var[:, :], root[:, :], w1[:, :], step, n + 1)
        dve.wait_ge(step, n)

        def normalise(i, h):
            dve.wait_ge(x_turned, before(i, h))
            for j in range(TB):
                t = (2 * i + h) * TB + j
                last = dve.tensor_scalar(xn[h][:, j, :], X[:, t, :], m[:, bass.ds(t, 1)], rstd[:, bass.ds(t, 1)],
                                         ALU.subtract, ALU.mult)
            last.then_inc(xn_ready, 1)

        def out(i, h):
            dve.wait_ge(o_ready, here(i, h))
            for j in range(TB):
                t = (2 * i + h) * TB + j
                last = dve.scalar_tensor_tensor(X[:, t, :], t_ps[j][:, :, :].rearrange("p c n -> p (c n)"),
                                                tg[:, gate:gate + 1], X[:, t, :], ALU.mult, ALU.add)
            last.then_inc(x_ready, 1)
            dve.wait_ge(x_ready, here(i, h))
            for j in range(TB):
                t = (2 * i + h) * TB + j
                last = dve.bn_stats(stats[:, t, :], X[:, t, :])
            last.then_inc(st_ready, 1)

        def unit(now, prev, nxt):
            i, h = now
            if nxt:
                normalise(*nxt)
            dve.wait_ge(e_ready, here(i, h))
            dve.wait_ge(nd_ready, before(i, h))
            dve.scalar_tensor_tensor(q[h][:, :, :], q_ps[:, :, :], 0.0, e[h][:, :, :], ALU.max, ALU.add).then_inc(q_ready, 1)
            dve.wait_ge(nd_ready, here(i, h))
            dve.wait_ge(sg_ready, here(i, h))
            dve.wait_ge(o_ready, before(i, h))
            dve.tensor_tensor(ag[h][:, :, :], n_ps[:, :, :], sg[h][:, :, :], ALU.mult).then_inc(ng_ready, 1)
            dve.wait_ge(dn_ready, here(i, h))
            dve.reciprocal(dn[h][:, :, :], dn[h][:, :, :]).then_inc(rd_ready, 1)
            dve.wait_ge(rd_ready, here(i, h))
            dve.tensor_tensor(ag[h][:, :, :], ag[h][:, :, :], dn[h][:, :, :], ALU.mult).then_inc(ag_ready, 1)
            if prev:
                out(*prev)

        normalise(0, 0)
        unit((0, 0), None, (0, 1))
        with dve.Fori(0, NP - 1) as i:
            unit((i, 1), (i, 0), (i + 1, 0))
            unit((i + 1, 0), (i, 1), (i + 1, 1))
        unit((NP - 1, 1), (NP - 1, 0), None)
        out(NP - 1, 1)

    ph.end()


def linker(eng, sem, at=0):
    count = [at]

    def link(ins):
        count[0] += 1
        ins.then_inc(sem, 1)
        eng.wait_ge(sem, count[0])
        return count[0]

    return link


def spline_phase(nc, R, A, gate):
    ph = Phase(nc, "L1f")
    X, ident, ones, tg, stats = R["X"], R["ident"], R["ones"], R["tg"], R["stats"]
    NTL, NCL, SL, GR = 64, 8, 8, 16
    NP = NT // 2
    BIG = 1e30
    TW = 2 * SL * GR + 3
    m, var, v0, r1, r2, root, w1, w2 = (ph.sb(n, [P, NT]) for n in ("m", "var", "v0", "r1", "r2", "root", "w1", "w2"))
    keep, shift = ph.sb("keep", [P, NT]), ph.sb("shift", [P, NT])
    gamma, beta, srow = ph.sb("gamma", [P, D]), ph.sb("beta", [P, D]), ph.sb("srow", [P, D])
    slopes, ss, sb_ = ph.sb("slopes", [P, DC, GR]), ph.sb("ss", [P, 3, DC]), ph.sb("sb", [P, DC, P])
    XF = ph.sb("XF", [P, NT, D])
    sg = [ph.sb(f"sg{h}", [P, D]) for h in range(2)]
    TS, OH, W1 = ph.sb("TS", [P, NT, NTL]), ph.sb("OH", [P, NT, NTL]), ph.sb("W1", [P, NT, NTL])
    CS, KM = ph.sb("CS", [P, NT, NCL]), ph.sb("KM", [P, NT])
    cio, tio, kio = ph.sb("cio", [P, NCL]), ph.sb("tio", [P, NCL, SL]), ph.sb("kio", [P, GR])
    XS, XM, MM = ph.sb("XS", [P, NT, SL]), ph.sb("XM", [P, 2, NT]), ph.sb("MM", [P, 2, NTL])
    TAB, OHT, LUT = ph.sb("TAB", [NTL, TW]), ph.sb("OHT", [NTL, NT, P]), ph.sb("LUT", [P, NT, TW])
    U, GI, Z, DL = (ph.sb(n, [P, NT, SL]) for n in ("U", "GI", "Z", "DL"))
    RG = ph.sb("RG", [P, NT])
    KN, KW = ph.sb("KN", [P, NT * SL, GR]), ph.sb("KW", [P, NT, SL * GR])
    s_ps, mm_ps = ph.ps("s_ps", [P, D]), ph.ps("mm_ps", [NTL, 2, P])
    oh_ps = [ph.ps(f"oh_ps{h}", [NTL, P]) for h in range(2)]
    l_ps = [ph.ps(f"l_ps{h}", [P, TW]) for h in range(2)]
    row_in, sl_in, tab_in, io_made = ph.sem("row_in"), ph.sem("sl_in"), ph.sem("tab_in"), ph.sem("io_made")
    step, chain, asked, rooted = ph.sem("step"), ph.sem("chain"), ph.sem("asked"), ph.sem("rooted")
    sgn_made, s_spread = ph.sem("sgn_made"), ph.sem("s_spread")
    xf_ready, xg_ready, xb_ready, sg_ready, sp_ready, ts_ready, gone = (ph.pair_sem(n) for n in ("xf", "xg", "xb", "sg", "sp", "ts", "gone"))
    xm_ready, xs_ready = ph.pair_sem("xm"), ph.pair_sem("xs")
    oh_made, oh_turned, oht_ready = ph.sem("oh_made"), ph.pair_sem("oh_turned"), ph.pair_sem("oht")
    mm_made, mm_turned, tab_ready = ph.sem("mm_made"), ph.sem("mm_turned"), ph.sem("tab_ready")
    l_ready, lut_ready, dl_made = ph.pair_sem("l"), ph.pair_sem("lut"), ph.sem("dl_made")
    put_ready, x_ready, st_ready = ph.pair_sem("put"), ph.pair_sem("x"), ph.pair_sem("st")
    block = ph.start()

    @block.sync
    def _(sp):
        sp.dma_start(slopes[:, :, :], A["L1_ffn_spline_slopes"].rearrange("a b g -> (a b) g").rearrange("(c p) g -> p c g", p=P)).then_inc(sl_in, 16)
        sp.dma_start(gamma[:, :], A["L1_ffn_ln_gamma"].partition_broadcast(P)).then_inc(row_in, 16)
        sp.dma_start(beta[:, :], A["L1_ffn_ln_beta"].partition_broadcast(P)).then_inc(row_in, 16)
        sp.dma_start(TAB[:, 0:SL * GR], A["L1_ffn_spline_bases"].rearrange("a b g -> a (b g)")).then_inc(tab_in, 16)
        sp.dma_start(TAB[:, SL * GR:2 * SL * GR], A["L1_ffn_spline_slopes"].rearrange("a b g -> a (b g)")).then_inc(tab_in, 16)
        sp.dma_start(TAB[:, TW - 1:TW], A["L1_ffn_output_scale"].unsqueeze(1)).then_inc(tab_in, 16)

    @block.gpsimd
    def _(pool):
        pool.iota(cio[:, :], pattern=[[-1, NCL]], base=0, channel_multiplier=0, allow_small_or_imprecise_dtypes=True).then_inc(io_made, 1)
        pool.iota(tio[:, :, :], pattern=[[0, NCL], [-1, SL]], base=0, channel_multiplier=0, allow_small_or_imprecise_dtypes=True).then_inc(io_made, 1)
        pool.iota(kio[:, :], pattern=[[1, GR]], base=0, channel_multiplier=0, allow_small_or_imprecise_dtypes=True).then_inc(io_made, 1)
        pool.wait_ge(dl_made, 1)
        with pool.Fori(0, NP) as i:
            for h in range(2):
                pool.wait_ge(x_ready, before(i, h))
                pool.tensor_tensor(sg[h][:, :].rearrange("p (a b) -> p a b", b=SL),
                                   OH[:, bass.ds(2 * i + h, 1), :].rearrange("p a b -> p (a b)").unsqueeze(2).to_broadcast([P, NTL, SL]),
                                   DL[:, bass.ds(2 * i + h, 1), :].to_broadcast([P, NTL, SL]), ALU.mult).then_inc(put_ready, 1)

    @block.tensor
    def _(pe):
        pe.wait_ge(sgn_made, DC)
        for c in range(DC):
            last = pe.matmul(s_ps[:, c * P:(c + 1) * P], lhsT=sb_[:, c, :], rhs=ident[:, :], start=True, stop=True)
        last.then_inc(s_spread, 1)
        pe.wait_ge(oh_made, 1)
        for t in range(NT):
            i, h = t // 2, t % 2
            pe.wait_ge(oht_ready, before(i, h))
            pe.transpose(oh_ps[h][:, :], OH[:, t, :], ident[:, :]).then_inc(oh_turned, 1)
        pe.wait_ge(mm_made, 1)
        for k in range(2):
            last = pe.transpose(mm_ps[:, k, :], MM[:, k, :], ident[:, :])
        last.then_inc(mm_turned, 1)
        pe.wait_ge(tab_ready, 1)
        for t in range(NT):
            i, h = t // 2, t % 2
            pe.wait_ge(oht_ready, here(i, h))
            pe.wait_ge(lut_ready, before(i, h))
            pe.matmul(l_ps[h][:, :], lhsT=OHT[:, t, :], rhs=TAB[:, :], start=True, stop=True).then_inc(l_ready, 1)

    @block.scalar
    def _(act):
        for n in range(2):
            act.wait_ge(asked, n + 1)
            act.activation(root[:, :], var[:, :], ACT.Sqrt).then_inc(rooted, 1)
        with act.Fori(0, NP) as i:
            for h in range(2):
                act.wait_ge(xb_ready, here(i, h))
                act.wait_ge(ts_ready, before(i, h))
                act.activation(sg[h][:, :], XF[:, 2 * i + h, :], ACT.Sign).then_inc(sg_ready, 1)
        with act.Fori(0, NP) as i:
            for h in range(2):
                act.wait_ge(oh_turned, here(i, h))
                act.activation(OHT[:, 2 * i + h, :], oh_ps[h][:, :], ACT.Copy).then_inc(oht_ready, 1)
        with act.Fori(0, NP) as i:
            for h in range(2):
                act.wait_ge(l_ready, here(i, h))
                act.activation(LUT[:, 2 * i + h, :], l_ps[h][:, :], ACT.Copy).then_inc(lut_ready, 1)

    @block.vector
    def _(dve):
        n = row_stats(dve, stats, m[:, :], v0[:, :], w1[:, :], w2[:, :], step, 0)
        dve.wait_ge(step, n)
        dve.tensor_scalar(var[:, :], v0[:, :], LN_EPS, None, ALU.add).then_inc(step, 1)
        n = rsqrt(dve, asked, rooted, 1, r1[:, :], var[:, :], root[:, :], w1[:, :], step, n + 1)
        dve.wait_ge(step, n)
        link = linker(dve, chain)
        link(dve.tensor_tensor(w2[:, :], v0[:, :], r1[:, :], ALU.mult))
        link(dve.tensor_tensor(w2[:, :], w2[:, :], r1[:, :], ALU.mult))
        link(dve.tensor_scalar(var[:, :], w2[:, :], LN_EPS, None, ALU.add))
        n = rsqrt(dve, asked, rooted, 2, r2[:, :], var[:, :], root[:, :], w1[:, :], step, n)
        dve.wait_ge(step, n)
        link(dve.tensor_tensor(r2[:, :], r2[:, :], r1[:, :], ALU.mult))
        link(dve.tensor_scalar(keep[:, :], r1[:, :], tg[:, gate:gate + 1], 1.0, ALU.mult, ALU.add))
        link(dve.tensor_tensor(shift[:, :], m[:, :], r1[:, :], ALU.mult))
        link(dve.tensor_scalar(shift[:, :], shift[:, :], tg[:, gate:gate + 1], -1.0, ALU.mult, ALU.mult))
        dve.wait_ge(sl_in, 16)
        link(dve.tensor_reduce(ss[:, 0, :], slopes[:, :, :], AX.X, ALU.add))
        link(dve.tensor_scalar(ss[:, 1, :], ss[:, 0, :], 0.0, None, ALU.is_gt))
        link(dve.tensor_scalar(ss[:, 2, :], ss[:, 0, :], 0.0, None, ALU.is_lt))
        link(dve.tensor_tensor(ss[:, 0, :], ss[:, 1, :], ss[:, 2, :], ALU.subtract))
        for c in range(DC):
            dve.tensor_scalar(sb_[:, c, :], ones[:, :], ss[:, 0, c:c + 1], None, ALU.mult).then_inc(sgn_made, 1)
        dve.wait_ge(s_spread, 1)
        link(dve.tensor_copy(srow[:, :], s_ps[:, :]))
        dve.wait_ge(row_in, 32)
        with dve.Fori(0, NP) as i:
            for h in range(2):
                t = 2 * i + h
                dve.tensor_scalar(XF[:, t, :], X[:, t, :], m[:, bass.ds(t, 1)], r2[:, bass.ds(t, 1)],
                                  ALU.subtract, ALU.mult).then_inc(xf_ready, 1)
            for h in range(2):
                t = 2 * i + h
                dve.wait_ge(xf_ready, here(i, h))
                dve.tensor_tensor(XF[:, t, :], XF[:, t, :], gamma[:, :], ALU.mult).then_inc(xg_ready, 1)
            for h in range(2):
                t = 2 * i + h
                dve.wait_ge(xg_ready, here(i, h))
                dve.tensor_tensor(XF[:, t, :], XF[:, t, :], beta[:, :], ALU.add).then_inc(xb_ready, 1)
            for h in range(2):
                t = 2 * i + h
                dve.tensor_scalar(X[:, t, :], X[:, t, :], keep[:, bass.ds(t, 1)], shift[:, bass.ds(t, 1)],
                                  ALU.mult, ALU.add).then_inc(gone, 1)
            for h in range(2):
                dve.wait_ge(sg_ready, here(i, h))
                dve.tensor_tensor(sg[h][:, :], sg[h][:, :], srow[:, :], ALU.mult).then_inc(sp_ready, 1)
            for h in range(2):
                t = 2 * i + h
                dve.wait_ge(sp_ready, here(i, h))
                dve.tensor_reduce(TS[:, t, :], sg[h][:, :].rearrange("p (a b) -> p a b", b=SL), AX.X, ALU.add).then_inc(ts_ready, 1)
        dve.wait_ge(ts_ready, 2 * NP + 2)
        dve.wait_ge(io_made, 3)
        link(dve.tensor_reduce(CS[:, :, :], TS[:, :, :].rearrange("p t (c a) -> p (t c) a", a=SL), AX.X, ALU.add))
        link(dve.scalar_tensor_tensor(CS[:, :, :], CS[:, :, :], 8.0, cio[:, :].unsqueeze(1).to_broadcast([P, NT, NCL]), ALU.mult, ALU.add))
        link(dve.scalar_tensor_tensor(TS[:, :, :], TS[:, :, :], 8.0,
                                      tio[:, :, :].rearrange("p a b -> p (a b)").unsqueeze(1).to_broadcast([P, NT, NTL]), ALU.mult, ALU.add))
        link(dve.scalar_tensor_tensor(TS[:, :, :].rearrange("p t (c a) -> p (t c) a", a=SL),
                                      CS[:, :, :].rearrange("p t c -> p (t c)").unsqueeze(2).to_broadcast([P, NT * NCL, SL]), 256.0,
                                      TS[:, :, :].rearrange("p t (c a) -> p (t c) a", a=SL), ALU.mult, ALU.add))
        link(dve.tensor_reduce(KM[:, :], TS[:, :, :], AX.X, ALU.max))
        dve.tensor_tensor(OH[:, :, :], TS[:, :, :], KM[:, :].unsqueeze(2).to_broadcast([P, NT, NTL]), ALU.is_equal).then_inc(oh_made, 1)
        dve.wait_ge(oh_made, 1)
        with dve.Fori(0, NP) as i:
            for h in range(2):
                t = 2 * i + h
                dve.wait_ge(xs_ready, before(i, h))
                dve.tensor_tensor(sg[h][:, :].rearrange("p (a b) -> p a b", b=SL),
                                  XF[:, bass.ds(t, 1), :].rearrange("p t (a b) -> p (t a) b", b=SL),
                                  OH[:, bass.ds(t, 1), :].rearrange("p a b -> p (a b)").unsqueeze(2).to_broadcast([P, NTL, SL]),
                                  ALU.mult).then_inc(xm_ready, 1)
            for h in range(2):
                dve.wait_ge(xm_ready, here(i, h))
                dve.tensor_reduce(XS[:, 2 * i + h, :], sg[h][:, :].rearrange("p (a b) -> p b a", b=SL), AX.X, ALU.add).then_inc(xs_ready, 1)
        dve.wait_ge(xs_ready, 2 * NP + 2)
        link(dve.tensor_reduce(XM[:, 0, :], XS[:, :, :], AX.X, ALU.max))
        link(dve.tensor_reduce(XM[:, 1, :], XS[:, :, :], AX.X, ALU.min, negate=True))
        link(dve.tensor_scalar(W1[:, :, :], OH[:, :, :], -1.0, BIG, ALU.add, ALU.mult))
        for k in range(2):
            link(dve.tensor_tensor(TS[:, :, :], OH[:, :, :], XM[:, k, :].unsqueeze(2).to_broadcast([P, NT, NTL]), ALU.mult))
            link(dve.tensor_tensor(TS[:, :, :], TS[:, :, :], W1[:, :, :], ALU.add))
            link(dve.tensor_reduce(MM[:, k, :], TS[:, :, :].rearrange("p t a -> p a t"), AX.X, ALU.max))
        dve.sem_inc(mm_made, 1)
        dve.wait_ge(mm_turned, 1)
        dve.wait_ge(tab_in, 48)
        dve.tensor_reduce(TAB[:, TW - 3:TW - 1], mm_ps[:, :, :], AX.X, ALU.max).then_inc(tab_ready, 1)
        dve.wait_ge(lut_ready, 2 * NP + 2)
        link(dve.tensor_tensor(RG[:, :], LUT[:, :, TW - 3], LUT[:, :, TW - 2], ALU.add))
        link(dve.tensor_scalar(RG[:, :], RG[:, :], 1e-8, None, ALU.add))
        link(dve.reciprocal(RG[:, :], RG[:, :]))
        link(dve.tensor_tensor(U[:, :, :], XS[:, :, :], LUT[:, :, TW - 2:TW - 1].to_broadcast([P, NT, SL]), ALU.add))
        link(dve.tensor_tensor(U[:, :, :], U[:, :, :], RG[:, :].unsqueeze(2).to_broadcast([P, NT, SL]), ALU.mult))
        link(dve.tensor_scalar(U[:, :, :], U[:, :, :], 0.0, 1.0 - 1e-6, ALU.max, ALU.min))
        link(dve.tensor_scalar(U[:, :, :], U[:, :, :], float(GR), None, ALU.mult))
        link(dve.tensor_scalar(GI[:, :, :], U[:, :, :], MAGIC, -MAGIC, ALU.add, ALU.add))
        link(dve.tensor_tensor(Z[:, :, :], GI[:, :, :], U[:, :, :], ALU.is_gt))
        link(dve.tensor_tensor(GI[:, :, :], GI[:, :, :], Z[:, :, :], ALU.subtract))
        link(dve.tensor_tensor(U[:, :, :], U[:, :, :], GI[:, :, :], ALU.subtract))
        link(dve.tensor_tensor(KN[:, :, :], kio[:, :].unsqueeze(1).to_broadcast([P, NT * SL, GR]),
                               GI[:, :, :].rearrange("p t j -> p (t j)").unsqueeze(2).to_broadcast([P, NT * SL, GR]), ALU.is_equal))
        for k, dst in ((0, Z), (1, DL)):
            link(dve.tensor_tensor(KW[:, :, :], KN[:, :, :].rearrange("p (t j) g -> p t (j g)", j=SL),
                                   LUT[:, :, k * SL * GR:(k + 1) * SL * GR], ALU.mult))
            link(dve.tensor_reduce(dst[:, :, :].rearrange("p t j -> p (t j)"),
                                   KW[:, :, :].rearrange("p t (j g) -> p (t j) g", g=GR), AX.X, ALU.add))
        link(dve.tensor_tensor(DL[:, :, :], DL[:, :, :], U[:, :, :], ALU.mult))
        link(dve.tensor_tensor(DL[:, :, :], DL[:, :, :], Z[:, :, :], ALU.add))
        link(dve.tensor_tensor(DL[:, :, :], DL[:, :, :], LUT[:, :, TW - 1:TW].to_broadcast([P, NT, SL]), ALU.mult))
        dve.tensor_scalar(DL[:, :, :], DL[:, :, :], tg[:, gate:gate + 1], None, ALU.mult).then_inc(dl_made, 1)
        with dve.Fori(0, NP) as i:
            for h in range(2):
                t = 2 * i + h
                dve.wait_ge(put_ready, here(i, h))
                dve.tensor_tensor(X[:, t, :], X[:, t, :], sg[h][:, :], ALU.add).then_inc(x_ready, 1)
            for h in range(2):
                t = 2 * i + h
                dve.wait_ge(x_ready, here(i, h))
                dve.bn_stats(stats[:, t, :], X[:, t, :]).then_inc(st_ready, 1)

    ph.end()


def experts_phase(nc, R, A, gate):
    ph = Phase(nc, "L2f")
    X, ident, tg, stats = R["X"], R["ident"], R["tg"], R["stats"]
    E, I = 8, 16
    EI = E * I
    NP = NT // 2
    m, var, rstd, root, w1, w2 = (ph.sb(n, [P, NT]) for n in ("m", "var", "rstd", "root", "w1", "w2"))
    w3 = ph.sb("w3", [P, 1])
    W, up = ph.sb("W", [P, DC, EI + E]), ph.sb("up", [P, D])
    H, LG = ph.sb("H", [P, NT, EI]), ph.sb("LG", [P, NT, E])
    MX, WT, FI, K1, MK, RM = ph.sb("MX", [P, NT]), ph.sb("WT", [P, NT, E]), ph.sb("FI", [P, E]), ph.sb("K1", [P, NT, E]), ph.sb("MK", [P, NT, E]), ph.sb("RM", [P, NT, E])

    def two(n, shape):
        return [ph.sb(f"{n}{h}", shape) for h in range(2)]

    xn, xT, a, aT = two("xn", [P, D]), two("xT", [P, DC, P]), two("a", [P, EI]), two("aT", [P, P])
    t_ps = [ph.ps(f"t_ps{h}", [P, DC, P]) for h in range(2)]
    h_ps = [ph.ps(f"h_ps{h}", [P, EI + E]) for h in range(2)]
    a_ps = [ph.ps(f"a_ps{h}", [P, P]) for h in range(2)]
    o_ps = [ph.ps(f"o_ps{h}", [P, D]) for h in range(2)]
    w_in, step, chain, asked, rooted, iota_made = (ph.sem(n) for n in ("w_in", "step", "chain", "asked", "rooted", "iota"))
    xn_ready, turned, xT_ready, h_ready, H_ready, LG_ready = (ph.pair_sem(n) for n in ("xn", "turned", "xT", "h", "H", "LG"))
    ex_asked, ex_ready = ph.sem("ex_asked"), ph.sem("ex")
    a_ready, a_turned, aT_ready, o_ready, x_ready, st_ready = (ph.pair_sem(n) for n in ("a", "a_turned", "aT", "o", "x", "st"))
    block = ph.start()

    @block.sync
    def _(sp):
        sp.dma_start(W[:, :, 0:EI], A["L2_ffn_downT"].rearrange("(c p) n -> p c n", p=P)).then_inc(w_in, 16)
        sp.dma_start(W[:, :, EI:EI + E], A["L2_ffn_routerT"].rearrange("(c p) n -> p c n", p=P)).then_inc(w_in, 16)
        sp.dma_start(up[:, :], A["L2_ffn_up"]).then_inc(w_in, 16)

    @block.gpsimd
    def _(pool):
        pool.iota(FI[:, :], pattern=[[-1, E]], base=E, channel_multiplier=0, allow_small_or_imprecise_dtypes=True).then_inc(iota_made, 1)

    @block.tensor
    def _(pe):
        pe.wait_ge(w_in, 48)
        with pe.Fori(0, NP) as i:
            for h in range(2):
                pe.wait_ge(xn_ready, here(i, h))
                pe.wait_ge(xT_ready, before(i, h))
                for c in range(DC):
                    last = pe.transpose(t_ps[h][:, c, :], xn[h][:, c * P:(c + 1) * P], ident[:, :])
                last.then_inc(turned, 1)
            for h in range(2):
                pe.wait_ge(xT_ready, here(i, h))
                pe.wait_ge(H_ready, before(i, h))
                pe.wait_ge(LG_ready, before(i, h))
                for c in range(DC):
                    last = pe.matmul(h_ps[h][:, :], lhsT=xT[h][:, c, :], rhs=W[:, c, :], start=(c == 0), stop=(c == DC - 1))
                last.then_inc(h_ready, 1)
        with pe.Fori(0, NP) as i:
            for h in range(2):
                pe.wait_ge(a_ready, here(i, h))
                pe.wait_ge(aT_ready, before(i, h))
                pe.transpose(a_ps[h][:, :], a[h][:, :], ident[:, :]).then_inc(a_turned, 1)
            for h in range(2):
                pe.wait_ge(aT_ready, here(i, h))
                pe.wait_ge(x_ready, before(i, h))
                pe.matmul(o_ps[h][:, :], lhsT=aT[h][:, :], rhs=up[:, :], start=True, stop=True).then_inc(o_ready, 1)

    @block.scalar
    def _(act):
        act.wait_ge(asked, 1)
        act.activation(root[:, :], var[:, :], ACT.Sqrt).then_inc(rooted, 1)
        act.activation(w3[:, :], tg[:, 0:1], ACT.Silu)
        with act.Fori(0, NP) as i:
            for h in range(2):
                act.wait_ge(turned, here(i, h))
                act.wait_ge(h_ready, before(i, h))
                act.activation(xT[h][:, :, :], t_ps[h][:, :, :], ACT.Copy).then_inc(xT_ready, 1)
            for h in range(2):
                act.wait_ge(h_ready, here(i, h))
                act.activation(H[:, 2 * i + h, :], h_ps[h][:, 0:EI], ACT.Silu).then_inc(H_ready, 1)
                act.activation(LG[:, 2 * i + h, :], h_ps[h][:, EI:EI + E], ACT.Copy).then_inc(LG_ready, 1)
        act.wait_ge(ex_asked, 1)
        act.activation(LG[:, :, :], LG[:, :, :], ACT.Exp).then_inc(ex_ready, 1)
        with act.Fori(0, NP) as i:
            for h in range(2):
                act.wait_ge(a_turned, here(i, h))
                act.wait_ge(o_ready, before(i, h))
                act.activation(aT[h][:, :], a_ps[h][:, :], ACT.Copy).then_inc(aT_ready, 1)

    @block.vector
    def _(dve):
        n = row_stats(dve, stats, m[:, :], var[:, :], w1[:, :], w2[:, :], step, 0)
        dve.wait_ge(step, n)
        dve.tensor_scalar(var[:, :], var[:, :], LN_EPS, None, ALU.add).then_inc(step, 1)
        n = rsqrt(dve, asked, rooted, 1, rstd[:, :], var[:, :], root[:, :], w1[:, :], step, n + 1)
        dve.wait_ge(step, n)
        with dve.Fori(0, NP) as i:
            for h in range(2):
                t = 2 * i + h
                dve.wait_ge(turned, before(i, h))
                dve.tensor_scalar(xn[h][:, :], X[:, t, :], m[:, bass.ds(t, 1)], rstd[:, bass.ds(t, 1)],
                                  ALU.subtract, ALU.mult).then_inc(xn_ready, 1)
        dve.wait_ge(LG_ready, 2 * NP + 2)
        link = linker(dve, chain)
        link(dve.tensor_reduce(MX[:, :], LG[:, :, :], AX.X, ALU.max))
        dve.tensor_tensor(LG[:, :, :], LG[:, :, :], MX[:, :].unsqueeze(2).to_broadcast([P, NT, E]), ALU.subtract).then_inc(ex_asked, 1)
        dve.wait_ge(ex_ready, 1)
        link(dve.tensor_reduce(MX[:, :], LG[:, :, :], AX.X, ALU.add))
        link(dve.reciprocal(MX[:, :], MX[:, :]))
        link(dve.tensor_tensor(WT[:, :, :], LG[:, :, :], MX[:, :].unsqueeze(2).to_broadcast([P, NT, E]), ALU.mult))
        link(dve.tensor_copy(RM[:, :, :], WT[:, :, :]))
        dve.wait_ge(iota_made, 1)
        for k in range(2):
            link(dve.tensor_reduce(MX[:, :], RM[:, :, :], AX.X, ALU.max))
            link(dve.tensor_tensor(K1[:, :, :], RM[:, :, :], MX[:, :].unsqueeze(2).to_broadcast([P, NT, E]), ALU.is_equal))
            link(dve.tensor_tensor(K1[:, :, :], K1[:, :, :], FI[:, :].unsqueeze(1).to_broadcast([P, NT, E]), ALU.mult))
            link(dve.tensor_reduce(MX[:, :], K1[:, :, :], AX.X, ALU.max))
            link(dve.tensor_tensor(K1[:, :, :], K1[:, :, :], MX[:, :].unsqueeze(2).to_broadcast([P, NT, E]), ALU.is_equal))
            if k == 0:
                link(dve.tensor_copy(MK[:, :, :], K1[:, :, :]))
                link(dve.scalar_tensor_tensor(RM[:, :, :], K1[:, :, :], -2.0, RM[:, :, :], ALU.mult, ALU.add))
            else:
                link(dve.tensor_tensor(MK[:, :, :], MK[:, :, :], K1[:, :, :], ALU.add))
        link(dve.tensor_tensor(WT[:, :, :], WT[:, :, :], MK[:, :, :], ALU.mult))
        dve.wait_ge(H_ready, 2 * NP + 2)
        with dve.Fori(0, NP) as i:
            for h in range(2):
                t = 2 * i + h
                dve.wait_ge(a_turned, before(i, h))
                dve.tensor_tensor(a[h][:, :].rearrange("p (e k) -> p e k", k=I),
                                  H[:, bass.ds(t, 1), :].rearrange("p t (e k) -> p (t e) k", k=I),
                                  WT[:, bass.ds(t, 1), :].rearrange("p a b -> p (a b)").unsqueeze(2).to_broadcast([P, E, I]),
                                  ALU.mult).then_inc(a_ready, 1)
            for h in range(2):
                t = 2 * i + h
                dve.wait_ge(o_ready, here(i, h))
                dve.scalar_tensor_tensor(X[:, t, :], o_ps[h][:, :], tg[:, gate:gate + 1], X[:, t, :], ALU.mult, ALU.add).then_inc(x_ready, 1)
            for h in range(2):
                t = 2 * i + h
                dve.wait_ge(x_ready, here(i, h))
                dve.bn_stats(stats[:, t, :], X[:, t, :]).then_inc(st_ready, 1)

    ph.end()


def decay_phase(nc, R, A, gate, x_dram):
    ph = Phase(nc, "L3x")
    X, ident, ones, tg, stats = R["X"], R["ident"], R["ones"], R["tg"], R["stats"]
    NP = NT // 2
    m, var, rstd, root, w1, w2 = (ph.sb(n, [P, NT]) for n in ("m", "var", "rstd", "root", "w1", "w2"))
    C = ph.sb("C", [P, NT, D])
    Y = ph.sb("Y", [P, NT, D])
    st2 = ph.sb("st2", [P, NT, 6])
    Wi, Wo = ph.sb("Wi", [P, DC, D]), ph.sb("Wo", [P, DC, D])
    K, rr, rt, wc = ph.sb("K", [P, 2]), ph.sb("rr", [P, T]), ph.sb("rt", [P, T]), ph.sb("wc", [P, TB + 1])
    wsel, sel = ph.sb("wsel", [P, NT, B]), ph.sb("sel", [B, B, P])
    gamma, beta, bo, bi = ph.sb("gamma", [P, D]), ph.sb("beta", [P, D]), ph.sb("bo", [B, D]), ph.sb("bi", [P, DC])
    s8, sT, mT, pr, SB = ph.sb("s8", [B, D]), ph.sb("sT", [P, DC, B]), ph.sb("mT", [P, DC, B]), ph.sb("pr", [B, D]), ph.sb("SB", [P, B, D])
    z = [ph.sb(f"z{h}", [P, D]) for h in range(2)]
    s_ps, t_ps, m_ps, p_ps = ph.ps("s_ps", [B, D]), ph.ps("t_ps", [P, DC, B]), ph.ps("m_ps", [P, DC, B]), ph.ps("p_ps", [B, D])
    b_ps = [ph.ps(f"b_ps{h}", [P, D]) for h in range(2)]
    c_in, w_in, v_in, d_in = [ph.sem(f"c_in{k}") for k in range(2)], ph.sem("w_in"), ph.sem("v_in"), ph.sem("d_in")
    step, chain, asked, rooted, kept, sel_made, wsel_made = (ph.sem(n) for n in ("step", "chain", "asked", "rooted", "kept", "sel", "wsel"))
    summed, copied, turned, turned_back, mixed, mixed_back, proj, proj_back = (ph.sem(n) for n in ("summed", "copied", "turned", "turned_back", "mixed", "mixed_back", "proj", "proj_back"))
    spread, SB_ready = ph.pair_sem("spread"), ph.pair_sem("SB")
    y_ready, y_stat, z_ready, xb_ready, x_ready = (ph.pair_sem(n) for n in ("y", "y_stat", "z", "xb", "x"))
    stored = ph.sem("stored")
    row_made = ph.sem("row_made")
    block = ph.start()

    @block.sync
    def _(sp):
        sp.dma_start(K[:, 0:1], A["L3_xattn_decay"].partition_broadcast(P)).then_inc(d_in, 16)
        for k in range(2):
            sp.dma_start(C[:, k * NT // 2:(k + 1) * NT // 2, :],
                         A["ctx"].rearrange("(t p) c -> p t c", p=P)[:, k * NT // 2:(k + 1) * NT // 2, :]).then_inc(c_in[k], 16)
        for w, n in ((Wi, "L3_xattn_W_inT"), (Wo, "L3_xattn_W_outT")):
            sp.dma_start(w[:, :, :], A[n].rearrange("(c p) n -> p c n", p=P)).then_inc(w_in, 16)
        sp.dma_start(gamma[:, :], A["L3_xattn_gamma"].partition_broadcast(P)).then_inc(v_in, 16)
        sp.dma_start(beta[:, :], A["L3_xattn_beta"].partition_broadcast(P)).then_inc(v_in, 16)
        sp.dma_start(bo[:, :], A["L3_xattn_b_out"].partition_broadcast(B)).then_inc(v_in, 16)
        sp.dma_start(bi[:, :], A["L3_xattn_b_in"].rearrange("(c p) -> p c", p=P), allow_slow_non_contiguous=True).then_inc(v_in, 16)
        xd = x_dram.rearrange("(t p) c -> p t c", p=P)
        with sp.Fori(0, NP) as i:
            sp.wait_ge(x_ready, both(i))
            sp.dma_start(xd[:, bass.ds(2 * i, 2), :], X[:, bass.ds(2 * i, 2), :]).then_inc(stored, 16)
        sp.wait_ge(stored, 16 * NP)

    @block.gpsimd
    def _(pool):
        pool.memset(sel[:, :, :], 0.0).then_inc(sel_made, 1)
        pool.wait_ge(sel_made, 1)
        pool.affine_select(out=sel[:, :, :], in_=sel[:, :, :], compare_op=ALU.not_equal, fill=1.0, base=0,
                           pattern=[[-1, B], [0, P]], channel_multiplier=1).then_inc(sel_made, 1)
        pool.wait_ge(row_made, 2)
        with pool.Fori(0, NP) as i:
            for h in range(2):
                pool.wait_ge(y_ready, here(i, h))
                pool.tensor_tensor(X[:, 2 * i + h, :], X[:, 2 * i + h, :], beta[:, :], ALU.add).then_inc(xb_ready, 1)

    @block.tensor
    def _(pe):
        pe.wait_ge(wsel_made, 1)
        for t in range(NT):
            if t % (NT // 2) == 0:
                pe.wait_ge(c_in[t // (NT // 2)], 16)
            last = pe.matmul(s_ps[:, :], lhsT=wsel[:, t, :], rhs=C[:, t, :], start=(t == 0), stop=(t == NT - 1))
        last.then_inc(summed, 1)
        pe.wait_ge(copied, 1)
        for c in range(DC):
            last = pe.transpose(t_ps[:, c, :], s8[:, c * P:(c + 1) * P], ident[0:B, 0:B])
        last.then_inc(turned, 1)
        pe.wait_ge(turned_back, 1)
        pe.wait_ge(w_in, 32)
        for o in range(DC):
            for c in range(DC):
                last = pe.matmul(m_ps[:, o, :], lhsT=Wi[:, c, o * P:(o + 1) * P], rhs=sT[:, c, :], start=(c == 0), stop=(c == DC - 1))
        last.then_inc(mixed, 1)
        pe.wait_ge(mixed_back, 1)
        for c in range(DC):
            last = pe.matmul(p_ps[:, :], lhsT=mT[:, c, :], rhs=Wo[:, c, :], start=(c == 0), stop=(c == DC - 1))
        last.then_inc(proj, 1)
        pe.wait_ge(proj_back, 1)
        pe.wait_ge(sel_made, 2)
        for b in range(B):
            pe.wait_ge(SB_ready, before(b // 2, b % 2))
            pe.matmul(b_ps[b % 2][:, :], lhsT=sel[:, b, :], rhs=pr[:, :], start=True, stop=True).then_inc(spread, 1)

    @block.scalar
    def _(act):
        act.wait_ge(d_in, 16)
        act.activation(K[:, 1:2], K[:, 0:1], ACT.Sigmoid).then_inc(kept, 1)
        for n in range(2):
            act.wait_ge(asked, n + 1)
            act.activation(root[:, :], var[:, :], ACT.Sqrt).then_inc(rooted, 1)
            if n == 0:
                for b in range(B):
                    act.wait_ge(spread, here(b // 2, b % 2))
                    act.activation(SB[:, b, :], b_ps[b % 2][:, :], ACT.Copy).then_inc(SB_ready, 1)

    @block.vector
    def _(dve):
        link = linker(dve, chain)
        dve.wait_ge(kept, 1)
        link(dve.tensor_copy(rt[:, :], ones[:, 0:1].to_broadcast([P, T])))
        link(dve.tensor_tensor_scan(rr[:, :], K[:, 1:2].to_broadcast([P, T]), rt[:, :], 0.0, ALU.mult, ALU.add))
        link(dve.tensor_reduce(wc[:, TB:TB + 1], rr[:, :], AX.X, ALU.add))
        link(dve.tensor_copy(rt[:, :], rr[:, ::-1]))
        for j in range(TB):
            link(dve.tensor_tensor(rr[:, 0:P], rt[:, j * P:(j + 1) * P], ident[:, :], ALU.mult))
            link(dve.tensor_reduce(wc[:, j:j + 1], rr[:, 0:P], AX.X, ALU.add))
        link(dve.tensor_scalar(wc[:, :], wc[:, :], 1.0 / T, None, ALU.mult))
        link(dve.memset(wsel[:, :, :], 0.0))
        for b in range(B):
            last = dve.tensor_copy(wsel[:, TB * b:TB * (b + 1), b], wc[:, 0:TB])
        last.then_inc(wsel_made, 1)
        dve.wait_ge(v_in, 64)
        dve.tensor_scalar(gamma[:, :], gamma[:, :], tg[:, gate:gate + 1], None, ALU.mult).then_inc(row_made, 1)
        dve.tensor_scalar(beta[:, :], beta[:, :], tg[:, gate:gate + 1], None, ALU.mult).then_inc(row_made, 1)
        n = row_stats(dve, stats, m[:, :], var[:, :], w1[:, :], w2[:, :], step, 0)
        dve.wait_ge(step, n)
        dve.tensor_scalar(var[:, :], var[:, :], LN_EPS, None, ALU.add).then_inc(step, 1)
        n = rsqrt(dve, asked, rooted, 1, rstd[:, :], var[:, :], root[:, :], w1[:, :], step, n + 1)
        dve.wait_ge(step, n)
        dve.wait_ge(summed, 1)
        dve.tensor_copy(s8[:, :], s_ps[:, :]).then_inc(copied, 1)
        dve.wait_ge(turned, 1)
        dve.tensor_copy(sT[:, :, :], t_ps[:, :, :]).then_inc(turned_back, 1)
        dve.wait_ge(mixed, 1)
        link(dve.tensor_scalar(bi[:, :], bi[:, :], wc[:, TB:TB + 1], None, ALU.mult))
        dve.tensor_tensor(mT[:, :, :], m_ps[:, :, :], bi[:, :].unsqueeze(2).to_broadcast([P, DC, B]), ALU.add).then_inc(mixed_back, 1)
        dve.wait_ge(proj, 1)
        dve.tensor_tensor(pr[:, :], p_ps[:, :], bo[:, :], ALU.add).then_inc(proj_back, 1)
        with dve.Fori(0, NP) as i:
            for h in range(2):
                t = 2 * i + h
                dve.wait_ge(SB_ready, i + 3)
                dve.scalar_tensor_tensor(Y[:, t, :], X[:, t, :], rstd[:, bass.ds(t, 1)], SB[:, i, :], ALU.mult, ALU.add).then_inc(y_ready, 1)
            for h in range(2):
                t = 2 * i + h
                dve.wait_ge(y_ready, here(i, h))
                dve.bn_stats(st2[:, t, :], Y[:, t, :]).then_inc(y_stat, 1)
        dve.wait_ge(y_stat, 2 * NP + 2)
        n = row_stats(dve, st2, m[:, :], var[:, :], w1[:, :], w2[:, :], step, n)
        dve.wait_ge(step, n)
        dve.tensor_scalar(var[:, :], var[:, :], LN_EPS, None, ALU.add).then_inc(step, 1)
        n = rsqrt(dve, asked, rooted, 2, rstd[:, :], var[:, :], root[:, :], w1[:, :], step, n + 1)
        dve.wait_ge(step, n)
        dve.wait_ge(row_made, 2)
        with dve.Fori(0, NP) as i:
            for h in range(2):
                t = 2 * i + h
                dve.wait_ge(x_ready, before(i, h))
                dve.scalar_tensor_tensor(z[h][:, :], Y[:, t, :], m[:, bass.ds(t, 1)], gamma[:, :], ALU.subtract, ALU.mult).then_inc(z_ready, 1)
            for h in range(2):
                t = 2 * i + h
                dve.wait_ge(z_ready, here(i, h))
                dve.wait_ge(xb_ready, here(i, h))
                dve.scalar_tensor_tensor(X[:, t, :], z[h][:, :], rstd[:, bass.ds(t, 1)], X[:, t, :], ALU.mult, ALU.add).then_inc(x_ready, 1)

    ph.end()


def route_phase(nc, R, A, name, x_dram, xT_dram, first, second):
    ph = Phase(nc, name)
    ident, ones = R["ident"], R["ones"]
    NP = NT // 2
    HD, NK, KB = 4, 128, 8
    S = HD * KB
    E1 = A["L3_ffn_e_down"].shape[0]
    xT = ph.sb("xT", [P, DC, 4, NT * 32])
    X8, stats = ph.sb("X8", [P, NT, D]), ph.sb("stats", [P, NT, 6])
    m, var, rstd, root, w1, w2 = (ph.sb(n, [P, NT]) for n in ("m", "var", "rstd", "root", "w1", "w2"))
    Wq, Kd = ph.sb("Wq", [P, DC, D]), ph.sb("Kd", [P, HD, 2 * NK])

    def two(n, shape, dt=F32):
        return [ph.sb(f"{n}{h}", shape, dt) for h in range(2)]

    xn, qT, sims = two("xn", [P, D]), two("qT", [P, HD, P]), two("sims", [P, 2 * HD, NK])
    best, at = two("best", [P, 2 * HD, KB]), two("at", [P, 2 * HD, KB], U32)
    sums, fin, pk = two("sums", [P, HD, KB, KB]), two("fin", [P, HD, KB]), two("pk", [P, HD, KB], U32)
    I, FW, PK = ph.sb("I", [P, 2, NT, S]), ph.sb("FW", [P, NT, S]), ph.sb("PK", [P, NT, S])
    PH = ph.sb("PH", [P, NT, S])
    kio, sec, M = ph.sb("kio", [P, KB]), ph.sb("sec", [P, 1]), ph.sb("M", [P, NT * S, KB])
    t_ps = [ph.ps(f"t_ps{h}", [P, DC, P]) for h in range(2)]
    q_ps = [ph.ps(f"q_ps{h}", [P, HD, P]) for h in range(2)]
    s_ps = [ph.ps(f"s_ps{h}", [P, 2 * HD, NK]) for h in range(2)]
    x_in, w_in, k_in, zeroed, io_made = [ph.sem(f"x_in{k}") for k in range(4)], ph.sem("w_in"), ph.sem("k_in"), ph.sem("zeroed"), ph.sem("io")
    step, chain, asked, rooted, xT_out = ph.sem("step"), ph.sem("chain"), ph.sem("asked"), ph.sem("rooted"), ph.sem("xT_out")
    xn_ready, turned, xT_ready, q_ready, qT_ready, s_ready, sims_ready = (ph.pair_sem(n) for n in ("xn", "turned", "xT", "q", "qT", "s", "sims"))
    best_ready, at_ready, sums_ready, fin_ready, pk_ready, kept = (ph.pair_sem(n) for n in ("best", "at", "sums", "fin", "pk", "kept"))
    block = ph.start()

    @block.sync
    def _(sp):
        for q in range(4):
            for a in range(4):
                r = (q * 4 + a) * P
                sp.dma_start(X8[a * 32:(a + 1) * 32, q * 4:(q + 1) * 4, :],
                             x_dram[r:r + P, :].rearrange("(t g) c -> g t c", g=32)).then_inc(x_in[q], 16)
            if q == 0:
                sp.dma_start(Wq[:, :, :], A["L3_ffn_Wq"].rearrange("(c p) n -> p c n", p=P)).then_inc(w_in, 16)
                sp.wait_ge(zeroed, 1)
                for j in range(2):
                    sp.dma_start(Kd[j * 64:(j + 1) * 64, :, j * NK:(j + 1) * NK],
                                 A["L3_ffn_keys"][j].rearrange("d h k -> d h k")).then_inc(k_in, 16)
        for q in range(4):
            sp.wait_ge(xT_ready, 4 * q + 6)
            for c in range(DC):
                sp.dma_start(xT_dram[q, :, c, :].rearrange("p (a l) -> p a l", a=4), xT[:, c, :, q * P:(q + 1) * P]).then_inc(xT_out, 16)
        sp.wait_ge(xT_out, 16 * 4 * DC)

    @block.gpsimd
    def _(pool):
        pool.memset(Kd[:, :, :], 0.0).then_inc(zeroed, 1)
        pool.iota(kio[:, :], pattern=[[1, KB]], base=0, channel_multiplier=0, allow_small_or_imprecise_dtypes=True).then_inc(io_made, 1)

    @block.tensor
    def _(pe):
        pe.wait_ge(w_in, 16)
        pe.wait_ge(k_in, 32)
        with pe.Fori(0, NP) as i:
            for h in range(2):
                pe.wait_ge(xn_ready, here(i, h))
                pe.wait_ge(xT_ready, before(i, h))
                for c in range(DC):
                    last = pe.transpose(t_ps[h][:, c, :], xn[h][:, c * P:(c + 1) * P], ident[:, :])
                last.then_inc(turned, 1)
            for h in range(2):
                pe.wait_ge(xT_ready, here(i, h))
                pe.wait_ge(qT_ready, before(i, h))
                for n in range(HD):
                    for c in range(DC):
                        last = pe.matmul(q_ps[h][:, n, :], lhsT=Wq[:, c, n * P:(n + 1) * P], rhs=xT[:, c, :, bass.ds((2 * i + h) * 32, 32)],
                                         start=(c == 0), stop=(c == DC - 1))
                last.then_inc(q_ready, 1)
            for h in range(2):
                pe.wait_ge(qT_ready, here(i, h))
                pe.wait_ge(sims_ready, before(i, h))
                for n in range(HD):
                    last = pe.matmul(s_ps[h][:, 2 * n:2 * n + 2, :], lhsT=qT[h][:, n, :], rhs=Kd[:, n, :], start=True, stop=True)
                last.then_inc(s_ready, 1)

    @block.scalar
    def _(act):
        act.wait_ge(asked, 1)
        act.activation(root[:, :], var[:, :], ACT.Sqrt).then_inc(rooted, 1)
        with act.Fori(0, NP) as i:
            for h in range(2):
                t = 2 * i + h
                act.wait_ge(turned, here(i, h))
                act.activation(xT[:, :, :, bass.ds(t * 32, 32)], t_ps[h][:, :, :].rearrange("p c (a g) -> p c a g", g=32),
                               ACT.Copy).then_inc(xT_ready, 1)
            for h in range(2):
                act.wait_ge(q_ready, here(i, h))
                act.wait_ge(s_ready, before(i, h))
                act.activation(qT[h][:, :, :], q_ps[h][:, :, :], ACT.Copy).then_inc(qT_ready, 1)
            for h in range(2):
                act.wait_ge(s_ready, here(i, h))
                act.wait_ge(at_ready, before(i, h))
                act.activation(sims[h][:, :, :], s_ps[h][:, :, :], ACT.Copy).then_inc(sims_ready, 1)

    @block.vector
    def _(dve):
        for k in range(4):
            dve.wait_ge(x_in[k], 64)
            for t in range(4 * k, 4 * k + 4):
                last = dve.bn_stats(stats[:, t, :], X8[:, t, :])
        last.then_inc(step, 1)
        dve.wait_ge(step, 1)
        n = row_stats(dve, stats, m[:, :], var[:, :], w1[:, :], w2[:, :], step, 1)
        dve.wait_ge(step, n)
        dve.tensor_scalar(var[:, :], var[:, :], LN_EPS, None, ALU.add).then_inc(step, 1)
        n = rsqrt(dve, asked, rooted, 1, rstd[:, :], var[:, :], root[:, :], w1[:, :], step, n + 1)
        dve.wait_ge(step, n)
        def normalise(t, h):
            dve.tensor_scalar(xn[h][:, :], X8[:, t, :], m[:, bass.ds(t, 1)], rstd[:, bass.ds(t, 1)],
                              ALU.subtract, ALU.mult).then_inc(xn_ready, 1)

        def choose(i, more):
            for h in range(2):
                dve.wait_ge(sims_ready, here(i, h))
                if more:
                    dve.wait_ge(turned, here(i, h))
                    normalise(2 * i + 2 + h, h)
                for n in range(2 * HD):
                    last = dve.max(out=best[h][:, n, :], in_=sims[h][:, n, :])
                last.then_inc(best_ready, 1)
            for h in range(2):
                dve.wait_ge(best_ready, here(i, h))
                bh = best[h][:, :, :].rearrange("p (n two) k -> p n two k", two=2)
                dve.tensor_tensor(sums[h][:, :, :, :], bh[:, :, 0, :].unsqueeze(3).to_broadcast([P, HD, KB, KB]),
                                  bh[:, :, 1, :].unsqueeze(2).to_broadcast([P, HD, KB, KB]), ALU.add).then_inc(sums_ready, 1)
                for n in range(2 * HD):
                    last = dve.max_index(out=at[h][:, n, :], in_max=best[h][:, n, :], in_values=sims[h][:, n, :])
                last.then_inc(at_ready, 1)
            for h in range(2):
                t = 2 * i + h
                dve.wait_ge(sums_ready, here(i, h))
                dve.wait_ge(at_ready, here(i, h))
                ah = at[h][:, :, :].rearrange("p (n two) k -> p two n k", two=2)
                for j in range(2):
                    dve.tensor_copy(I[:, j, bass.ds(t, 1), :].rearrange("p a (n k) -> p (a n) k", k=KB), ah[:, j, :, :])
                for n in range(HD):
                    last = dve.max(out=fin[h][:, n, :], in_=sums[h][:, n, :, :].rearrange("p a b -> p (a b)"))
                last.then_inc(fin_ready, 1)
            for h in range(2):
                t = 2 * i + h
                dve.wait_ge(fin_ready, here(i, h))
                dve.tensor_scalar(FW[:, bass.ds(t, 1), :].rearrange("p a (n k) -> p (a n) k", k=KB), fin[h][:, :, :], 0.0, None, ALU.max)
                for n in range(HD):
                    last = dve.max_index(out=pk[h][:, n, :], in_max=fin[h][:, n, :], in_values=sums[h][:, n, :, :].rearrange("p a b -> p (a b)"))
                last.then_inc(pk_ready, 1)
            for h in range(2):
                t = 2 * i + h
                dve.wait_ge(pk_ready, here(i, h))
                dve.tensor_copy(PK[:, bass.ds(t, 1), :].rearrange("p a (n k) -> p (a n) k", k=KB), pk[h][:, :, :]).then_inc(kept, 1)

        for h in range(2):
            normalise(h, h)
        with dve.Fori(0, NP - 1) as i:
            choose(i, True)
        choose(NP - 1, False)
        dve.wait_ge(kept, 2 * NP + 2)
        dve.wait_ge(io_made, 1)
        link = linker(dve, chain)
        for a in range(4):
            link(dve.memset(sec[a * 32:(a + 1) * 32, :], 32.0 * a))
        link(dve.tensor_scalar(PH[:, :, :], PK[:, :, :], 1.0 / KB, -(KB - 1) / (2 * KB), ALU.mult, ALU.add))
        link(dve.tensor_scalar(PH[:, :, :], PH[:, :, :], MAGIC, None, ALU.add))
        link(dve.tensor_scalar(PH[:, :, :], PH[:, :, :], -MAGIC, None, ALU.add))
        link(dve.scalar_tensor_tensor(PK[:, :, :], PH[:, :, :], -float(KB), PK[:, :, :], ALU.mult, ALU.add))
        for j, r in ((0, PH), (1, PK)):
            link(dve.tensor_tensor(M[:, :, :], r[:, :, :].rearrange("p t s -> p (t s)").unsqueeze(2).to_broadcast([P, NT * S, KB]),
                                   kio[:, :].unsqueeze(1).to_broadcast([P, NT * S, KB]), ALU.is_equal))
            M4 = M[:, :, :].rearrange("p (a s) k -> p a s k", s=KB)
            link(dve.tensor_tensor(M4, M4, I[:, j, :, :].rearrange("p t (n k) -> p (t n) k", k=KB).unsqueeze(2).to_broadcast([P, NT * HD, KB, KB]), ALU.mult))
            link(dve.tensor_reduce(r[:, :, :].rearrange("p t s -> p (t s)"), M[:, :, :], AX.X, ALU.add))
        link(dve.tensor_scalar(M[:, 0:NT * S // KB, :].rearrange("p a k -> p (a k)"), PH[:, :, :].rearrange("p t s -> p (t s)"), float(E1), float(NK - 1), ALU.is_ge, ALU.mult))
        link(dve.tensor_tensor(PK[:, :, :].rearrange("p t s -> p (t s)"), PK[:, :, :].rearrange("p t s -> p (t s)"), M[:, 0:NT * S // KB, :].rearrange("p a k -> p (a k)"), ALU.max))
        link(dve.tensor_scalar(PH[:, :, :], PH[:, :, :], float(E1 - 1), None, ALU.min))
        for r, dst in ((PH, first[:, 0, :]), (FW, first[:, 1, :]), (PK, M[:, 0:NT * S // KB, :].rearrange("p a k -> p (a k)"))):
            link(dve.transpose(dst, r[:, :, :].rearrange("p t s -> p (t s)")))
        link(dve.tensor_copy(second[:, :], M[:, 0:NT * S // KB, :].rearrange("p a k -> p (a k)")))
        link(dve.tensor_scalar(first[:, 0, :], first[:, 0, :], sec[:, 0:1], None, ALU.add))

    ph.end()


def retrieve_phase(nc, R, A, name, x_dram, xT_dram, first, second, gate, out):
    ph = Phase(nc, name)
    tg = R["tg"]
    NQ, CH = N // 512, 512
    EB = A["L3_ffn_e_down"].shape[0]
    NP = EB // 2
    GR = CH // 4 // EB

    def two(n, shape, dt=F32):
        return [ph.sb(f"{n}{h}", shape, dt) for h in range(2)]

    G = ph.sb("G", [P, 2, EB, CH])
    xc, xh, xl = ph.sb("xc", [P, DC, CH]), ph.sb("xh", [P, DC, CH], F32R), ph.sb("xl", [P, DC, CH], F32R)
    ed, edh, edl = ph.sb("ed", [P, DC, P]), two("edh", [P, DC, P], F32R), two("edl", [P, DC, P], F32R)
    eu, euh, eul = ph.sb("eu", [P, D]), two("euh", [P, D], F32R), two("eul", [P, D], F32R)
    at, ath, atl = two("at", [P, CH]), two("ath", [P, CH], F32R), two("atl", [P, CH], F32R)
    oh2, oh1 = two("oh2", [P, GR, P]), two("oh1", [P, GR, P])
    one = ph.sb("one", [P, 1])
    xr, io, zero = ph.sb("xr", [P, 4, D]), ph.sb("io", [P, P]), ph.sb("zero", [P, P], BF16)
    h_ps = [ph.ps(f"h_ps{h}", [P, CH]) for h in range(2)]
    g_ps = [ph.ps(f"g_ps{h}", [P, GR, P]) for h in range(2)]
    o_ps = [ph.ps(f"o_ps{a}", [P, D]) for a in range(4)]
    io_made, zeroed = ph.sem("io"), ph.sem("zeroed")
    ed_in, eu_in, xc_in = ph.sem("ed_in"), ph.sem("eu_in"), ph.sem("xc_in")
    xh_ready, xl_ready = ph.sem("xh"), ph.sem("xl")
    edh_ready, edl_ready, euh_ready, eul_ready = (ph.pair_sem(n) for n in ("edh", "edl", "euh", "eul"))
    h_ready, sl_ready, at_ready, ath_ready, atl_ready, used = (ph.pair_sem(n) for n in ("h", "sl", "at", "ath", "atl", "used"))
    oh_ready, g_ready, G_ready = (ph.pair_sem(n) for n in ("oh", "g", "G"))
    xr_in, summed, y_ready, stored = ph.sem("xr_in"), ph.sem("summed"), ph.sem("y"), ph.sem("stored")
    block = ph.start()

    @block.sync
    def _(sp):
        def load_down(n):
            sp.wait_ge(edl_ready, n + 2)
            sp.dma_start(ed[:, :, :], A["L3_ffn_e_down"][bass.ds(n % EB, 1)].rearrange("e p c k -> p (e c) k")).then_inc(ed_in, 16)

        def load_up(n):
            sp.wait_ge(eul_ready, n + 2)
            sp.dma_start(eu[:, :], A["L3_ffn_e_up"][bass.ds(n % EB, 1)].rearrange("e p c -> p (e c)")).then_inc(eu_in, 16)

        load_up(0)
        load_down(0)
        load_down(1)
        with sp.Fori(2, NQ * EB) as n:
            load_down(n)
            load_up(n - 1)
        load_up(NQ * EB - 1)

    @block.gpsimd
    def _(pool):
        def down_low(n, h):
            pool.wait_ge(edh_ready, n + 3)
            pool.tensor_tensor(edl[h][:, :, :], ed[:, :, :], edh[h][:, :, :].bitcast(F32), ALU.subtract).then_inc(edl_ready, 1)

        def up_low(n, h):
            pool.wait_ge(euh_ready, n + 3)
            pool.tensor_tensor(eul[h][:, :], eu[:, :], euh[h][:, :].bitcast(F32), ALU.subtract).then_inc(eul_ready, 1)

        pool.dma_start(xc[:, :, :], xT_dram[0]).then_inc(xc_in, 16)
        pool.iota(io[:, :], pattern=[[1, P]], base=0, channel_multiplier=0, allow_small_or_imprecise_dtypes=True).then_inc(io_made, 1)
        pool.memset(zero[:, :], 0.0).then_inc(zeroed, 1)
        up_low(0, 0)
        for h in range(2):
            down_low(h, h)
        for q in range(NQ):
            if q < NQ - 1:
                pool.wait_ge(xl_ready, DC * (q + 1))
                pool.dma_start(xc[:, :, :], xT_dram[q + 1]).then_inc(xc_in, 16)
            rows = slice(q * CH, (q + 1) * CH)
            if q:
                pool.wait_ge(stored, 16 * q)
            pool.dma_start(xr[:, :, :], x_dram[rows, :].rearrange("(a p) c -> p a c", p=P)).then_inc(xr_in, 16)
            with pool.Fori(0, NP - (q == NQ - 1)) as k:
                n = q * EB + 2 * k
                down_low(n + 2, 0)
                up_low(n + 1, 1)
                down_low(n + 3, 1)
                up_low(n + 2, 0)
            if q == NQ - 1:
                up_low(NQ * EB - 1, 1)
            pool.wait_ge(y_ready, 4 * (q + 1))
            pool.dma_start(out[rows, :].rearrange("(a p) c -> p a c", p=P), xr[:, :, :]).then_inc(stored, 16)
        pool.wait_ge(stored, 16 * NQ)

    @block.tensor
    def _(pe):
        def weigh(n, h):
            pe.wait_ge(oh_ready, n + 3)
            pe.wait_ge(G_ready, n + 1)
            for g in range(GR):
                last = pe.matmul(g_ps[h][:, g, :], lhsT=oh2[h][:, g, :], rhs=oh1[h][:, g, :], start=True, stop=True)
            last.then_inc(g_ready, 1)

        def begin(q):
            if q:
                pe.wait_ge(y_ready, 4 * q)
            for a in range(4):
                pe.matmul(o_ps[a][:, :], lhsT=zero[:, :], rhs=zero[:, 0:1].to_broadcast([P, D]), start=True, stop=False)

        def hidden(n):
            for h in range(2):
                pe.wait_ge(edl_ready, n + h + 3)
                pe.wait_ge(sl_ready, n + h + 1)
                for c in range(DC):
                    for m, (w, x) in enumerate(((edh, xh), (edh, xl), (edl, xh))):
                        last = pe.matmul(h_ps[h][:, :], lhsT=w[h][:, c, :], rhs=x[:, c, :],
                                         start=(c == 0 and m == 0), stop=(c == DC - 1 and m == 2))
                last.then_inc(h_ready, 1)

        def add_up(n, more):
            for h in range(2):
                if more:
                    weigh(n + h + EB, h)
                pe.wait_ge(eul_ready, n + h + 3)
                pe.wait_ge(atl_ready, n + h + 3)
                for a in range(4):
                    for w, x in ((ath, euh), (ath, eul), (atl, euh)):
                        last = pe.matmul(o_ps[a][:, :], lhsT=w[h][:, a * P:(a + 1) * P], rhs=x[h][:, :], start=False, stop=False)
                last.then_inc(used, 1)

        def end():
            for a in range(4):
                last = pe.matmul(o_ps[a][:, :], lhsT=zero[:, :], rhs=zero[:, 0:1].to_broadcast([P, D]), start=False, stop=True)
            last.then_inc(summed, 1)

        pe.wait_ge(zeroed, 1)
        with pe.Fori(0, NP) as i:
            for h in range(2):
                weigh(2 * i + h, h)
        for q in range(NQ):
            pe.wait_ge(xl_ready, DC * (q + 1))
            hidden(q * EB)
            begin(q)
            add_up(q * EB, q < NQ - 1)
            with pe.Fori(1, NP) as k:
                hidden(q * EB + 2 * k)
                add_up(q * EB + 2 * k, q < NQ - 1)
            end()

    @block.scalar
    def _(act):
        def down_high(n, h):
            act.wait_ge(ed_in, 16 * n + 16)
            act.wait_ge(h_ready, n + 1)
            act.activation(edh[h][:, :, :], ed[:, :, :], ACT.Copy).then_inc(edh_ready, 1)

        def up_high(n, h):
            act.wait_ge(eu_in, 16 * n + 16)
            act.wait_ge(used, n + 1)
            act.activation(euh[h][:, :], eu[:, :], ACT.Copy).then_inc(euh_ready, 1)

        def silu(n, h):
            act.wait_ge(h_ready, n + 3)
            act.wait_ge(atl_ready, n + 1)
            act.activation(at[h][:, :], h_ps[h][:, :], ACT.Silu).then_inc(sl_ready, 1)

        def high(n, h):
            act.wait_ge(at_ready, n + 3)
            act.wait_ge(used, n + 1)
            act.activation(ath[h][:, :], at[h][:, :], ACT.Copy).then_inc(ath_ready, 1)

        def keep(n, q, k, h):
            act.wait_ge(g_ready, n + 3)
            act.activation(G[:, q % 2, :, :].rearrange("p e (a l) -> p a e l", a=4)[:, :, :, bass.ds((2 * k + h) * GR, GR)],
                           g_ps[h][:, :, :].rearrange("p g (a e) -> p a e g", a=4), ACT.Copy).then_inc(G_ready, 1)

        def turn(q, k, more):
            n = q * EB + 2 * k
            silu(n, 0)
            if more:
                down_high(n + 2, 0)
            high(n, 0)
            up_high(n + 1, 1)
            silu(n + 1, 1)
            high(n + 1, 1)
            if q < NQ - 1:
                keep(n + EB, q + 1, k, 0)
            if more:
                down_high(n + 3, 1)
            if q < NQ - 1:
                keep(n + 1 + EB, q + 1, k, 1)
            if more:
                up_high(n + 2, 0)

        act.wait_ge(zeroed, 1)
        act.activation(one[:, :], zero[:, 0:1], ACT.Silu)
        up_high(0, 0)
        for h in range(2):
            down_high(h, h)
        for q in range(NQ):
            act.wait_ge(xc_in, 16 * q + 16)
            act.wait_ge(h_ready, q * EB + 2)
            for c in range(DC):
                act.activation(xh[:, c, :], xc[:, c, :], ACT.Copy).then_inc(xh_ready, 1)
            if q == 0:
                with act.Fori(0, NP) as i:
                    for h in range(2):
                        keep(2 * i + h, 0, i, h)
            with act.Fori(0, NP - (q == NQ - 1)) as k:
                turn(q, k, True)
        turn(NQ - 1, NP - 1, False)

    @block.vector
    def _(dve):
        def one_hots(n, h):
            dve.wait_ge(g_ready, n + 1)
            dve.tensor_tensor(oh2[h][:, :, :], io[:, :].unsqueeze(1).to_broadcast([P, GR, P]),
                              second[:, bass.ds(n * GR, GR)].unsqueeze(2).to_broadcast([P, GR, P]), ALU.is_equal)
            for g in range(GR):
                at_g = bass.ds(n * GR + g, 1)
                last = dve.tensor_scalar(oh1[h][:, g, :], io[:, :], first[:, 0, at_g], first[:, 1, at_g], ALU.is_equal, ALU.mult)
            last.then_inc(oh_ready, 1)

        def weight(n, q, k, h):
            dve.wait_ge(sl_ready, n + 3)
            dve.tensor_tensor(at[h][:, :], at[h][:, :], G[:, q % 2, 2 * k + h, :], ALU.mult).then_inc(at_ready, 1)

        def low(n, h):
            dve.wait_ge(ath_ready, n + 3)
            dve.tensor_tensor(atl[h][:, :], at[h][:, :], ath[h][:, :].bitcast(F32), ALU.subtract).then_inc(atl_ready, 1)

        def split_x(q):
            for c in range(DC):
                dve.wait_ge(xh_ready, DC * q + c + 1)
                dve.tensor_tensor(xl[:, c, :], xc[:, c, :], xh[:, c, :].bitcast(F32), ALU.subtract).then_inc(xl_ready, 1)

        def turn(q, k, more):
            n = q * EB + 2 * k
            weight(n, q, k, 0)
            low(n, 0)
            weight(n + 1, q, k, 1)
            low(n + 1, 1)
            if more:
                for h in range(2):
                    one_hots(n + EB + 2 + h, h)

        dve.wait_ge(io_made, 1)
        split_x(0)
        with dve.Fori(0, NP + 1) as i:
            for h in range(2):
                one_hots(2 * i + h, h)
        for q in range(NQ):
            dve.wait_ge(G_ready, (q + 1) * EB + 2)
            alone = q == NQ - 2
            with dve.Fori(0, NP - alone) as k:
                turn(q, k, q < NQ - 1)
            if alone:
                turn(q, NP - 1, False)
            if q < NQ - 1:
                split_x(q + 1)
            dve.wait_ge(summed, q + 1)
            dve.wait_ge(xr_in, 16 * (q + 1))
            for a in range(4):
                dve.scalar_tensor_tensor(xr[:, a, :], o_ps[a][:, :], tg[:, gate:gate + 1], xr[:, a, :],
                                         ALU.mult, ALU.add).then_inc(y_ready, 1)

    ph.end()


def build(nc, A, out):
    with ExitStack() as ctx:
        def sb(name, shape, dt=F32):
            return ctx.enter_context(nc.sbuf_tensor(name, shape, dt))

        R = {"ident": sb("ident", [P, P]), "identb": sb("identb", [P, P], BF16), "ones": sb("ones", [P, P]),
             "tg": sb("tg", [P, 8]), "stats": sb("stats", [P, NT, 6]), "magic": sb("magic", [P, 2])}
        x7 = nc.dram_tensor("x7", (N, D), F32, kind="Internal").ap()
        F = A["L0_ffn_w_downT"].shape[0]
        with nc.sbuf_tensor("X", [P, NT, D], F32) as X:
            R["X"] = X
            setup_phase(nc, R, A)
            with nc.sbuf_tensor("KV", [P, B * DC, 2 * P], F32) as KV:
                wkv_phase(nc, R, A, "L0x", 0, "L0_xattn_w", "L0_xattn_u", False, KV)
                with nc.sbuf_tensor("wgu_q", [P, DC, 2 * F], BF16) as wgu_q, nc.sbuf_tensor("wd_q", [P, F // P, D], BF16) as wd_q, \
                        nc.sbuf_tensor("unit", [P, 3], F32) as unit:
                    ternary_phase(nc, R, A, wgu_q, wd_q, unit)
                    bitnet_phase(nc, R, A, wgu_q, wd_q, unit, 4)
                linear_attention_phase(nc, R, A, KV, 1)
            spline_phase(nc, R, A, 5)
            wkv_phase(nc, R, A, "L2x", 2, "L2_xattn_time_decay", "L2_xattn_time_first", True)
            experts_phase(nc, R, A, 6)
            decay_phase(nc, R, A, 3, x7)
        xT = nc.dram_tensor("xT", (4, P, DC, D), F32, kind="Internal").ap()
        with nc.sbuf_tensor("first", [P, 2, NT * 32], F32) as first, nc.sbuf_tensor("second", [P, NT * 32], BF16) as second:
            route_phase(nc, R, A, "L3r", x7, xT, first, second)
            retrieve_phase(nc, R, A, "L3f", x7, xT, first, second, 7, out)


def kernel(**inputs):
    import numpy as np
    import concourse.bacc as bacc
    from concourse.bass_utils import run_bass_kernel_spmd

    def rows(name, n):
        return np.ascontiguousarray(inputs[name]).reshape(n, -1)

    def turned(name, n):
        return np.ascontiguousarray(rows(name, n).T)

    laid = {
        "x": rows("x", N),
        "ctxT": turned("ctx_2048", N),
        "g_xattn": inputs["g_xattn"], "g_ffn": inputs["g_ffn"],
        "L0_ffn_w_gate_upT": turned("L0_ffn_w_gate_up", 2816), "L0_ffn_w_downT": turned("L0_ffn_w_down", 512),
        "L0_ffn_norm_weight": inputs["L0_ffn_norm_weight"],
        "L1_xattn_WqT": turned("L1_xattn_Wq", D), "L1_xattn_WgT": turned("L1_xattn_Wg", D),
        "L1_xattn_WkvT": turned("L1_xattn_Wkv", 2 * D), "L1_xattn_WoT": turned("L1_xattn_Wo", D),
        "L1_xattn_bg": inputs["L1_xattn_bg"],
        **{n: inputs[n] for n in ("L1_ffn_ln_gamma", "L1_ffn_ln_beta", "L1_ffn_spline_bases", "L1_ffn_spline_slopes",
                                  "L1_ffn_output_scale", "L2_xattn_time_decay", "L2_xattn_time_first")},
        "L2_ffn_downT": turned("L2_ffn_down_w", 128), "L2_ffn_routerT": turned("L2_ffn_router_w", 8),
        "L2_ffn_up": np.transpose(inputs["L2_ffn_up_w"], (0, 2, 1)).reshape(128, D),
        "ctx": rows("ctx_2048", N),
        "L3_xattn_decay": np.asarray(inputs["L3_xattn_decay"]).reshape(1),
        "L3_xattn_W_inT": turned("L3_xattn_W_in", D), "L3_xattn_W_outT": turned("L3_xattn_W_out", D),
        **{n: inputs[n] for n in ("L3_xattn_b_in", "L3_xattn_b_out", "L3_xattn_gamma", "L3_xattn_beta")},
        "L3_ffn_Wq": inputs["L3_ffn_Wq"],
        "L3_ffn_keys": np.transpose(inputs["L3_ffn_keys"], (2, 3, 0, 1)),
        "L3_ffn_e_down": np.transpose(np.reshape(inputs["L3_ffn_e_down"], (32, P, DC, P)), (0, 3, 2, 1)),
        "L3_ffn_e_up": np.reshape(inputs["L3_ffn_e_up"], (32, P, D)),
        "L0_xattn_w": inputs["L0_xattn_w"], "L0_xattn_u": inputs["L0_xattn_u"],
    }
    nc = bacc.Bacc("TRN2", target_bir_lowering=False, num_devices=1)
    arrays, A = {}, {}
    for name, a in laid.items():
        a = np.ascontiguousarray(a)
        arrays[f"in_{name}"] = a
        A[name] = nc.dram_tensor(f"in_{name}", a.shape, mybir.dt.from_np(a.dtype), kind="ExternalInput").ap()
    out = nc.dram_tensor("out", (N, D), F32, kind="ExternalOutput").ap()
    build(nc, A, out)
    r = run_bass_kernel_spmd(nc, [arrays], core_ids=[0])
    return r.results[0]["out"].reshape(B, T, D)
```
